# Optimizing a Trainium2 kernel written in Bass

```python
import numpy as np
import jax
import jax.numpy as jnp

def _softmax(x, axis=-1):
    return jax.nn.softmax(x, axis=axis)

def _gelu(x):
    return jax.nn.gelu(x, approximate=True)

def _silu(x):
    return jax.nn.silu(x)

def _sigmoid(x):
    return jax.nn.sigmoid(x)

def _layernorm(x, axis=-1, eps=1e-05):
    m = jnp.mean(x, axis=axis, keepdims=True)
    v = jnp.var(x, axis=axis, keepdims=True)
    return (x - m) / jnp.sqrt(v + eps)

def _scatter_add(tgt, idx, src, axis=0):
    return tgt.at[idx].add(src)

def _segment_sum(src, seg, n):
    return jax.ops.segment_sum(src, seg, n)
kernel_name = 'mk_seq_postln_d2_jaxref_r8_9faede'

def setup_inputs(seed: int=0):
    np.random.seed(seed)
    _w = jnp.asarray

    def _L0_attn_setup():
        import jax, jax.numpy as jnp
        import numpy as np
        import math
        DIM = 128
        HEADS = 16
        HEAD_DIM = DIM // HEADS
        key = jax.random.key(seed)
        ks = jax.random.split(key, 7)
        b, n = (2, 256)
        scale = 1.0 / math.sqrt(DIM)
        x = jax.random.normal(ks[0], (b, n, DIM), dtype=jnp.float32)
        Wq = jax.random.normal(ks[1], (DIM, DIM), dtype=jnp.float32) * scale
        Wk = jax.random.normal(ks[2], (DIM, DIM), dtype=jnp.float32) * scale
        Wv = jax.random.normal(ks[3], (DIM, DIM), dtype=jnp.float32) * scale
        Wo = jax.random.normal(ks[4], (DIM, DIM), dtype=jnp.float32) * scale
        bo = jnp.zeros((DIM,), dtype=jnp.float32)
        denom_bias = jnp.zeros((1, HEADS, 1, 1), dtype=jnp.float32)
        return {'x': x, 'Wq': Wq, 'Wk': Wk, 'Wv': Wv, 'Wo': Wo, 'bo': bo, 'denom_bias': denom_bias}
    _L0_attn_in = _L0_attn_setup()

    def _L0_ffn_setup():
        import jax, jax.numpy as jnp
        import numpy as np
        B, S, H, F, E, K = (4, 512, 128, 512, 8, 2)
        key = jax.random.key(seed)
        ks = jax.random.split(key, 4)
        x = jax.random.normal(ks[0], (B, S, H), dtype=jnp.float32)
        Wg = jax.random.normal(ks[1], (H, E), dtype=jnp.float32) * (1.0 / np.sqrt(H))
        W1 = jax.random.normal(ks[2], (E, H, F), dtype=jnp.float32) * (1.0 / np.sqrt(H))
        b1 = jnp.zeros((E, F), dtype=jnp.float32)
        W2 = jax.random.normal(ks[3], (E, F, H), dtype=jnp.float32) * (1.0 / np.sqrt(F))
        b2 = jnp.zeros((E, H), dtype=jnp.float32)
        return {'x': x, 'Wg': Wg, 'W1': W1, 'b1': b1, 'W2': W2, 'b2': b2}
    _L0_ffn_in = _L0_ffn_setup()

    def _L1_attn_setup():
        import jax, jax.numpy as jnp
        import numpy as np
        D_MODEL = 128
        RANK = 32
        INIT_ALPHA = 0.5
        key = jax.random.key(seed)
        ks = jax.random.split(key, 12)
        D, R = (D_MODEL, RANK)
        s = 0.02
        return {'x': jax.random.normal(ks[0], (4, 256, D), dtype=jnp.float32), 'Wq': jax.random.normal(ks[1], (D, D), dtype=jnp.float32) * s, 'Wk': jax.random.normal(ks[2], (D, D), dtype=jnp.float32) * s, 'Wo': jax.random.normal(ks[3], (D, D), dtype=jnp.float32) * s, 'U_b': jax.random.normal(ks[4], (D, R), dtype=jnp.float32) * s, 'V_b': jax.random.normal(ks[5], (D, R), dtype=jnp.float32) * s, 'W_b': jax.random.normal(ks[6], (D, R), dtype=jnp.float32) * s, 'bias_b': jnp.zeros((D,), dtype=jnp.float32), 'U_t': jax.random.normal(ks[7], (D, R), dtype=jnp.float32) * s, 'V_t': jax.random.normal(ks[8], (D, R), dtype=jnp.float32) * s, 'W_t': jax.random.normal(ks[9], (D, R), dtype=jnp.float32) * s, 'X_t': jax.random.normal(ks[10], (D, R), dtype=jnp.float32) * s, 'bias_t': jnp.zeros((D,), dtype=jnp.float32), 'alpha': jnp.asarray(INIT_ALPHA, dtype=jnp.float32)}
    _L1_attn_in = _L1_attn_setup()

    def _L1_ffn_setup():
        import jax, jax.numpy as jnp
        import numpy as np
        LN_EPS = 1e-05

        def layer_norm(x, g, b):
            mu = jnp.mean(x, axis=-1, keepdims=True)
            var = jnp.var(x, axis=-1, keepdims=True)
            return (x - mu) / jnp.sqrt(var + LN_EPS) * g + b

        def balanced_assignment(scores):
            T, E = scores.shape
            C = T // E
            taken = jnp.zeros((T,), dtype=bool)
            parts = []
            for e in range(E):
                s = jnp.where(taken, -jnp.inf, scores[:, e])
                _, idx = jax.lax.top_k(s, C)
                parts.append(idx)
                taken = taken.at[idx].set(True)
            return jnp.concatenate(parts)
        key = jax.random.key(seed)
        ks = jax.random.split(key, 4)
        B, S, D, F, E = (4, 256, 128, 512, 8)
        return {'x': jax.random.normal(ks[0], (B, S, D), dtype=jnp.float32), 'centroids': jax.random.normal(ks[1], (E, D), dtype=jnp.float32) * 0.1, 'ln_g': jnp.ones((D,), dtype=jnp.float32), 'ln_b': jnp.zeros((D,), dtype=jnp.float32), 'w1': jax.random.normal(ks[2], (E, D, F), dtype=jnp.float32) * 0.02, 'b1': jnp.zeros((E, F), dtype=jnp.float32), 'w2': jax.random.normal(ks[3], (E, F, D), dtype=jnp.float32) * 0.02, 'b2': jnp.zeros((E, D), dtype=jnp.float32)}
    _L1_ffn_in = _L1_ffn_setup()
    _d = {'L0_attn_x': _L0_attn_in['x'], 'L0_attn_Wq': _L0_attn_in['Wq'], 'L0_attn_Wk': _L0_attn_in['Wk'], 'L0_attn_Wv': _L0_attn_in['Wv'], 'L0_attn_Wo': _L0_attn_in['Wo'], 'L0_attn_bo': _L0_attn_in['bo'], 'L0_attn_denom_bias': _L0_attn_in['denom_bias'], 'L0_ffn_Wg': _L0_ffn_in['Wg'], 'L0_ffn_W1': _L0_ffn_in['W1'], 'L0_ffn_b1': _L0_ffn_in['b1'], 'L0_ffn_W2': _L0_ffn_in['W2'], 'L0_ffn_b2': _L0_ffn_in['b2'], 'L1_attn_Wq': _L1_attn_in['Wq'], 'L1_attn_Wk': _L1_attn_in['Wk'], 'L1_attn_Wo': _L1_attn_in['Wo'], 'L1_attn_U_b': _L1_attn_in['U_b'], 'L1_attn_V_b': _L1_attn_in['V_b'], 'L1_attn_W_b': _L1_attn_in['W_b'], 'L1_attn_bias_b': _L1_attn_in['bias_b'], 'L1_attn_U_t': _L1_attn_in['U_t'], 'L1_attn_V_t': _L1_attn_in['V_t'], 'L1_attn_W_t': _L1_attn_in['W_t'], 'L1_attn_X_t': _L1_attn_in['X_t'], 'L1_attn_bias_t': _L1_attn_in['bias_t'], 'L1_attn_alpha': _L1_attn_in['alpha'], 'L1_ffn_centroids': _L1_ffn_in['centroids'], 'L1_ffn_ln_g': _L1_ffn_in['ln_g'], 'L1_ffn_ln_b': _L1_ffn_in['ln_b'], 'L1_ffn_w1': _L1_ffn_in['w1'], 'L1_ffn_b1': _L1_ffn_in['b1'], 'L1_ffn_w2': _L1_ffn_in['w2'], 'L1_ffn_b2': _L1_ffn_in['b2']}
    _x0 = _d['L0_attn_x']
    _d['L0_attn_x'] = jax.random.normal(jax.random.fold_in(jax.random.key(seed), 1), (8, 512, 128), dtype=_x0.dtype)
    del _x0
    return _d

def reference(L0_attn_x, L0_attn_Wq, L0_attn_Wk, L0_attn_Wv, L0_attn_Wo, L0_attn_bo, L0_attn_denom_bias, L0_ffn_Wg, L0_ffn_W1, L0_ffn_b1, L0_ffn_W2, L0_ffn_b2, L1_attn_Wq, L1_attn_Wk, L1_attn_Wo, L1_attn_U_b, L1_attn_V_b, L1_attn_W_b, L1_attn_bias_b, L1_attn_U_t, L1_attn_V_t, L1_attn_W_t, L1_attn_X_t, L1_attn_bias_t, L1_attn_alpha, L1_ffn_centroids, L1_ffn_ln_g, L1_ffn_ln_b, L1_ffn_w1, L1_ffn_b1, L1_ffn_w2, L1_ffn_b2):

    def _L0_attn_ref(x, Wq, Wk, Wv, Wo, bo, denom_bias):
        import jax, jax.numpy as jnp
        import numpy as np
        import math
        DIM = 128
        HEADS = 16
        HEAD_DIM = DIM // HEADS
        b, n, d = x.shape
        h, hd = (HEADS, HEAD_DIM)

        def split_heads(t):
            return t.reshape(b, n, h, hd).transpose(0, 2, 1, 3)
        q = split_heads(x @ Wq.T)
        k = split_heads(x @ Wk.T)
        v = split_heads(x @ Wv.T)
        sim = jnp.einsum('bhid,bhjd->bhij', q, k) / math.sqrt(hd)
        causal_mask = jnp.triu(jnp.ones((n, n), dtype=bool), k=1)
        neg = -jnp.finfo(sim.dtype).max
        sim = jnp.where(causal_mask, neg, sim)
        sim_max = jnp.max(sim, axis=-1, keepdims=True)
        exp_sim = jnp.exp(sim - sim_max)
        denom = jnp.sum(exp_sim, axis=-1, keepdims=True) + jnp.exp(denom_bias)
        attn = exp_sim / denom
        out = jnp.einsum('bhij,bhjd->bhid', attn, v)
        out = out.transpose(0, 2, 1, 3).reshape(b, n, d)
        return out @ Wo.T + bo

    def _L0_ffn_ref(x, Wg, W1, b1, W2, b2):
        import jax, jax.numpy as jnp
        import numpy as np
        B, S, H, F, E, K = (4, 512, 128, 512, 8, 2)
        b, s, h = x.shape
        e = W1.shape[0]
        xf = x.reshape(-1, h)
        logits = xf @ Wg
        top_vals, top_idx = jax.lax.top_k(logits, K)
        gate_w = jax.nn.softmax(top_vals, axis=-1)
        comb = jnp.sum(gate_w[..., None] * jax.nn.one_hot(top_idx, e, dtype=xf.dtype), axis=1)
        out = jnp.zeros_like(xf)
        for ei in range(e):
            hdd = jax.nn.gelu(xf @ W1[ei] + b1[ei])
            y = hdd @ W2[ei] + b2[ei]
            out = out + comb[:, ei:ei + 1] * y
        return out.reshape(b, s, h)

    def _L1_attn_ref(x, Wq, Wk, Wo, U_b, V_b, W_b, bias_b, U_t, V_t, W_t, X_t, bias_t, alpha):
        import jax, jax.numpy as jnp
        import numpy as np
        D_MODEL = 128
        RANK = 32
        INIT_ALPHA = 0.5
        B, T, D = x.shape
        Q = x @ Wq.T
        K = x @ Wk.T
        counts = jnp.arange(1, T + 1, dtype=x.dtype)[None, :, None]
        Z = jnp.cumsum(x, axis=1) / counts
        a_b = Q @ V_b
        c_b = jnp.cumsum(K @ W_b, axis=1)
        bil = a_b * c_b @ U_b.T
        a_t = Q @ V_t
        c_t = jnp.cumsum(K @ W_t, axis=1)
        z_t = Z @ X_t
        tri = a_t * z_t * c_t @ U_t.T
        out = (bil + alpha * tri) / counts + (bias_b + alpha * bias_t)
        return out @ Wo.T

    def _L1_ffn_ref(x, centroids, ln_g, ln_b, w1, b1, w2, b2):
        import jax, jax.numpy as jnp
        import numpy as np
        LN_EPS = 1e-05

        def layer_norm(x, g, b):
            mu = jnp.mean(x, axis=-1, keepdims=True)
            var = jnp.var(x, axis=-1, keepdims=True)
            return (x - mu) / jnp.sqrt(var + LN_EPS) * g + b

        def balanced_assignment(scores):
            T, E = scores.shape
            C = T // E
            taken = jnp.zeros((T,), dtype=bool)
            parts = []
            for e in range(E):
                s = jnp.where(taken, -jnp.inf, scores[:, e])
                _, idx = jax.lax.top_k(s, C)
                parts.append(idx)
                taken = taken.at[idx].set(True)
            return jnp.concatenate(parts)
        D = x.shape[-1]
        feat = x.reshape(-1, D)
        T = feat.shape[0]
        E = centroids.shape[0]
        C = T // E
        norm = layer_norm(feat, ln_g, ln_b)
        scores = jax.lax.stop_gradient(norm @ centroids.T)
        sort_by_expert = balanced_assignment(scores)
        routed = feat[sort_by_expert].reshape(E, C, D)
        h = layer_norm(routed, ln_g, ln_b)
        h = jax.nn.gelu(jnp.einsum('ecd,edf->ecf', h, w1) + b1[:, None, :])
        h = jnp.einsum('ecf,efd->ecd', h, w2) + b2[:, None, :]
        out = routed + h
        inv = jnp.zeros((T,), dtype=jnp.int32).at[sort_by_expert].set(jnp.arange(T, dtype=jnp.int32))
        return out.reshape(T, D)[inv].reshape(x.shape)
    x = L0_attn_x
    x = _layernorm(x + _L0_attn_ref(x, L0_attn_Wq, L0_attn_Wk, L0_attn_Wv, L0_attn_Wo, L0_attn_bo, L0_attn_denom_bias), axis=-1)
    x = _layernorm(x + _L0_ffn_ref(x, L0_ffn_Wg, L0_ffn_W1, L0_ffn_b1, L0_ffn_W2, L0_ffn_b2), axis=-1)
    x = _layernorm(x + _L1_attn_ref(x, L1_attn_Wq, L1_attn_Wk, L1_attn_Wo, L1_attn_U_b, L1_attn_V_b, L1_attn_W_b, L1_attn_bias_b, L1_attn_U_t, L1_attn_V_t, L1_attn_W_t, L1_attn_X_t, L1_attn_bias_t, L1_attn_alpha), axis=-1)
    x = _layernorm(x + _L1_ffn_ref(x, L1_ffn_centroids, L1_ffn_ln_g, L1_ffn_ln_b, L1_ffn_w1, L1_ffn_b1, L1_ffn_w2, L1_ffn_b2), axis=-1)
    return x

_drawn_inputs = setup_inputs


def setup_inputs(seed=0):
    import zlib

    import numpy as np

    out = dict(_drawn_inputs(seed))
    spreads = {'L0_attn_bo': (0.0, 0.1),
     'L0_attn_denom_bias': (0.0, 0.693),
     'L0_ffn_b1': (0.0, 0.1),
     'L0_ffn_b2': (0.0, 0.1),
     'L1_attn_bias_b': (0.0, 0.351),
     'L1_attn_bias_t': (0.0, 0.667),
     'L1_ffn_ln_g': (1.0, 0.2),
     'L1_ffn_ln_b': (0.0, 2.0),
     'L1_ffn_b1': (0.0, 0.654),
     'L1_ffn_b2': (0.0, 0.1)}
    factors = {'L1_attn_Wq': 8.0,
     'L1_attn_Wk': 8.0,
     'L1_attn_U_b': 8.0,
     'L1_attn_V_b': 8.0,
     'L1_attn_W_b': 8.0,
     'L1_attn_U_t': 8.0,
     'L1_attn_V_t': 8.0,
     'L1_attn_W_t': 8.0,
     'L1_attn_X_t': 8.0}
    for name, (base, spread) in spreads.items():
        noise = np.random.default_rng([zlib.crc32(name.encode()), seed]).standard_normal(out[name].shape)
        drawn = base * np.exp(spread * noise) if base else spread * noise
        out[name] = jnp.asarray(drawn.astype(out[name].dtype))
    for name, factor in factors.items():
        out[name] = (out[name] * factor).astype(out[name].dtype)
    return out
```

```python
import concourse.bass as bass
from concourse import mybir
from contextlib import ExitStack


def sequence_stack_kernel(nc, I, out):
    f32 = mybir.dt.float32
    bf16 = mybir.dt.bfloat16
    i32 = mybir.dt.int32
    ALU = mybir.AluOpType
    ACT = mybir.ActivationFunctionType
    AX = mybir.AxisListType

    B, S, D = 8, 512, 128
    P = 128
    T = S // P
    H, HD = 16, 8
    E, F = 8, 512
    FC = F // P
    R = 32
    NT = B * T
    CAP = B * S // E
    PARTS = 3
    QROWS = 6 * HD
    MROW = 96
    SCALE = float(HD) ** -0.5
    EPS = 1e-5
    QUADS = H // 4
    UNITS = 10
    Q_PART = [0, 0, 1, 1, 0, 2]
    K_PART = [0, 1, 0, 1, 2, 0]
    DIGITS = [18, 14, 10, 6, 2, 0]
    WAYS = 15

    ctx = ExitStack()
    with ctx:
        def sb(name, shape, dt=f32):
            return ctx.enter_context(nc.sbuf_tensor(name, shape, dt))

        def sem(name):
            return ctx.enter_context(nc.semaphore(name))

        identf = sb("identf", [P, P])
        identb = sb("identb", [P, P], bf16)
        mask_a = sb("mask_a", [P, P], bf16)
        mask_t = sb("mask_t", [P, P], bf16)
        onesb = sb("onesb", [P, P], bf16)
        onesf = sb("onesf", [P, S])
        inv_count = sb("inv_count", [P, S])
        iota8 = sb("iota8", [P, E])
        kstep = sb("kstep", [P, 1 + len(DIGITS), WAYS])
        tie = sb("tie", [P, NT])
        half = sb("half", [P, T])

        wq0 = sb("wq0", [P, D])
        wk0 = sb("wk0", [P, D])
        wv0 = sb("wv0", [P, D])
        wo0 = sb("wo0", [P, D])
        bo0 = sb("bo0", [P, D])
        expdb = sb("expdb", [P, H])
        wg = sb("wg", [P, E])
        w1a = sb("w1a", [P, E, F])
        w2a = sb("w2a", [P, E, FC, D])
        b1a = sb("b1a", [P, E, FC])
        b2a = sb("b2a", [P, E, D])
        wq1 = sb("wq1", [P, D])
        wk1 = sb("wk1", [P, D])
        wo1 = sb("wo1", [P, D])
        vcat = sb("vcat", [P, 3 * R])
        wcat = sb("wcat", [P, 2 * R])
        ucat = sb("ucat", [P, 2 * R + 1])
        bias_t = sb("bias_t", [P, 1])
        alpha = sb("alpha", [P, 1])
        wa = sb("wa", [P, 3 * R])
        wb = sb("wb", [P, 3 * R])
        uc = sb("uc", [2 * R + 1, D])
        cent = sb("cent", [P, E])
        lng = sb("lng", [P, D])
        lnb = sb("lnb", [P, D])

        xT = sb("xT", [P, S])
        xtok = sb("xtok", [P, T, D])
        qparts = [sb(f"q{i}", [P, S], bf16) for i in range(PARTS)]
        kparts = [sb(f"k{i}", [P, S], bf16) for i in range(PARTS)]
        qrest = sb("qrest", [P, S])
        krest = sb("krest", [P, S])
        QP = sb("QP", [P, H, S], bf16)
        KP = sb("KP", [P, H, S], bf16)
        Vaug = sb("Vaug", [P, T, H, 32])
        M = sb("M", [P, T, H])
        mrest = sb("mrest", [P, T, H])
        NM = sb("NM", [P, T, P // H, H], bf16)
        NMT = sb("NMT", [PARTS * H, S], bf16)
        PR = sb("PR", [P, 2, UNITS, S])
        OT = sb("OT", [P, QUADS, S])
        den = sb("den", [P, T, H])
        att = sb("att", [P, T, D])
        attT = sb("attT", [P, S])
        res = sb("res", [P, T, D])
        X1 = sb("X1", [P, T, D])
        X1T = sb("X1T", [P, S])
        X2 = sb("X2", [P, T, D])
        X2T = sb("X2T", [P, S])
        X3 = sb("X3", [P, NT, D])
        N3T = sb("N3T", [P, B, S])
        stats = sb("stats", [P, T, 6])
        mv = sb("mv", [P, T, 2])
        rstd = sb("rstd", [P, T])
        top = sb("top", [P, T, 8])
        topi = sb("topi", [P, T, 8], mybir.dt.uint32)
        topf = sb("topf", [P, T, 8])
        logit = sb("logit", [P, T, E])
        gate = sb("gate", [P, T, 2])
        comb = sb("comb", [P, T, E])
        comb2 = sb("comb2", [P, T, E])
        Hh = PR[:, :, 0:FC, :]
        ytmp = sb("ytmp", [P, T, D])
        SC = OT[0:3 * R, 0, :]
        SCN = OT[0:3 * R, 1, :]
        TZ = OT[0:2 * R, 2, :]
        G = sb("G", [3 * R, S])
        score = sb("score", [P, NT, E])

        keyhi = KP[:].rearrange("p h n -> p (h n)")[:, 0:2 * E * NT].bitcast(f32).rearrange("p (e t) -> p e t", e=E)
        keylo = KP[:].rearrange("p h n -> p (h n)")[:, 2 * E * NT:4 * E * NT].bitcast(f32).rearrange("p (e t) -> p e t", e=E)
        kwork = QP[:].rearrange("p h n -> p (h n)")[:, 0:2 * E * NT].bitcast(i32).rearrange("p (e t) -> p e t", e=E)
        kwork2 = QP[:].rearrange("p h n -> p (h n)")[:, 2 * E * NT:4 * E * NT].bitcast(i32).rearrange("p (e t) -> p e t", e=E)
        cmp = krest[:, 0:WAYS * NT].rearrange("p (w t) -> p w t", w=WAYS)
        base = sb("base", [P, 2])
        need = sb("need", [P, 1])
        nsel = sb("nsel", [P, 1])
        eq = sb("eq", [P, NT])
        lo2 = sb("lo2", [P, NT])
        sel = sb("sel", [P, NT])
        free = sb("free", [P, NT])
        taken = KP[:].rearrange("p h n -> p (h n)")[:, 4 * E * NT:6 * E * NT].bitcast(f32).rearrange("p (t e) -> p t e", e=E)
        junk = sb("junk", [P, 16])
        hi = sb("hi", [P, NT])

        cnt = sb("cnt", [P, 16], bf16)
        COUNTS = 7 * (2 * len(DIGITS) + 1)

        bank = [ctx.enter_context(nc.psum_tensor(f"bank{i}", [P, S], f32)) for i in range(8)]

        s_const = sem("s_const")
        def later(b):
            return not (isinstance(b, int) and b == 0)

        block = ctx.enter_context(nc.Block())
        names = ("uready x_in x_tok x_T proj q1 r1 q2 q3 vready rearr sa mx nm nmt nmtc mrow st ex pv ocopy ot onorm at atc yo x1 x1t "
                 "x1tc lg comb h gelu y acc x2 x2t x2tc ab g yl x3 n3 n3t n3tc sc scc "
                 "pre prec misc init asn y2 o2 out").split()
        s = {n: sem("s_" + n) for n in names}
        s["ocopy2"] = sem("s_rsqrt")
        s["o3"], s["w"], s["store"] = sem("s_swap"), sem("s_w"), sem("s_store")
        s["spill"] = [sem(f"s_spill{i}") for i in range(PARTS)]
        s["mspill"] = sem("s_mspill")
        q_dram = nc.dram_tensor("q_dram", (PARTS, P, S), bf16, kind="Internal").ap()
        k_dram = nc.dram_tensor("k_dram", (PARTS, P, S), bf16, kind="Internal").ap()
        m_dram = nc.dram_tensor("m_dram", (PARTS * H, S), bf16, kind="Internal").ap()
        dch, ach, pch = sem("s_dve_chain"), sem("s_act_chain"), sem("s_pool_chain")

        loads = [(identf, "identf"), (identb, "identb"), (mask_a, "mask_a"), (mask_t, "mask_t"),
                 (inv_count, "inv_count"), (iota8, "iota8"), (kstep, "kstep"), (tie, "tie"),
                 (wq0, "wq0"), (wk0, "wk0"), (wv0, "wv0"), (wo0, "wo0"), (bo0, "bo0"), (expdb, "denom_bias"), (wg, "wg"),
                 (w1a, "w1a"), (w2a, "w2a"), (b1a, "b1a"), (b2a, "b2a"),
                 (wq1, "wq1"), (wk1, "wk1"), (wo1, "wo1"), (alpha, "alpha"), (cent, "cent"), (lng, "lng"), (lnb, "lnb")]
        n_loads = len(loads) + 8

        @block.sync
        def _(sp):
            for t, n in loads:
                dst = t[:]
                src = I[n]
                if n in ("bo0", "denom_bias", "lng", "lnb", "b2a"):
                    src = src.partition_broadcast(P)
                sp.dma_start(dst, src).then_inc(s_const, 16)
            for dst, n in ((vcat[:, 0:R], "V_b"), (vcat[:, R:2 * R], "V_t"), (vcat[:, 2 * R:3 * R], "V_t"),
                           (wcat[:, 0:R], "W_b"), (wcat[:, R:2 * R], "W_t"), (ucat[:, 0:R], "U_b"), (ucat[:, R:2 * R], "U_t"),
                           (bias_t[:, 0:1], "bias_t")):
                sp.dma_start(dst, I[n]).then_inc(s_const, 16)
            sp.dma_start(wb[:, 2 * R:3 * R], I["X_t"]).then_inc(s["x_in"], 16)
            sp.dma_start(ucat[:, 2 * R:2 * R + 1], I["bias_b"]).then_inc(s["x_in"], 16)
            sp.wait_ge(s["init"], 1)
            def block_steps(b):
                if later(b):
                    sp.wait_ge(s["proj"], b * 3)
                sp.dma_start(xT[:], I["xT"][b, :, :]).then_inc(s["x_T"], 16)
                if later(b):
                    sp.wait_ge(s["x1"], b)
                sp.dma_start(xtok[:], I["x"][b, :, :].rearrange("(t p) d -> p t d", p=P)).then_inc(s["x_tok"], 16)
                if later(b):
                    sp.wait_ge(s["pv"], b * QUADS)
                for part in range(PARTS):
                    sp.wait_ge(s["q1" if part == 0 else "q2" if part == 1 else "q3"], 2 * b + 2)
                    sp.dma_start(q_dram[part], qparts[part][:]).then_inc(s["spill"][part], 16)
                    sp.dma_start(k_dram[part], kparts[part][:]).then_inc(s["spill"][part], 16)
                for part in range(PARTS):
                    sp.wait_ge(s["spill"][part], b * 32 + 32)
                    for dst, src, order in ((QP, q_dram, Q_PART), (KP, k_dram, K_PART)):
                        for g in range(6):
                            if order[g] == part:
                                sp.dma_start(dst[g * HD:(g + 1) * HD, :, :],
                                             src[part].rearrange("(h d) n -> d h n", d=HD)).then_inc(s["rearr"], 16)
                sp.wait_ge(s["nmtc"], b + 1)
                sp.dma_start(m_dram, NMT[:]).then_inc(s["mspill"], 16)
                sp.wait_ge(s["mspill"], b * 16 + 16)
                sp.dma_start(QP[MROW:MROW + PARTS, :, :], m_dram.rearrange("(q h) n -> q h n", q=PARTS)).then_inc(s["mrow"], 16)

            block_steps(0)
            with sp.Fori(1, B) as b:
                block_steps(b)
        QR = 12 * 16

        def ffn(pe, b, src, w1, w2):
            mm = nc.tensor.matmul
            def up(e):
                for f in range(FC):
                    n = e * FC + f
                    if n >= 4:
                        pe.wait_ge(s["gelu"], b * E * FC + n - 3)
                    mm(bank[n % 4][:], w1[:, e, f * P:(f + 1) * P], src, start=True, stop=True).then_inc(s["h"], 1)

            def down(e):
                pe.wait_ge(s["gelu"], b * E * FC + (e + 1) * FC)
                if e >= 2:
                    pe.wait_ge(s["y2"], b * E + e - 1)
                for t in range(T):
                    for f in range(FC):
                        last = mm(bank[4 + e % 2][:, t * P:(t + 1) * P], Hh[:, e % 2, f, t * P:(t + 1) * P], w2[:, e, f, :],
                                  start=(f == 0), stop=(f == FC - 1))
                last.then_inc(s["y"], 1)

            if later(b):
                pe.wait_ge(s["gelu"], b * E * FC)
            if later(b):
                pe.wait_ge(s["y2"], b * E)
            up(0)
            for e in range(1, E):
                up(e)
                down(e - 1)
            down(E - 1)

        @block.tensor
        def _(pe):
            mm, tr = nc.tensor.matmul, nc.tensor.transpose
            pe.wait_ge(s_const, 16 * n_loads)
            pe.wait_ge(s["x_in"], 32)
            pe.wait_ge(s["init"], 3)
            pe.wait_ge(s["uready"], 1)
            mm(bank[0][:, 0:3 * R], wq1[:], vcat[:], start=True, stop=True)
            mm(bank[1][:, 0:2 * R], wk1[:], wcat[:], start=True, stop=True)
            mm(bank[2][0:2 * R + 1, 0:D], ucat[:], wo1[:], start=True, stop=True).then_inc(s["pre"], 1)
            pe.wait_ge(s["prec"], 3)
            def block_steps(b):
                pe.wait_ge(s["x_T"], b * 16 + 16)
                if later(b):
                    pe.wait_ge(s["n3tc"], b)
                if later(b):
                    pe.wait_ge(s["scc"], b)
                mm(bank[0][:], wq0[:], xT[:], start=True, stop=True).then_inc(s["proj"], 1)
                mm(bank[1][:], wk0[:], xT[:], start=True, stop=True).then_inc(s["proj"], 1)
                for t in range(T):
                    last = mm(bank[2][:, t * P:(t + 1) * P], xT[:, t * P:(t + 1) * P], wv0[:], start=True, stop=True)
                last.then_inc(s["proj"], 1)
                pe.wait_ge(s["rearr"], b * QR + QR)
                pe.wait_ge(s["r1"], 2 * b + 2)
                pe.wait_ge(s["vready"], b + 1)

                def qk(bk, cols, h, t, mask):
                    n = (t + 1) * P
                    mm(bk[:, cols:cols + n], QP[0:MROW, h, t * P:(t + 1) * P], KP[0:MROW, h, 0:n], start=True, stop=False)
                    return mm(bk[:, cols + n - P:cols + n], identb[:], mask[:], start=False, stop=True)

                def kq(bk, cols, h, u, mask):
                    n = S - u * P
                    mm(bk[:, cols:cols + n], KP[:, h, u * P:(u + 1) * P], QP[:, h, u * P:S], start=True, stop=False)
                    return mm(bk[:, cols:cols + P], identb[:], mask[:], start=False, stop=True)

                for q in range(QUADS):
                    for k in range(UNITS):
                        n = q * UNITS + k
                        if n >= 3:
                            pe.wait_ge(s["mx"], b * 40 + n - 2)
                        bk = bank[n % 3]
                        h = 4 * q + k % 4
                        if k < 4:
                            last = qk(bk, 0, h, 3, mask_a)
                        elif k < 8:
                            qk(bk, 0, h, 2, mask_a)
                            last = qk(bk, 3 * P, h, 0, mask_a)
                        else:
                            h = 4 * q + 2 * (k - 8)
                            qk(bk, 0, h, 1, mask_a)
                            last = qk(bk, 2 * P, h + 1, 1, mask_a)
                        last.then_inc(s["sa"], 1)
                pe.wait_ge(s["nm"], b + 1)
                for t in range(T):
                    last = tr(bank[7][:].bitcast(bf16)[:, t * P:(t + 1) * P], NM[:, t, :, :], identb[:])
                last.then_inc(s["nmt"], 1)
                pe.wait_ge(s["mrow"], (b + 1) * 16)
                pe.wait_ge(s["nmtc"], b + 1)

                def pv(q):
                    ob = bank[6 + q % 2]
                    if q >= 2:
                        pe.wait_ge(s["ocopy"], b * QUADS + q - 1)
                    pr = PR[:, q % 2]
                    for u in (0, 1, 3, 2):
                        n = S - u * P
                        for j in range(4):
                            h = 4 * q + j
                            src = {0: pr[:, j, 0:n], 1: pr[:, 4 + j, 0:n], 3: pr[:, 4 + j, 3 * P:4 * P],
                                   2: pr[:, 8 + j // 2, (j % 2) * 2 * P:(j % 2 + 1) * 2 * P]}[u]
                            last = mm(ob[32 * j:32 * j + 32, u * P:S], Vaug[:, u, h, :], src, start=(u == 0), stop=(u == 2))
                    last.then_inc(s["pv"], 1)

                for q in range(QUADS):
                    for k in range(UNITS):
                        n = q * UNITS + k
                        if n >= 3:
                            pe.wait_ge(s["ex"], b * 40 + n - 2)
                        bk = bank[3 + n % 3]
                        h = 4 * q + k % 4
                        if k < 4:
                            last = kq(bk, 0, h, 0, mask_t)
                        elif k < 8:
                            kq(bk, 0, h, 1, mask_t)
                            last = kq(bk, 3 * P, h, 3, mask_t)
                        else:
                            h = 4 * q + 2 * (k - 8)
                            kq(bk, 0, h, 2, mask_t)
                            last = kq(bk, 2 * P, h + 1, 2, mask_t)
                        last.then_inc(s["st"], 1)
                        if k == 3 and q >= 1:
                            pe.wait_ge(s["ex"], b * 40 + q * UNITS)
                            pv(q - 1)
                pe.wait_ge(s["ex"], b * 40 + 40)
                pv(QUADS - 1)
                pe.wait_ge(s["ocopy"], (b + 1) * QUADS)
                pe.wait_ge(s["mx"], b * 40 + 40)
                for t in range(T):
                    for q in range(QUADS):
                        last = tr(bank[t][:, q * P:(q + 1) * P], OT[:, q, t * P:(t + 1) * P], identf[:])
                    last.then_inc(s["ot"], 1)
                pe.wait_ge(s["onorm"], b + 1)
                for t in range(T):
                    last = tr(bank[4][:, t * P:(t + 1) * P], att[:, t, :], identf[:])
                last.then_inc(s["at"], 1)
                pe.wait_ge(s["atc"], b + 1)
                for t in range(T):
                    last = mm(bank[5][:, t * P:(t + 1) * P], attT[:, t * P:(t + 1) * P], wo0[:], start=True, stop=True)
                last.then_inc(s["yo"], 1)
                pe.wait_ge(s["x1"], b + 1)
                for t in range(T):
                    last = tr(bank[6][:, t * P:(t + 1) * P], X1[:, t, :], identf[:])
                last.then_inc(s["x1t"], 1)
                pe.wait_ge(s["x1tc"], b + 1)
                for t in range(T):
                    last = mm(bank[7][:, t * E:(t + 1) * E], X1T[:, t * P:(t + 1) * P], wg[:], start=True, stop=True)
                last.then_inc(s["lg"], 1)
                ffn(pe, b, X1T[:], w1a, w2a)
                pe.wait_ge(s["x2"], b + 1)
                for t in range(T):
                    last = tr(bank[6][:, t * P:(t + 1) * P], X2[:, t, :], identf[:])
                last.then_inc(s["x2t"], 1)
                pe.wait_ge(s["x2tc"], b + 1)
                mm(bank[0][0:3 * R, :], wa[:], X2T[:], start=True, stop=True)
                mm(bank[1][0:3 * R, :], wb[:], X2T[:], start=True, stop=True).then_inc(s["ab"], 1)
                pe.wait_ge(s["g"], b + 1)
                for t in range(T):
                    last = mm(bank[2][:, t * P:(t + 1) * P], G[0:2 * R + 1, t * P:(t + 1) * P], uc[:], start=True, stop=True)
                last.then_inc(s["yl"], 1)
                pe.wait_ge(s["n3"], b + 1)
                for t in range(T):
                    last = tr(bank[6][:, t * P:(t + 1) * P], res[:, t, :], identf[:])
                last.then_inc(s["n3t"], 1)
                pe.wait_ge(s["n3tc"], b + 1)
                for t in range(T):
                    last = mm(bank[7][:, t * E:(t + 1) * E], attT[:, t * P:(t + 1) * P], cent[:], start=True, stop=True)
                last.then_inc(s["sc"], 1)

            block_steps(0)
            with pe.Fori(1, B) as b:
                block_steps(b)
            pe.wait_ge(s["scc"], B)
            for n in range(COUNTS):
                pe.wait_ge(s["asn"], n + 1)
                mm(bank[0][:, 0:16], onesb[:], cnt[:, :], start=True, stop=True).then_inc(s["misc"], 1)
            pe.wait_ge(s["o2"], 1)
            def block_steps(b):
                ffn(pe, b + B, N3T[:, b, :], w1a, w2a)

            block_steps(0)
            with pe.Fori(1, B) as b:
                block_steps(b)
        @block.scalar
        def _(act):
            A = nc.scalar.activation
            Cp, Id = ACT.Copy, ACT.Identity

            def gelu(b, b1):
                for e in range(E):
                    if e >= 2:
                        act.wait_ge(s["y"], b * E + e - 1)
                    else:
                        if later(b):
                            act.wait_ge(s["y"], b * E)
                    for f in range(FC):
                        act.wait_ge(s["h"], b * E * FC + e * FC + f + 1)
                        A(Hh[:, e % 2, f, :], bank[(e * FC + f) % 4][:], ACT.Gelu_apprx_tanh, bias=b1[:, e, f:f + 1]).then_inc(s["gelu"], 1)

            act.wait_ge(s_const, 16 * n_loads)
            act.wait_ge(s["init"], 3)
            A(expdb[:], expdb[:], ACT.Exp).then_inc(s["prec"], 1)
            def block_steps(b):
                for i, (dst, bk) in enumerate(((qparts[0], 0), (kparts[0], 1))):
                    act.wait_ge(s["proj"], 3 * b + i + 1)
                    if later(b):
                        act.wait_ge(s["rearr"], b * QR)
                    A(dst[:], bank[bk][:], Cp).then_inc(s["q1"], 1)
                act.wait_ge(s["proj"], 3 * b + 3)
                if later(b):
                    act.wait_ge(s["pv"], b * QUADS)
                A(Vaug[:, :, :, 0:HD], bank[2][:].rearrange("p (t h d) -> p t h d", t=T, h=H), Cp).then_inc(s["vready"], 1)
                for i, (dst, src) in enumerate(((qparts[1], qrest), (kparts[1], krest))):
                    act.wait_ge(s["r1"], 2 * b + i + 1)
                    A(dst[:], src[:], Cp).then_inc(s["q2"], 1)
                act.wait_ge(s["nmt"], b + 1)
                if later(b):
                    act.wait_ge(s["mrow"], b * 16)
                A(NMT[:], bank[7][:].bitcast(bf16)[0:PARTS * H, 0:S], Cp).then_inc(s["nmtc"], 1)

                def ocopy(q):
                    if q == 0:
                        if later(b):
                            act.wait_ge(s["g"], b)
                    act.wait_ge(s["pv"], b * QUADS + q + 1)
                    A(OT[:, q, :], bank[6 + q % 2][:], Cp).then_inc(s["ocopy"], 1)

                for q in range(QUADS):
                    for k in range(UNITS):
                        n = q * UNITS + k
                        act.wait_ge(s["st"], b * 40 + n + 1)
                        if k == 0 and q >= 2:
                            act.wait_ge(s["pv"], b * QUADS + q - 1)
                        if k == 0 and q == 0:
                            if later(b):
                                act.wait_ge(s["ot"], b * T)
                            if later(b):
                                act.wait_ge(s["y"], b * E)
                        A(PR[:, q % 2, k, :], bank[3 + n % 3][:], ACT.Exp, scale=SCALE).then_inc(s["ex"], 1)
                    if q >= 1:
                        ocopy(q - 1)
                ocopy(QUADS - 1)
                act.wait_ge(s["at"], b + 1)
                A(attT[:], bank[4][:], Cp).then_inc(s["atc"], 1)
                act.wait_ge(s["x1t"], b + 1)
                A(X1T[:], bank[6][:], Cp).then_inc(s["x1tc"], 1)
                act.wait_ge(s["misc"], b + 1)
                A(gate[:, :, 1], gate[:, :, 0], ACT.Exp).then_inc(s["pre"], 1)
                gelu(b, b1a)
                act.wait_ge(s["x2t"], b + 1)
                A(X2T[:], bank[6][:], Cp).then_inc(s["x2tc"], 1)
                act.wait_ge(s["n3t"], b + 1)
                A(attT[:], bank[6][:], Cp).then_inc(ach, 1)
                act.wait_ge(ach, b + 1)
                A(N3T[:, b, :], attT[:], Cp).then_inc(s["n3tc"], 1)

            block_steps(0)
            with act.Fori(1, B) as b:
                block_steps(b)
            act.wait_ge(s["o2"], 1)
            def block_steps(b):
                gelu(b + B, b1a)

            block_steps(0)
            with act.Fori(1, B) as b:
                block_steps(b)
        @block.gpsimd
        def _(pool):
            g = nc.gpsimd
            g.memset(QP[:], 0.0).then_inc(s["init"], 1)
            pool.wait_ge(s["init"], 1)
            g.memset(onesf[:], 1.0)
            g.memset(onesb[:], 1.0)
            g.memset(half[:], -0.5)
            g.memset(NM[:], 0.0)
            g.memset(G[:], 1.0)
            g.memset(KP[:], 0.0).then_inc(pch, 1)
            pool.wait_ge(pch, 1)
            g.memset(KP[MROW:P, :, :], 1.0).then_inc(pch, 1)
            pool.wait_ge(pch, 2)
            g.memset(Vaug[:], 0.0).then_inc(pch, 1)
            pool.wait_ge(pch, 3)
            g.memset(Vaug[:, :, :, HD:HD + 1], 1.0).then_inc(s["init"], 2)

            def rsqrt(n):
                pool.wait_ge(s["out"], n)
                g.tensor_tensor(rstd[:], rstd[:], half[:], ALU.pow).then_inc(s["ocopy2"], 1)

            def block_steps(b):
                for i, (dst, src, sub) in enumerate(((qparts[2], qrest, qparts[1]), (kparts[2], krest, kparts[1]))):
                    pool.wait_ge(s["q2"], 2 * b + i + 1)
                    g.tensor_tensor(dst[:], src[:], sub[:], ALU.subtract).then_inc(s["q3"], 1)
                for k in range(4):
                    rsqrt(b * 4 + k + 1)

            block_steps(0)
            with pool.Fori(1, B) as b:
                block_steps(b)
            def block_steps(b):
                rsqrt(4 * B + b + 1)

            block_steps(0)
            with pool.Fori(1, B) as b:
                block_steps(b)
        @block.vector
        def _(dve):
            v = nc.vector
            state = {"n": 0, "per": 0, "off": 0}

            def link(ins):
                ins.then_inc(dch, 1)
                state["n"] += 1
                dve.wait_ge(dch, state["off"] + state["n"])

            def layer_norm(dst, src, count):
                for t in range(T):
                    last = v.bn_stats(stats[:, t, :], src[:, t, :])
                link(last)
                v.tensor_copy(junk[:, 0:1], half[:, 0:1])
                for t in range(T):
                    last = v.bn_aggr(mv[:, t, :], stats[:, t, :])
                link(last)
                v.tensor_scalar(rstd[:], mv[:, :, 1], EPS, None, ALU.add).then_inc(s["out"], 1)
                dve.wait_ge(s["ocopy2"], count)
                for t in range(T):
                    last = v.tensor_scalar(dst[:, t, :], src[:, t, :], mv[:, t, 0:1], rstd[:, t:t + 1], ALU.subtract, ALU.mult)
                return last

            def combine(b, acc, weights):
                for e in range(E):
                    dve.wait_ge(s["y"], b * E + e + 1)
                    y = bank[4 + e % 2][:].rearrange("p (t d) -> p t d", t=T)
                    v.tensor_tensor(ytmp[:], y, b2a[:, e:e + 1, :].to_broadcast([P, T, D]), ALU.add).then_inc(s["y2"], 1)
                    dve.wait_ge(s["y2"], b * E + e + 1)
                    for t in range(T):
                        last = v.scalar_tensor_tensor(acc[:, t, :], ytmp[:, t, :], weights(t, e), acc[:, t, :], ALU.mult, ALU.add)
                    link(last)

            dve.wait_ge(s_const, 16 * n_loads)
            dve.wait_ge(s["x_in"], 32)
            v.tensor_scalar(ucat[:, R:2 * R], ucat[:, R:2 * R], alpha[:], None, ALU.mult)
            v.scalar_tensor_tensor(ucat[:, 2 * R:2 * R + 1], bias_t[:], alpha[:], ucat[:, 2 * R:2 * R + 1], ALU.mult,
                                   ALU.add).then_inc(s["uready"], 1)
            dve.wait_ge(s["pre"], 1)
            v.tensor_copy(wa[:], bank[0][:, 0:3 * R])
            v.tensor_copy(wb[:, 0:2 * R], bank[1][:, 0:2 * R])
            v.tensor_copy(uc[:], bank[2][0:2 * R + 1, 0:D]).then_inc(s["prec"], 2)

            def body(b):
                for i, (rest, p0, bk) in enumerate(((qrest, qparts[0], 0), (krest, kparts[0], 1))):
                    dve.wait_ge(s["q1"], 2 * b + i + 1)
                    if later(b):
                        dve.wait_ge(s["q3"], 2 * b)
                    v.tensor_tensor(rest[:], bank[bk][:], p0[:], ALU.subtract).then_inc(s["r1"], 1)
                for q in range(QUADS):
                    for k in range(UNITS):
                        n = q * UNITS + k
                        dve.wait_ge(s["sa"], b * 40 + n + 1)
                        bk = bank[n % 3]
                        h = 4 * q + k % 4
                        if k < 4:
                            last = v.tensor_reduce(M[:, 3, h:h + 1], bk[:], AX.X, ALU.max)
                        elif k < 8:
                            v.tensor_reduce(M[:, 2, h:h + 1], bk[:, 0:3 * P], AX.X, ALU.max)
                            last = v.tensor_reduce(M[:, 0, h:h + 1], bk[:, 3 * P:4 * P], AX.X, ALU.max)
                        else:
                            h = 4 * q + 2 * (k - 8)
                            last = v.tensor_reduce(M[:, 1, h:h + 2], bk[:].rearrange("p (h n) -> p h n", h=2), AX.X, ALU.max)
                        last.then_inc(s["mx"], 1)
                dve.wait_ge(s["mx"], b * 40 + 40)
                link(v.tensor_scalar(NM[:, :, 0, :], M[:], -1.0, None, ALU.mult))
                link(v.scalar_tensor_tensor(mrest[:], M[:], -1.0, NM[:, :, 0, :], ALU.mult, ALU.subtract))
                link(v.tensor_copy(NM[:, :, 1, :], mrest[:]))
                v.tensor_tensor(NM[:, :, 2, :], mrest[:], NM[:, :, 1, :], ALU.subtract).then_inc(s["nm"], 1)
                dve.wait_ge(s["x_tok"], b * 16 + 16)
                v.tensor_tensor(res[:], xtok[:], bo0[:].rearrange("p (o d) -> p o d", o=1).to_broadcast([P, T, D]), ALU.add)
                for t in range(T):
                    dve.wait_ge(s["ot"], b * T + t + 1)
                    o = bank[t][:].rearrange("p (h c) -> p h c", h=H)
                    link(v.tensor_tensor(den[:, t, :], o[:, :, HD], expdb[:], ALU.add))
                    link(v.reciprocal(den[:, t, :], den[:, t, :]))
                    last = v.tensor_tensor(att[:, t, :].rearrange("p (h d) -> p h d", h=H), o[:, :, 0:HD],
                                           den[:, t, :].rearrange("p (h o) -> p h o", o=1).to_broadcast([P, H, HD]), ALU.mult)
                last.then_inc(s["onorm"], 1)
                dve.wait_ge(s["yo"], b + 1)
                link(v.tensor_tensor(res[:], bank[5][:].rearrange("p (t d) -> p t d", t=T), res[:], ALU.add))
                layer_norm(X1, res, 4 * b + 1).then_inc(s["x1"], 1)
                dve.wait_ge(s["lg"], b + 1)
                link(v.tensor_copy(logit[:], bank[7][:, 0:T * E].rearrange("p (t e) -> p t e", t=T)))
                v.tensor_copy(junk[:, 0:1], half[:, 0:1])
                for t in range(T):
                    last = v.max(top[:, t, :], logit[:, t, :])
                link(last)
                v.tensor_copy(junk[:, 1:2], half[:, 0:1])
                for t in range(T):
                    last = v.max_index(topi[:, t, :], top[:, t, :], logit[:, t, :])
                link(v.tensor_tensor(gate[:, :, 0], top[:, :, 1], top[:, :, 0], ALU.subtract))
                link(v.tensor_copy(topf[:], topi[:]))
                v.tensor_copy(junk[:, 0:1], half[:, 0:1]).then_inc(s["misc"], 1)
                dve.wait_ge(s["pre"], b + 2)
                link(v.tensor_scalar(gate[:, :, 0], gate[:, :, 1], 1.0, None, ALU.add))
                link(v.reciprocal(gate[:, :, 0], gate[:, :, 0]))
                link(v.tensor_tensor(gate[:, :, 1], gate[:, :, 1], gate[:, :, 0], ALU.mult))
                for t in range(T):
                    v.tensor_scalar(comb[:, t, :], iota8[:], topf[:, t, 0:1], gate[:, t, 0:1], ALU.is_equal, ALU.mult)
                    last = v.tensor_scalar(comb2[:, t, :], iota8[:], topf[:, t, 1:2], gate[:, t, 1:2], ALU.is_equal, ALU.mult)
                link(last)
                link(v.tensor_tensor(comb[:], comb[:], comb2[:], ALU.add))
                link(v.tensor_copy(res[:], X1[:]))
                combine(b, res, lambda t, e: comb[:, t, e:e + 1])
                layer_norm(X2, res, 4 * b + 2).then_inc(s["x2"], 1)
                dve.wait_ge(s["ab"], b + 1)
                link(v.tensor_tensor_scan(SC, onesf[0:3 * R, :], bank[1][0:3 * R, :], 0.0, ALU.mult, ALU.add))
                link(v.tensor_tensor(SCN, SC, inv_count[0:3 * R, :], ALU.mult))
                v.tensor_tensor(G[0:R, :], bank[0][0:R, :], SCN[0:R, :], ALU.mult)
                link(v.tensor_tensor(TZ[R:2 * R, :], bank[0][2 * R:3 * R, :], SCN[2 * R:3 * R, :], ALU.mult))
                v.tensor_tensor(G[R:2 * R, :], TZ[R:2 * R, :], SCN[R:2 * R, :], ALU.mult).then_inc(s["g"], 1)
                dve.wait_ge(s["yl"], b + 1)
                link(v.tensor_tensor(res[:], bank[2][:].rearrange("p (t d) -> p t d", t=T), X2[:], ALU.add))
                link(layer_norm(ytmp, res, 4 * b + 3))
                link(v.tensor_copy(X3[:, bass.ds(b * T, T), :], ytmp[:]))
                link(layer_norm(res, ytmp, 4 * b + 4))
                link(v.tensor_tensor(res[:], res[:], lng[:].rearrange("p (o d) -> p o d", o=1).to_broadcast([P, T, D]), ALU.mult))
                v.tensor_tensor(res[:], res[:], lnb[:].rearrange("p (o d) -> p o d", o=1).to_broadcast([P, T, D]), ALU.add).then_inc(s["n3"], 1)
                dve.wait_ge(s["sc"], b + 1)
                v.tensor_copy(score[:, bass.ds(b * T, T), :], bank[7][:, 0:T * E].rearrange("p (t e) -> p t e", t=T)).then_inc(s["scc"], 1)

            PER = 38 + E
            def block_steps(b):
                state["off"], state["n"] = b * PER, 0
                body(b)

            block_steps(0)
            with dve.Fori(1, B) as b:
                block_steps(b)
            assert state["n"] == PER, state["n"]
            state["off"], state["n"] = 0, B * PER
            dve.wait_ge(s["scc"], B)
            link(v.tensor_copy(kwork.bitcast(f32), score[:].rearrange("p t e -> p e t")))
            link(v.tensor_scalar(kwork2, kwork, 31, None, ALU.arith_shift_right))
            link(v.tensor_scalar(kwork2, kwork2, -2147483648, None, ALU.bitwise_or))
            link(v.tensor_tensor(kwork, kwork, kwork2, ALU.bitwise_xor))
            link(v.tensor_scalar(kwork2, kwork, 10, None, ALU.logical_shift_right))
            link(v.tensor_copy(keyhi, kwork2))
            link(v.tensor_scalar(kwork2, kwork, 1023, 12, ALU.bitwise_and, ALU.logical_shift_left))
            link(v.tensor_copy(keylo, kwork2))
            link(v.tensor_tensor(keylo, keylo, tie[:].rearrange("p (o t) -> p o t", o=1).to_broadcast([P, E, NT]), ALU.add))
            v.memset(cnt[:], 0.0)
            link(v.memset(free[:], 1.0))
            rounds = [0]

            def total(ins):
                link(ins)
                v.tensor_copy(junk[:, 0:1], half[:, 0:1]).then_inc(s["asn"], 1)
                rounds[0] += 1
                dve.wait_ge(s["misc"], B + rounds[0])

            def search(keys, want, col):
                link(v.memset(base[:, col:col + 1], 0.0))
                for d in range(len(DIGITS)):
                    ways = 15 if DIGITS[d] > 0 else 3
                    k3 = keys.rearrange("p (o t) -> p o t", o=1).to_broadcast([P, ways, NT])
                    st = kstep[:, d, 0:ways].rearrange("p (w o) -> p w o", o=1).to_broadcast([P, ways, NT])
                    link(v.scalar_tensor_tensor(cmp[:, 0:ways, :], k3, base[:, col:col + 1], st, ALU.subtract, ALU.is_ge))
                    with nc.allow_low_precision(reason="counts up to 32 are exact"):
                        ins = v.tensor_reduce(cnt[:, 0:ways], cmp[:, 0:ways, :], AX.X, ALU.add)
                    total(ins)
                    link(v.tensor_scalar(junk[:, 0:ways], bank[0][:, 0:ways], want, None, ALU.is_ge, ALU.add, accum_out=nsel[:]))
                    link(v.scalar_tensor_tensor(base[:, col:col + 1], nsel[:], float(2 ** DIGITS[d]), base[:, col:col + 1], ALU.mult, ALU.add))

            for e in range(E - 1):
                link(v.scalar_tensor_tensor(hi[:], keyhi[:, e, :], 1.0, free[:], ALU.add, ALU.mult))
                link(v.tensor_scalar(hi[:], hi[:], 1.0, None, ALU.subtract))
                search(hi[:], float(CAP), 0)
                link(v.tensor_scalar(sel[:], hi[:], base[:, 0:1], None, ALU.is_gt))
                with nc.allow_low_precision(reason="counts up to 32 are exact"):
                    ins = v.tensor_reduce(cnt[:, 0:1], sel[:], AX.X, ALU.add)
                total(ins)
                link(v.tensor_scalar(need[:], bank[0][:, 0:1], -1.0, float(CAP), ALU.mult, ALU.add))
                link(v.tensor_scalar(eq[:], hi[:], base[:, 0:1], None, ALU.is_equal))
                link(v.scalar_tensor_tensor(lo2[:], keylo[:, e, :], 1.0, eq[:], ALU.add, ALU.mult))
                link(v.tensor_scalar(lo2[:], lo2[:], 1.0, None, ALU.subtract))
                search(lo2[:], need[:], 1)
                link(v.scalar_tensor_tensor(sel[:], lo2[:], base[:, 1:2], sel[:], ALU.is_ge, ALU.add))
                link(v.tensor_copy(taken[:, :, e], sel[:]))
                link(v.tensor_tensor(free[:], free[:], sel[:], ALU.subtract))
            assert rounds[0] == COUNTS
            link(v.tensor_copy(taken[:, :, E - 1], free[:]))
            v.tensor_copy(junk[:, 0:1], half[:, 0:1]).then_inc(s["o3"], 1)
            dve.wait_ge(s["w"], 64)
            v.tensor_copy(junk[:, 1:2], half[:, 0:1]).then_inc(s["o2"], 1)
            n0 = state["n"]
            PER2 = 5 + E
            def block_steps(b):
                state["off"], state["n"] = b * PER2 + n0, 0
                link(v.tensor_copy(X1[:], X3[:, bass.ds(b * T, T), :]))
                link(v.tensor_tensor(res[:], X1[:], X1[:], ALU.add))
                link(v.tensor_copy(comb[:], taken[:, bass.ds(b * T, T), :]))
                combine(b + B, res, lambda t, e: comb[:, t, e:e + 1])
                if later(b):
                    dve.wait_ge(s["store"], b * 16)
                layer_norm(X2, res, 4 * B + b + 1).then_inc(s["x2"], 1)
                assert state["n"] == PER2, state["n"]

            block_steps(0)
            with dve.Fori(1, B) as b:
                block_steps(b)
        @block.sync
        def _(sp):
            sp.wait_ge(s["o3"], 1)
            sp.wait_ge(s["y"], B * E)
            for t, n in ((w1a, "w1b"), (w2a, "w2b"), (b1a, "b1b"), (b2a, "b2b")):
                src = I[n]
                if n == "b2b":
                    src = src.partition_broadcast(P)
                sp.dma_start(t[:], src).then_inc(s["w"], 16)
            def block_steps(b):
                sp.wait_ge(s["x2"], B + b + 1)
                sp.dma_start(out[b, :, :].rearrange("(t p) d -> p t d", p=P), X2[:]).then_inc(s["store"], 16)

            block_steps(0)
            with sp.Fori(1, B) as b:
                block_steps(b)
            sp.wait_ge(s["store"], 16 * B)


def kernel(**inputs):
    import numpy as np
    import ml_dtypes
    import concourse.bacc as bacc
    from concourse import mybir as mb
    from concourse.bass_utils import run_bass_kernel_spmd as run

    nc = bacc.Bacc("TRN2", target_bir_lowering=False, num_devices=1)
    a = {k: np.asarray(x) for k, x in inputs.items()}
    w = lambda name: a[name]
    p = np.arange(128)
    i512 = np.arange(512)
    big = -3.0e38
    bf = ml_dtypes.bfloat16
    digits = [18, 14, 10, 6, 2, 0]
    arr = {
        "identf": np.eye(128, dtype=np.float32), "identb": np.eye(128).astype(bf),
        "mask_a": np.where(p[None, :] > p[:, None], big, 0.0).astype(bf),
        "mask_t": np.where(p[:, None] > p[None, :], big, 0.0).astype(bf),
        "inv_count": np.broadcast_to((1.0 / (1.0 + i512)).astype(np.float32), (128, 512)),
        "iota8": np.broadcast_to(np.arange(8, dtype=np.float32), (128, 8)),
        "kstep": np.broadcast_to(np.array([[float((k + 1) << d) for k in range(15)] for d in digits + [0]], np.float32), (128, 7, 15)),
        "tie": (4095 - (np.arange(32)[None, :] * 128 + p[:, None])).astype(np.float32),
        "x": a["L0_attn_x"], "xT": a["L0_attn_x"].transpose(0, 2, 1),
        "wq0": a["L0_attn_Wq"].T, "wk0": a["L0_attn_Wk"].T, "wv0": a["L0_attn_Wv"].T, "wo0": a["L0_attn_Wo"].T,
        "bo0": a["L0_attn_bo"], "denom_bias": a["L0_attn_denom_bias"].reshape(16), "wg": a["L0_ffn_Wg"],
        "wq1": a["L1_attn_Wq"], "wk1": a["L1_attn_Wk"], "wo1": a["L1_attn_Wo"].T,
        "V_b": a["L1_attn_V_b"], "V_t": a["L1_attn_V_t"], "W_b": a["L1_attn_W_b"], "W_t": a["L1_attn_W_t"],
        "U_b": a["L1_attn_U_b"], "U_t": a["L1_attn_U_t"], "X_t": a["L1_attn_X_t"],
        "bias_b": a["L1_attn_bias_b"].reshape(128, 1), "bias_t": a["L1_attn_bias_t"].reshape(128, 1),
        "alpha": np.broadcast_to(a["L1_attn_alpha"].reshape(1, 1), (128, 1)),
        "cent": a["L1_ffn_centroids"].T, "lng": a["L1_ffn_ln_g"], "lnb": a["L1_ffn_ln_b"],
    }
    for tag, w1, b1, w2, b2 in (("a", "L0_ffn_W1", "L0_ffn_b1", "L0_ffn_W2", "L0_ffn_b2"), ("b", "L1_ffn_w1", "L1_ffn_b1", "L1_ffn_w2", "L1_ffn_b2")):
        arr["w1" + tag] = a[w1].transpose(1, 0, 2)
        arr["w2" + tag] = a[w2].reshape(8, 4, 128, 128).transpose(2, 0, 1, 3)
        arr["b1" + tag] = a[b1].reshape(8, 4, 128).transpose(2, 0, 1)
        arr["b2" + tag] = a[b2]
    arrays, I = {}, {}
    for n, x in arr.items():
        x = np.ascontiguousarray(x)
        arrays["in_" + n] = x
        I[n] = nc.dram_tensor("in_" + n, x.shape, mb.dt.from_np(x.dtype), kind="ExternalInput").ap()
    out = nc.dram_tensor("out_x", (8, 512, 128), mb.dt.float32, kind="ExternalOutput").ap()
    sequence_stack_kernel(nc, I, out)
    r = run(nc, [arrays], core_ids=[0])
    return r.results[0]["out_x"]
```

```python
import concourse.bass as bass
from concourse import mybir
from contextlib import ExitStack


def sequence_stack_kernel(nc, I, out):
    f32 = mybir.dt.float32
    bf16 = mybir.dt.bfloat16
    i32 = mybir.dt.int32
    u32 = mybir.dt.uint32
    ALU = mybir.AluOpType
    ACT = mybir.ActivationFunctionType
    AX = mybir.AxisListType
    Cp = ACT.Copy

    B, S, D = 8, 512, 128
    P = 128
    T = S // P
    H, HD = 16, 8
    E, F = 8, 512
    FC = F // P
    R = 32
    NT = B * T
    CAP = B * S // E
    PARTS = 3
    MROW = 96
    SCALE = float(HD) ** -0.5
    EPS = 1e-5
    QUADS = H // 4
    UNITS = 10
    UB = QUADS * UNITS
    Q_PART = [0, 0, 1, 1, 0, 2]
    K_PART = [0, 1, 0, 1, 2, 0]
    HH = H // 2
    MCOLS = P // HH
    STRIDE = B * S + P
    TILES = 2 * B * S // P + E
    DUMP = E * STRIDE
    DIGITS = [18, 14, 10, 6, 2, 0]
    WAYS = 15
    COUNTS = (E - 1) * (2 * len(DIGITS) + 1)

    ctx = ExitStack()
    with ctx:
        def sb(name, shape, dt=f32):
            return ctx.enter_context(nc.sbuf_tensor(name, shape, dt))

        def sem(name):
            return ctx.enter_context(nc.semaphore("s_" + name))

        def later(b):
            return not (isinstance(b, int) and b == 0)

        def spread_count(n, buf):
            return 12 * 16 // 2 * (n - buf) + 12 * 16

        identf = sb("identf", [P, P])
        identb = sb("identb", [P, P], bf16)
        mask_a = sb("mask_a", [P, P], bf16)
        mask_t = sb("mask_t", [P, P], bf16)
        before = sb("before", [P, P], bf16)
        onesb = sb("onesb", [P, P], bf16)
        inv_count = sb("inv_count", [3 * R, S])
        iota8 = sb("iota8", [P, E])
        ebase = sb("ebase", [P, E])
        pad_row = sb("pad_row", [P, E])
        kstep = sb("kstep", [P, len(DIGITS), WAYS])
        tie = sb("tie", [P, NT])
        jrow = sb("jrow", [P, 2, TILES])
        half = sb("half", [P, T])
        wq0 = sb("wq0", [P, D])
        wk0 = sb("wk0", [P, D])
        wv0 = sb("wv0", [P, D])
        wo0 = sb("wo0", [P, D])
        bo0 = sb("bo0", [P, D])
        expdb = sb("expdb", [P, H])
        wg = sb("wg", [P, E])
        wq1 = sb("wq1", [P, D])
        wk1 = sb("wk1", [P, D])
        wo1 = sb("wo1", [P, D])
        vcat = sb("vcat", [P, 3 * R])
        wcat = sb("wcat", [P, 2 * R])
        ucat = sb("ucat", [P, 2 * R + 1])
        bias_t = sb("bias_t", [P, 1])
        alpha = sb("alpha", [P, 1])
        wa = sb("wa", [P, 3 * R])
        wb = sb("wb", [P, 3 * R])
        uc = sb("uc", [2 * R + 1, D])
        cent = sb("cent", [P, E])
        lng = sb("lng", [P, D])
        lnb = sb("lnb", [P, D])
        w1 = sb("w1", [P, E, F])
        w2 = sb("w2", [P, E, FC, D])
        b1c = sb("b1c", [P, E, FC])
        POS = sb("POS", [P, NT, 2])
        GATE = sb("GATE", [P, NT, 2])
        res = sb("res", [P, T, D])
        stats = sb("stats", [P, T, 6])
        mv = sb("mv", [P, T, 2])
        rstd = sb("rstd", [P, T])
        junk = sb("junk", [P, 16])
        pool_junk = sb("pool_junk", [P, 4])
        Xb = [sb(f"Xb{i}", [P, T, D]) for i in range(2)]
        posb = [sb(f"posb{i}", [P, T, 2], i32) for i in range(2)]
        run = sb("run", [P, E])
        zeros = sb("zeros", [P, D])

        arena = sb("arena", [P, 30300])
        place = [0]

        def at(n, shape, dt=f32):
            size = 1
            for x in shape:
                size *= x
            words = size * (2 if dt == bf16 else 4) // 4
            a = arena[:, place[0]:place[0] + words]
            place[0] += words
            assert place[0] <= 30300, (n, place[0])
            if dt != f32:
                a = a.bitcast(dt)
            names = " ".join("abcd"[:len(shape)])
            if len(shape) == 1:
                return a
            return a.rearrange(f"p ({names}) -> p {names}", **{"abcd"[i]: shape[i] for i in range(len(shape))})

        QP = [at("QP", [H, S], bf16) for i in range(2)]
        KP = [at("KP", [H, S], bf16) for i in range(2)]
        PR = at("PR", [2, UNITS, S])
        xT = [at("xT", [S]) for i in range(2)]
        qparts = [at("q", [S], bf16) for i in range(PARTS)]
        kparts = [at("k", [S], bf16) for i in range(PARTS)]
        qrest = at("qrest", [S])
        krest = at("krest", [S])
        NM = [sb(f"NM{i}", [P, T, MCOLS, HH], bf16) for i in range(2)]
        NMT = [sb(f"NMT{i}", [PARTS * HH, S], bf16) for i in range(2)]
        mrest = sb("mrest", [P, T, HH])
        M = sb("M", [P, T, H])
        Vaug = [sb(f"Vaug{i}", [P, T, H, 32]) for i in range(2)]
        OT = [sb(f"OT{i}", [P, S]) for i in range(2)]
        den = sb("den", [P, T, 4])
        att = sb("att", [P, T, D])
        attT = sb("attT", [P, S])
        xres = sb("xres", [P, T, D])
        X1T = sb("X1T", [P, S])
        logit = sb("logit", [P, T, E])
        top = sb("top", [P, T, 8])
        topi = sb("topi", [P, T, 8], u32)
        topf = sb("topf", [P, T, 8])
        gate = sb("gate", [P, T, 2])
        oh = sb("oh", [P, 2, T, E])
        ohb = sb("ohb", [P, T, E], bf16)
        tpre = sb("tpre", [P, T + 1, E])
        posf = sb("posf", [P, T, E])
        pos2 = sb("pos2", [P, 2, T])
        place[0] = 0
        b2a = at("b2a", [E, D])
        XS = [at("XS", [D]) for i in range(2)]
        XST = [at("XST", [P]) for i in range(2)]
        W1C = [at("W1C", [F]) for i in range(2)]
        HT = [at("HT", [F]) for i in range(2)]
        YS = [at("YS", [D]) for i in range(2)]
        cntf = at("cntf", [E])
        cnti = at("cnti", [E], i32)
        ntile = at("ntile", [E])
        tend = at("tend", [E])
        tge = at("tge", [TILES, E])
        tnt = at("tnt", [TILES, E])
        tej = at("tej", [TILES])
        tst = at("tst", [TILES])
        tused = at("tused", [TILES])
        trow = at("trow", [TILES])
        tableb = at("table", [2, TILES], i32)
        padi = at("padi", [E], i32)
        ypos = sb("ypos", [P, NT, 2])
        yadd = sb("yadd", [P, NT, 2])
        ystep = sb("ystep", [P, E])
        place[0] = max(place[0], E * D + 9 * S)
        X3 = at("X3", [NT, D])
        N3 = at("N3", [NT, D])
        Y = [[at("Y", [T, D]) for j in range(2)] for i in range(2)]
        SC = at("SC", [S])
        SCN = at("SCN", [S])
        TZ = at("TZ", [S])
        G = at("G", [S])
        onesf = at("onesf", [S])
        X2 = at("X2", [T, D])
        X2T = at("X2T", [S])
        N3b = at("N3b", [T, D])
        N3T = at("N3T", [S])
        score = at("score", [NT, E])
        GB = sb("GB", [P, T, 2])
        n_c = place[0]
        place[0] = n_c
        keyhi = at("keyhi", [E, NT])
        keylo = at("keylo", [E, NT])
        kwork = at("kwork", [E, NT], i32)
        kwork2 = at("kwork2", [E, NT], i32)
        cmp = at("cmp", [WAYS, NT])
        base = at("base", [2])
        need = at("need", [1])
        nsel = at("nsel", [1])
        eq = at("eq", [NT])
        lo2 = at("lo2", [NT])
        sel = at("sel", [NT])
        free = at("free", [NT])
        hi = at("hi", [NT])
        taken = at("taken", [NT, E])
        takenb = at("takenb", [NT, E], bf16)
        cnt = at("cnt", [16], bf16)
        hib = at("hib", [NT, E])
        rank = at("rank", [NT, E])
        pos3 = at("pos3", [NT])
        pos3i = at("pos3i", [NT], i32)
        place[0] = E * D
        XE = at("XE", [T, D])
        XET = at("XET", [S])
        HE = at("HE", [FC, S])
        YE = at("YE", [T, D])
        YG = [at("YG", [T, D]) for i in range(2)]

        bank = [ctx.enter_context(nc.psum_tensor(f"bank{i}", [P, S], f32)) for i in range(8)]
        bA, bB, bC = bank[5], bank[6], bank[7]

        q_dram = nc.dram_tensor("q_dram", (PARTS, P, S), bf16, kind="Internal").ap()
        k_dram = nc.dram_tensor("k_dram", (PARTS, P, S), bf16, kind="Internal").ap()
        m_dram = nc.dram_tensor("m_dram", (2, PARTS * HH, S), bf16, kind="Internal").ap()
        x1_dram = nc.dram_tensor("x1_dram", (B, P, T, D), f32, kind="Internal").ap()
        xs_dram = nc.dram_tensor("xs_dram", (E * STRIDE, D), f32, kind="Internal").ap()
        ys_dram = nc.dram_tensor("ys_dram", (TILES * P, D), f32, kind="Internal").ap()
        xe_dram = nc.dram_tensor("xe_dram", (B * S, D), f32, kind="Internal").ap()
        ye_dram = nc.dram_tensor("ye_dram", (B * S, D), f32, kind="Internal").ap()

        names = ("x1save x1load const setup uready weff weffc init init_act qk r1 q1 q2 q3 v vready sa mx nm nmt nmtc mspill st ex pv ocopy "
                 "ntr nrm attt atc wo x1 x1t x1tc lg gd ge ohr rk posr xT xtok xres var rstd "
                 "xs_t xs_c h w1c hg y ys xload ystore table pads posc pcopy gath mixed x2t x2tc ab g yl n3 n3t n3tc sc scc "
                 "asn tot rk3 rk3m pos3 wload stageB stageC xeload xet xetc he heg ye yes yestore yg fin store posw cleared w2free scat scatE gpos").split()
        s = {n: sem(n) for n in names}
        rearr = [[sem(f"rearr{hf}_{buf}") for buf in range(2)] for hf in range(2)]
        mrow = [sem("mrow0"), sem("mrow1")]
        scat = [sem(f"scat{buf}") for buf in range(2)]
        x1save = [sem(f"x1save{buf}") for buf in range(2)]
        xload, ystore, x1load, gath, yg = ([sem(f"{n}{buf}") for buf in range(2)] for n in ("xload", "ystore", "x1load", "gath", "yg"))
        spill = [sem(f"spill{i}") for i in range(PARTS)]
        dch, pch = sem("dve_chain"), sem("pool_chain")

        loads = [(identf, "identf"), (identb, "identb"), (mask_a, "mask_a"), (mask_t, "mask_t"), (before, "before"),
                 (inv_count, "inv_count"), (iota8, "iota8"), (ebase, "ebase"), (pad_row, "pad_row"), (kstep, "kstep"),
                 (tie, "tie"), (jrow, "jrow"),
                 (wq0, "wq0"), (wk0, "wk0"), (wv0, "wv0"), (wo0, "wo0"), (bo0, "bo0"), (expdb, "denom_bias"), (wg, "wg"),
                 (wq1, "wq1"), (wk1, "wk1"), (wo1, "wo1"), (alpha, "alpha"), (cent, "cent"), (lng, "lng"), (lnb, "lnb")]
        small = [(vcat[:, 0:R], "V_b"), (vcat[:, R:2 * R], "V_t"), (vcat[:, 2 * R:3 * R], "V_t"),
                 (wcat[:, 0:R], "W_b"), (wcat[:, R:2 * R], "W_t"), (ucat[:, 0:R], "U_b"), (ucat[:, R:2 * R], "U_t"),
                 (bias_t[:, 0:1], "bias_t"), (wb[:, 2 * R:3 * R], "X_t"), (ucat[:, 2 * R:2 * R + 1], "bias_b")]
        n_const = 16 * (len(loads) + len(small))
        ROWS = ("bo0", "denom_bias", "lng", "lnb")

        block = ctx.enter_context(nc.Block())

        @block.sync
        def _(sp):
            def load_xT(b, buf):
                sp.dma_start(xT[buf], I["xT"][b, :, :]).then_inc(s["xT"], 16)

            load_xT(0, 0)
            for t, n in loads:
                sp.dma_start(t[:], I[n].partition_broadcast(P) if n in ROWS else I[n]).then_inc(s["const"], 16)
            for dst, n in small:
                sp.dma_start(dst, I[n]).then_inc(s["const"], 16)
            sp.wait_ge(s["xT"], 16)
            load_xT(1, 1)

            def spill_parts(n):
                for part in range(PARTS):
                    sp.wait_ge(s[("q1", "q2", "q3")[part]], 2 * n + 2)
                    sp.dma_start(q_dram[part], qparts[part]).then_inc(spill[part], 16)
                    sp.dma_start(k_dram[part], kparts[part]).then_inc(spill[part], 16)

            def spread(n, hf, buf):
                for part in range(PARTS):
                    if hf == 0:
                        sp.wait_ge(spill[part], 32 * n + 32)
                    for dst, src, order in ((QP[buf], q_dram, Q_PART), (KP[buf], k_dram, K_PART)):
                        for g in range(6):
                            if order[g] == part:
                                sp.dma_start(dst[g * HD:(g + 1) * HD, hf * HH:(hf + 1) * HH, :],
                                             src[part].rearrange("(f h d) n -> f d h n", f=2, d=HD)[hf]).then_inc(rearr[hf][buf], 16)

            def max_rows(n, hf, buf):
                sp.wait_ge(s["nmtc"], 2 * n + hf + 1)
                sp.dma_start(m_dram[hf], NMT[hf][:]).then_inc(s["mspill"], 16)
                sp.wait_ge(s["mspill"], 32 * n + 16 * hf + 16)
                sp.dma_start(QP[buf][MROW:MROW + PARTS, hf * HH:(hf + 1) * HH, :],
                             m_dram[hf].rearrange("(q h) n -> q h n", q=PARTS)).then_inc(mrow[hf], 16)

            def spill_wait_reads(n, buf):
                for hf in range(2):
                    sp.wait_ge(rearr[hf][buf], spread_count(n, buf))

            sp.wait_ge(s["init"], 5)
            spill_parts(0)
            spread(0, 0, 0)
            spread(0, 1, 0)
            spill_wait_reads(0, 0)
            spill_parts(1)
            spread(1, 0, 1)
            spread(1, 1, 1)
            max_rows(0, 0, 0)

            def step(b, buf, prev=True, nxt=True):
                if nxt:
                    sp.wait_ge(s["v"], b + 1)
                    load_xT((b + 2) % B, buf)
                max_rows(b, 1, buf)
                if prev:
                    if not (isinstance(b, int) and b == 1):
                        sp.wait_ge(s["x1"], b - 1)
                    sp.dma_start(xres[:], I["x"][b - 1, :, :].rearrange("(t p) d -> p t d", p=P)).then_inc(s["xtok"], 16)
                if nxt:
                    spill_wait_reads(b + 1, 1 - buf)
                    spill_parts(b + 2)
                    sp.wait_ge(s["st"], UB * b + UB // 2)
                    spread(b + 2, 0, buf)
                    max_rows(b + 1, 0, 1 - buf)
                    sp.wait_ge(s["st"], UB * b + UB)
                    spread(b + 2, 1, buf)

            def save_x1(n, buf):
                sp.wait_ge(s["x1"], n + 1)
                sp.dma_start(x1_dram[n, :, :, :], Xb[buf][:]).then_inc(x1save[buf], 16)

            step(0, 0, prev=False)
            with sp.Fori(0, 3) as i:
                step(2 * i + 1, 1)
                save_x1(2 * i, 0)
                step(2 * i + 2, 0)
                save_x1(2 * i + 1, 1)
            step(7, 1, nxt=False)
            save_x1(6, 0)
            spill_wait_reads(B, 0)
            sp.wait_ge(s["x1"], 7)
            sp.dma_start(xres[:], I["x"][7, :, :].rearrange("(t p) d -> p t d", p=P)).then_inc(s["xtok"], 16)

            save_x1(7, 1)

            sp.wait_ge(s["stageB"], 1)
            sp.dma_start(b2a, I["b2a"].partition_broadcast(P)).then_inc(s["wload"], 16)
            sp.wait_ge(s["table"], 1)
            for buf in range(2):
                sp.wait_ge(scat[buf], 16 * NT)
            sp.wait_ge(s["pads"], 16 * E)

            def load_slots(j, buf, first=False):
                if not first:
                    sp.wait_ge(s["xs_t"], j - 1)
                row = sp.value_load(tableb[0:1, 0, bass.ds(j, 1)], min_val=0, max_val=E * STRIDE - P)
                sp.dma_start(XS[buf], xs_dram[bass.ds(row, P), :]).then_inc(xload[buf], 16)

            def store_slots(j, buf):
                sp.wait_ge(s["ys"], j + 1)
                sp.dma_start(ys_dram[bass.ds(j * P, P), :], YS[buf]).then_inc(ystore[buf], 16)

            load_slots(0, 0, True)
            load_slots(1, 1, True)
            load_slots(2, 0)
            load_slots(3, 1)
            load_slots(4, 0)
            load_slots(5, 1)
            store_slots(0, 0)
            with sp.Fori(0, TILES // 2 - 3) as i:
                load_slots(2 * i + 6, 0)
                store_slots(2 * i + 1, 1)
                load_slots(2 * i + 7, 1)
                store_slots(2 * i + 2, 0)
            for j in range(TILES - 5, TILES):
                store_slots(j, j % 2)
            for buf in range(2):
                sp.wait_ge(ystore[buf], 8 * TILES)
            for t, n in ((w1[:], "w1b"), (w2[:], "w2b"), (b1c[:], "b1b")):
                sp.dma_start(t, I[n]).then_inc(s["wload"], 16)
            sp.dma_start(b2a, I["b2b"].partition_broadcast(P)).then_inc(s["wload"], 16)

            def load_x1(b, buf):
                if not isinstance(b, int) or b >= 2:
                    sp.wait_ge(s["mixed"], b - 1)
                sp.dma_start(Xb[buf][:], x1_dram[b, :, :, :]).then_inc(x1load[buf], 16)

            load_x1(0, 0)
            load_x1(1, 1)
            with sp.Fori(0, 3) as i:
                load_x1(2 * i + 2, 0)
                load_x1(2 * i + 3, 1)

            sp.wait_ge(s["scatE"], 16 * NT)

            def expert_load(e):
                if later(e):
                    sp.wait_ge(s["xet"], e)
                sp.dma_start(XE, xe_dram[bass.ds(e * CAP, CAP), :].rearrange("(t p) d -> p t d", p=P)).then_inc(s["xeload"], 16)

            def expert_store(e):
                sp.wait_ge(s["yes"], e + 1)
                sp.dma_start(ye_dram[bass.ds(e * CAP, CAP), :].rearrange("(t p) d -> p t d", p=P), YE).then_inc(s["yestore"], 16)

            expert_load(0)
            for e in range(E):
                if e + 1 < E:
                    expert_load(e + 1)
                expert_store(e)

            def store(b):
                sp.wait_ge(s["fin"], b + 1)
                sp.dma_start(out[b, :, :].rearrange("(t p) d -> p t d", p=P), X2).then_inc(s["store"], 16)

            store(0)
            with sp.Fori(1, B) as b:
                store(b)
            sp.wait_ge(s["store"], 16 * B)


        @block.tensor
        def _(pe):
            mm, tr = nc.tensor.matmul, nc.tensor.transpose
            pe.wait_ge(s["const"], n_const)
            pe.wait_ge(s["uready"], 1)
            mm(bank[0][:, 0:3 * R], wq1[:], vcat[:], start=True, stop=True)
            mm(bank[1][:, 0:2 * R], wk1[:], wcat[:], start=True, stop=True)
            mm(bank[2][0:2 * R + 1, 0:D], ucat[:], wo1[:], start=True, stop=True).then_inc(s["weff"], 1)

            def project_qk(n, buf):
                mm(bB[:], wq0[:], xT[buf], start=True, stop=True).then_inc(s["qk"], 1)
                mm(bC[:], wk0[:], xT[buf], start=True, stop=True).then_inc(s["qk"], 1)

            def project_v(n, buf, bk):
                for t in range(T):
                    last = mm(bk[:, t * P:(t + 1) * P], xT[buf][:, t * P:(t + 1) * P], wv0[:], start=True, stop=True)
                last.then_inc(s["v"], 1)

            def sa_unit(n, buf, q, k):
                u = q * UNITS + k
                if not (isinstance(n, int) and n == 0 and u < 2):
                    pe.wait_ge(s["mx"], 2 * UB * n + 2 * (u - 1))
                bk = bank[u % 2]

                def qk(cols, h, t):
                    w = (t + 1) * P
                    mm(bk[:, cols:cols + w], QP[buf][0:MROW, h, t * P:(t + 1) * P], KP[buf][0:MROW, h, 0:w], start=True, stop=False)
                    return mm(bk[:, cols + w - P:cols + w], identb[:], mask_a[:], start=False, stop=True)

                h = 4 * q + k % 4
                if k < 4:
                    last = qk(0, h, 3)
                elif k < 8:
                    qk(0, h, 2)
                    last = qk(3 * P, h, 0)
                else:
                    h = 4 * q + 2 * (k - 8)
                    qk(0, h, 1)
                    last = qk(2 * P, h + 1, 1)
                last.then_inc(s["sa"], 1)

            def st_unit(n, buf, q, k):
                u = q * UNITS + k
                if not (isinstance(n, int) and n == 0 and u < 2):
                    pe.wait_ge(s["ex"], UB * n + u - 1)
                bk = bank[2 + u % 2]

                def kq(cols, h, t):
                    w = S - t * P
                    mm(bk[:, cols:cols + w], KP[buf][:, h, t * P:(t + 1) * P], QP[buf][:, h, t * P:S], start=True, stop=False)
                    return mm(bk[:, cols:cols + P], identb[:], mask_t[:], start=False, stop=True)

                h = 4 * q + k % 4
                if k < 4:
                    last = kq(0, h, 0)
                elif k < 8:
                    kq(0, h, 1)
                    last = kq(3 * P, h, 3)
                else:
                    h = 4 * q + 2 * (k - 8)
                    kq(0, h, 2)
                    last = kq(2 * P, h + 1, 2)
                last.then_inc(s["st"], 1)

            def pv(n, buf, q):
                pe.wait_ge(s["ex"], UB * n + UNITS * (q + 1))
                if not (isinstance(n, int) and n == 0 and q == 0):
                    pe.wait_ge(s["ocopy"], QUADS * n + q)
                pr = PR[:, q % 2]
                for u in (0, 1, 3, 2):
                    w = S - u * P
                    for j in range(4):
                        src = {0: pr[:, j, 0:w], 1: pr[:, 4 + j, 0:w], 3: pr[:, 4 + j, 3 * P:4 * P],
                               2: pr[:, 8 + j // 2, (j % 2) * 2 * P:(j % 2 + 1) * 2 * P]}[u]
                        last = mm(bank[4][32 * j:32 * j + 32, u * P:S], Vaug[buf][:, u, 4 * q + j, :], src,
                                  start=(u == 0), stop=(u == 2))
                last.then_inc(s["pv"], 1)

            def tokens_first(n, q, bk):
                pe.wait_ge(s["ocopy"], QUADS * n + q + 1)
                for t in range(T):
                    last = tr(bk[:, t * P:(t + 1) * P], OT[q % 2][:, t * P:(t + 1) * P], identf[:])
                last.then_inc(s["ntr"], 1)

            def max_transpose(n, hf, bk):
                pe.wait_ge(s["nm"], 2 * n + hf + 1)
                for t in range(T):
                    last = tr(bk[:].bitcast(bf16)[:, t * P:(t + 1) * P], NM[hf][:, t, :, :], identb[:])
                last.then_inc(s["nmt"], 1)

            def att_transpose(n):
                pe.wait_ge(s["nrm"], QUADS * (n + 1))
                for t in range(T):
                    last = tr(bA[:, t * P:(t + 1) * P], att[:, t, :], identf[:])
                last.then_inc(s["attt"], 1)

            def out_project(n):
                pe.wait_ge(s["atc"], n + 1)
                for t in range(T):
                    last = mm(bA[:, t * P:(t + 1) * P], attT[:, t * P:(t + 1) * P], wo0[:], start=True, stop=True)
                last.then_inc(s["wo"], 1)

            def x1_transpose(n, buf):
                pe.wait_ge(s["x1"], n + 1)
                for t in range(T):
                    last = tr(bA[:, t * P:(t + 1) * P], Xb[buf][:, t, :], identf[:])
                last.then_inc(s["x1t"], 1)

            def gate_logits(n):
                pe.wait_ge(s["x1tc"], n + 1)
                for t in range(T):
                    last = mm(bB[:, t * E:(t + 1) * E], X1T[:, t * P:(t + 1) * P], wg[:], start=True, stop=True)
                last.then_inc(s["lg"], 1)

            def ranks(n):
                pe.wait_ge(s["ohr"], n + 1)
                mm(bA[:, 0:T * E], before[:], ohb[:], start=True, stop=True)
                mm(bA[:, T * E:2 * T * E], onesb[:], ohb[:], start=True, stop=True).then_inc(s["rk"], 1)

            pe.wait_ge(s["xT"], 16)
            project_qk(0, 0)
            project_v(0, 0, bA)
            pe.wait_ge(s["r1"], 2)
            pe.wait_ge(s["xT"], 32)
            project_qk(1, 1)
            pe.wait_ge(s["weffc"], 3)
            pe.wait_ge(s["init"], 5)
            for q in range(QUADS):
                if q % 2 == 0:
                    pe.wait_ge(rearr[q // 2][0], spread_count(0, 0))
                for k in range(UNITS):
                    sa_unit(0, 0, q, k)
                if q == 2:
                    pe.wait_ge(s["r1"], 4)
                    max_transpose(0, 0, bC)

            def step(b, buf, prev=True, nxt=True, nxt2=True):
                o = 1 - buf
                for q in range(QUADS):
                    if nxt and q % 2 == 0:
                        pe.wait_ge(rearr[q // 2][o], spread_count(b + 1, o))
                    if q % 2 == 0:
                        pe.wait_ge(mrow[q // 2], 16 * (b + 1))
                    for k in range(UNITS):
                        st_unit(b, buf, q, k)
                        if nxt:
                            sa_unit(b + 1, o, q, k)
                        if q == 0 and k == 3 and prev:
                            pv(b - 1, o, 3)
                        if q == 0 and k == 4:
                            if prev:
                                pe.wait_ge(s["nrm"], QUADS * b - 1)
                            pe.wait_ge(s["nmtc"], 2 * b + 1)
                            max_transpose(b, 1, bC)
                        if q == 0 and k == 8 and prev:
                            if not (isinstance(b, int) and b == 1):
                                pe.wait_ge(s["posr"], b - 1)
                            tokens_first(b - 1, 3, bA)
                        if q == 1 and k == 1 and nxt:
                            if prev and not (isinstance(b, int) and b == 1):
                                pe.wait_ge(s["gd"], b - 1)
                            pe.wait_ge(s["nmtc"], 2 * b + 2)
                            pe.wait_ge(s["xT"], 16 * (b + 3))
                            project_qk(b + 2, buf)
                        if q == 1 and k == 3:
                            pv(b, buf, 0)
                        if q == 1 and k == 5 and prev:
                            att_transpose(b - 1)
                        if q == 1 and k == 6 and nxt:
                            pe.wait_ge(s["r1"], 2 * b + 6)
                            pe.wait_ge(s["pv"], QUADS * b) if later(b) else None
                            project_v(b + 1, o, bB)
                        if q == 1 and k == 8:
                            tokens_first(b, 0, bC)
                        if q == 1 and k == 9 and prev:
                            out_project(b - 1)
                        if q == 2 and k == 3:
                            pv(b, buf, 1)
                        if q == 2 and k == 7 and nxt:
                            pe.wait_ge(s["vready"], b + 2)
                            max_transpose(b + 1, 0, bB)
                        if q == 2 and k == 8:
                            pe.wait_ge(s["nrm"], QUADS * b + 1)
                            tokens_first(b, 1, bC)
                        if q == 2 and k == 9 and prev:
                            x1_transpose(b - 1, o)
                        if q == 3 and k == 3:
                            pv(b, buf, 2)
                        if q == 3 and k == 4 and prev:
                            if nxt:
                                pe.wait_ge(s["nmtc"], 2 * b + 3)
                            gate_logits(b - 1)
                        if q == 3 and k == 8:
                            pe.wait_ge(s["nrm"], QUADS * b + 2)
                            tokens_first(b, 2, bC)
                        if q == 3 and k == 9 and prev:
                            ranks(b - 1)

            step(0, 0, prev=False)
            with pe.Fori(0, 3) as i:
                step(2 * i + 1, 1)
                step(2 * i + 2, 0)
            step(7, 1, nxt=False)
            pv(7, 1, 3)
            pe.wait_ge(s["posr"], 7)
            tokens_first(7, 3, bA)
            att_transpose(7)
            out_project(7)
            x1_transpose(7, 1)
            gate_logits(7)
            ranks(7)

            pe.wait_ge(s["table"], 1)
            pe.wait_ge(s["posr"], B)

            def slot_transpose(j, buf, first=False):
                pe.wait_ge(xload[buf], 8 * (j - buf) + 16)
                if not first:
                    pe.wait_ge(s["xs_c"], j - 1)
                tr(bank[6 + buf][:, 0:P], XS[buf], identf[:]).then_inc(s["xs_t"], 1)

            def up(j, buf, first=False):
                pe.wait_ge(s["xs_c"], j + 1)
                pe.wait_ge(s["w1c"], j + 1)
                if not first:
                    pe.wait_ge(s["hg"], j - 1)
                for f in range(FC):
                    last = mm(bank[buf][:, f * P:(f + 1) * P], W1C[buf][:, f * P:(f + 1) * P], XST[buf], start=True, stop=True)
                last.then_inc(s["h"], 1)

            def down(j, buf, first=False):
                e = pe.value_load(tableb[0:1, 1, bass.ds(j, 1)], min_val=0, max_val=E - 1)
                pe.wait_ge(s["hg"], j + 1)
                if not first:
                    pe.wait_ge(s["ys"], j - 1)
                for f in range(FC):
                    last = mm(bank[2 + buf][:, 0:D], HT[buf][:, f * P:(f + 1) * P], w2[:, bass.ds(e, 1), f, :].rearrange("p o d -> p (o d)"),
                              start=(f == 0), stop=(f == FC - 1))
                last.then_inc(s["y"], 1)

            pe.wait_ge(s["wload"], 16 + 48)
            slot_transpose(0, 0, True)
            slot_transpose(1, 1, True)
            up(0, 0, True)
            slot_transpose(2, 0)
            up(1, 1, True)
            down(0, 0, True)
            slot_transpose(3, 1)
            up(2, 0)
            down(1, 1, True)
            with pe.Fori(0, TILES // 2 - 2) as i:
                slot_transpose(2 * i + 4, 0)
                up(2 * i + 3, 1)
                down(2 * i + 2, 0)
                slot_transpose(2 * i + 5, 1)
                up(2 * i + 4, 0)
                down(2 * i + 3, 1)
            up(TILES - 1, 1)
            down(TILES - 2, 0)
            down(TILES - 1, 1)

            def mixer(b):
                pe.wait_ge(s["mixed"], b + 1)
                for t in range(T):
                    last = tr(bank[6][:, t * P:(t + 1) * P], X2[:, t, :], identf[:])
                last.then_inc(s["x2t"], 1)
                pe.wait_ge(s["x2tc"], b + 1)
                mm(bank[0][0:3 * R, :], wa[:], X2T, start=True, stop=True)
                mm(bank[1][0:3 * R, :], wb[:], X2T, start=True, stop=True).then_inc(s["ab"], 1)
                pe.wait_ge(s["g"], b + 1)
                for t in range(T):
                    last = mm(bank[2][:, t * P:(t + 1) * P], G[0:2 * R + 1, t * P:(t + 1) * P], uc[:], start=True, stop=True)
                last.then_inc(s["yl"], 1)
                pe.wait_ge(s["n3"], b + 1)
                for t in range(T):
                    last = tr(bank[7][:, t * P:(t + 1) * P], N3b[:, t, :], identf[:])
                last.then_inc(s["n3t"], 1)
                pe.wait_ge(s["n3tc"], b + 1)
                for t in range(T):
                    last = mm(bank[3][:, t * E:(t + 1) * E], N3T[:, t * P:(t + 1) * P], cent[:], start=True, stop=True)
                last.then_inc(s["sc"], 1)

            pe.wait_ge(s["ys"], TILES)
            mixer(0)
            with pe.Fori(1, B) as b:
                mixer(b)

            for n in range(COUNTS):
                pe.wait_ge(s["asn"], n + 1)
                mm(bank[0][:, 0:16], onesb[:], cnt, start=True, stop=True).then_inc(s["tot"], 1)
            pe.wait_ge(s["rk3"], 1)
            mm(bank[1][:, 0:NT * E], before[:], takenb, start=True, stop=True)
            mm(bank[2][:, 0:NT * E], onesb[:], takenb, start=True, stop=True).then_inc(s["rk3m"], 1)

            pe.wait_ge(s["pos3"], 1)
            pe.wait_ge(s["wload"], 16 * 8)
            for e in range(E):
                pe.wait_ge(s["xeload"], 16 * (e + 1))
                for t in range(T):
                    last = tr(bank[6][:, t * P:(t + 1) * P], XE[:, t, :], identf[:])
                last.then_inc(s["xet"], 1)
                pe.wait_ge(s["xetc"], e + 1)
                for f in range(FC):
                    n = e * FC + f
                    if n >= 4:
                        pe.wait_ge(s["heg"], n - 3)
                    mm(bank[n % 4][:], w1[:, e, f * P:(f + 1) * P], XET, start=True, stop=True).then_inc(s["he"], 1)
                pe.wait_ge(s["heg"], FC * (e + 1))
                if e >= 1:
                    pe.wait_ge(s["yes"], e)
                for t in range(T):
                    for f in range(FC):
                        last = mm(bank[4][:, t * P:(t + 1) * P], HE[:, f, t * P:(t + 1) * P], w2[:, e, f, :],
                                  start=(f == 0), stop=(f == FC - 1))
                last.then_inc(s["ye"], 1)

        @block.scalar
        def _(act):
            A = nc.scalar.activation
            act.dma_start(w1[:], I["w1a"]).then_inc(s["wload"], 16)
            act.dma_start(w2[:], I["w2a"]).then_inc(s["wload"], 16)
            act.dma_start(b1c[:], I["b1a"]).then_inc(s["wload"], 16)
            act.wait_ge(s["const"], n_const)
            A(expdb[:], expdb[:], ACT.Exp).then_inc(s["init_act"], 1)

            def q_first(n):
                for i, (dst, bk) in enumerate(((qparts[0], bB), (kparts[0], bC))):
                    act.wait_ge(s["qk"], 2 * n + i + 1)
                    if later(n):
                        act.wait_ge(spill[0], 32 * n)
                    A(dst, bk[:], Cp).then_inc(s["q1"], 1)

            def v_copy(n, buf, bk):
                act.wait_ge(s["v"], n + 1)
                A(Vaug[buf][:, :, :, 0:HD], bk[:].rearrange("p (t h d) -> p t h d", t=T, h=H), Cp).then_inc(s["vready"], 1)

            def nmt_copy(n, hf, bk):
                act.wait_ge(s["nmt"], 2 * n + hf + 1)
                if later(n):
                    act.wait_ge(s["mspill"], 32 * n - 16 + 16 * hf)
                A(NMT[hf][:], bk[:].bitcast(bf16)[0:PARTS * HH, 0:S], Cp).then_inc(s["nmtc"], 1)

            def o_copy(n, q):
                act.wait_ge(s["pv"], QUADS * n + q + 1)
                if not (isinstance(n, int) and n == 0 and q < 2):
                    act.wait_ge(s["ntr"], QUADS * n + q - 1)
                A(OT[q % 2][:], bank[4][:], Cp).then_inc(s["ocopy"], 1)

            act.wait_ge(s["init"], 5)
            q_first(0)
            v_copy(0, 0, bA)
            act.wait_ge(s["r1"], 2)
            q_first(1)
            nmt_copy(0, 0, bC)

            def step(b, buf, prev=True, nxt=True):
                o = 1 - buf
                for q in range(QUADS):
                    for k in range(UNITS):
                        u = q * UNITS + k
                        act.wait_ge(s["st"], UB * b + u + 1)
                        if k == 0 and not (isinstance(b, int) and b == 0 and q < 2):
                            act.wait_ge(s["pv"], QUADS * b + q - 1)
                        A(PR[:, q % 2, k, :], bank[2 + u % 2][:], ACT.Exp, scale=SCALE).then_inc(s["ex"], 1)
                        if q == 0 and k == 5:
                            if prev:
                                o_copy(b - 1, 3)
                            nmt_copy(b, 1, bC)
                        if q == 1 and k == 2 and nxt:
                            q_first(b + 2)
                        if k == 4 and q >= 1:
                            o_copy(b, q - 1)
                        if q == 1 and k == 7 and prev:
                            act.wait_ge(s["attt"], b)
                            A(attT[:], bA[:], Cp).then_inc(s["atc"], 1)
                        if q == 1 and k == 8 and nxt:
                            v_copy(b + 1, o, bB)
                        if q == 2 and k == 9 and nxt:
                            nmt_copy(b + 1, 0, bB)
                        if q == 3 and k == 0 and prev:
                            x1t_copy(b - 1)
                        if q == 3 and k == 7 and prev:
                            gate_exp(b - 1)

            def x1t_copy(n):
                act.wait_ge(s["x1t"], n + 1)
                A(X1T[:], bA[:], Cp).then_inc(s["x1tc"], 1)

            def gate_exp(n):
                act.wait_ge(s["gd"], n + 1)
                A(gate[:, :, 1], gate[:, :, 0], ACT.Exp).then_inc(s["ge"], 1)

            step(0, 0, prev=False)
            with act.Fori(0, 3) as i:
                step(2 * i + 1, 1)
                step(2 * i + 2, 0)
            step(7, 1, nxt=False)
            o_copy(7, 3)
            act.wait_ge(s["attt"], 8)
            A(attT[:], bA[:], Cp).then_inc(s["atc"], 1)
            x1t_copy(7)
            gate_exp(7)

            act.wait_ge(s["table"], 1)

            def slots(j, buf, first=False):
                act.wait_ge(s["xs_t"], j + 1)
                if not first:
                    act.wait_ge(s["h"], j - 1)
                A(XST[buf], bank[6 + buf][:, 0:P], Cp).then_inc(s["xs_c"], 1)

            def hidden(j, buf, first=False):
                e = act.value_load(tableb[0:1, 1, bass.ds(j, 1)], min_val=0, max_val=E - 1)
                act.wait_ge(s["h"], j + 1)
                if not first:
                    act.wait_ge(s["y"], j - 1)
                for f in range(FC):
                    last = A(HT[buf][:, f * P:(f + 1) * P], bank[buf][:, f * P:(f + 1) * P], ACT.Gelu_apprx_tanh,
                             bias=b1c[:, bass.ds(e, 1), f:f + 1].rearrange("p o f -> p (o f)"))
                last.then_inc(s["hg"], 1)

            act.wait_ge(s["wload"], 64)
            slots(0, 0, True)
            slots(1, 1, True)
            hidden(0, 0, True)
            slots(2, 0)
            hidden(1, 1, True)
            slots(3, 1)
            with act.Fori(0, TILES // 2 - 2) as i:
                hidden(2 * i + 2, 0)
                slots(2 * i + 4, 0)
                hidden(2 * i + 3, 1)
                slots(2 * i + 5, 1)
            hidden(TILES - 2, 0)
            hidden(TILES - 1, 1)

            def mixer(b):
                act.wait_ge(s["x2t"], b + 1)
                A(X2T, bank[6][:], Cp).then_inc(s["x2tc"], 1)
                act.wait_ge(s["n3t"], b + 1)
                A(N3T, bank[7][:], Cp).then_inc(s["n3tc"], 1)

            mixer(0)
            with act.Fori(1, B) as b:
                mixer(b)

            for e in range(E):
                act.wait_ge(s["xet"], e + 1)
                A(XET, bank[6][:], Cp).then_inc(s["xetc"], 1)
                if e >= 1:
                    act.wait_ge(s["ye"], e)
                for f in range(FC):
                    act.wait_ge(s["he"], e * FC + f + 1)
                    A(HE[:, f, :], bank[(e * FC + f) % 4][:], ACT.Gelu_apprx_tanh, bias=b1c[:, e, f:f + 1]).then_inc(s["heg"], 1)

        @block.gpsimd
        def _(pool):
            g = nc.gpsimd
            for i in range(2):
                g.memset(QP[i], 0.0)
                g.memset(Vaug[i][:], 0.0)
                g.memset(NM[i][:], 0.0)
                g.memset(KP[i], 0.0)
            g.memset(onesb[:], 1.0)
            g.memset(half[:], -0.5)
            g.memset(run[:], 0.0)
            g.memset(zeros[:], 0.0).then_inc(s["init"], 1)
            pool.wait_ge(s["init"], 1)
            for i in range(2):
                g.memset(KP[i][MROW:P, :, :], 1.0).then_inc(s["init"], 1)
                pool.wait_ge(s["init"], 2 * i + 2)
                g.memset(Vaug[i][:, :, :, HD:HD + 1], 1.0).then_inc(s["init"], 1)
                pool.wait_ge(s["init"], 2 * i + 3)

            def after_wait(k):
                g.tensor_tensor(pool_junk[:, k:k + 1], half[:, 0:1], half[:, 0:1], ALU.add)

            def parts(n):
                for i, (dst, src) in enumerate(((qparts[1], qrest), (kparts[1], krest))):
                    pool.wait_ge(s["r1"], 2 * n + i + 1)
                    if later(n):
                        pool.wait_ge(spill[1], 32 * n)
                        after_wait(i)
                    g.tensor_copy(dst, src).then_inc(s["q2"], 1)
                for i, (dst, src, sub) in enumerate(((qparts[2], qrest, qparts[1]), (kparts[2], krest, kparts[1]))):
                    pool.wait_ge(s["q2"], 2 * n + i + 1)
                    if later(n):
                        pool.wait_ge(spill[2], 32 * n)
                    g.tensor_tensor(dst, src, sub, ALU.subtract).then_inc(s["q3"], 1)

            def rsqrt(n):
                pool.wait_ge(s["var"], n)
                g.tensor_tensor(rstd[:], rstd[:], half[:], ALU.pow).then_inc(s["rstd"], 1)

            def residual(n):
                pool.wait_ge(s["xtok"], 16 * n + 16)
                g.tensor_tensor(xres[:], xres[:], bo0[:].rearrange("p (o d) -> p o d", o=1).to_broadcast([P, T, D]), ALU.add)\
                 .then_inc(s["xres"], 1)

            def scatter(n, buf):
                pool.wait_ge(s["posr"], n + 1)
                if not isinstance(n, int):
                    after_wait(2)
                for t in range(T):
                    for i in range(2):
                        g.indirect_dma_start(xs_dram, bass.IndirectOffsetOnAxis(ap=posb[buf][:, t, i:i + 1], axis=0),
                                             Xb[buf][:, t, :], None).then_inc(scat[buf], 16)

            parts(0)
            parts(1)

            def step(b, buf, prev=True, nxt=True):
                if prev:
                    residual(b - 1)
                if nxt:
                    parts(b + 2)
                if prev:
                    rsqrt(b)
                    scatter(b - 1, 1 - buf)

            step(0, 0, prev=False)
            with pool.Fori(0, 3) as i:
                step(2 * i + 1, 1)
                step(2 * i + 2, 0)
            step(7, 1, nxt=False)
            residual(7)
            rsqrt(8)
            scatter(7, 1)
            pool.wait_ge(s["table"], 1)
            for e in range(E):
                g.indirect_dma_start(xs_dram, bass.IndirectOffsetOnAxis(ap=padi[:, e:e + 1], axis=0),
                                     zeros[:], None).then_inc(s["pads"], 16)

            pool.wait_ge(s["ys"], TILES)
            g.memset(G, 1.0)
            g.memset(onesf, 1.0).then_inc(s["cleared"], 1)
            for buf in range(2):
                pool.wait_ge(ystore[buf], 8 * TILES)

            def gather(b, buf):
                pool.wait_ge(s["gpos"], b + 1)
                if not isinstance(b, int):
                    after_wait(3)
                for t in range(T):
                    for i in range(2):
                        g.indirect_dma_start(Y[buf][i][:, t, :], None, ys_dram,
                                             bass.IndirectOffsetOnAxis(ap=posb[buf][:, t, i:i + 1], axis=0)).then_inc(gath[buf], 16)

            def mixer(b):
                for k in range(3):
                    rsqrt(8 + 3 * b + k + 1)

            gather(0, 0)
            with pool.Fori(0, 3) as i:
                gather(2 * i + 1, 1)
                mixer(2 * i)
                gather(2 * i + 2, 0)
                mixer(2 * i + 1)
            gather(7, 1)
            mixer(6)
            mixer(7)

            pool.wait_ge(s["pos3"], 1)
            for t in range(NT):
                g.indirect_dma_start(xe_dram, bass.IndirectOffsetOnAxis(ap=pos3i[:, t:t + 1], axis=0),
                                     N3[:, t, :], None).then_inc(s["scatE"], 16)
            pool.wait_ge(s["yestore"], 16 * E)
            for b in range(B):
                if b >= 2:
                    pool.wait_ge(s["fin"], b - 1)
                for t in range(T):
                    g.indirect_dma_start(YG[b % 2][:, t, :], None, ye_dram,
                                         bass.IndirectOffsetOnAxis(ap=pos3i[:, b * T + t:b * T + t + 1], axis=0)).then_inc(yg[b % 2], 16)
                if b >= 1:
                    rsqrt(8 + 24 + b)
            rsqrt(8 + 24 + 8)

        @block.vector
        def _(dve):
            v = nc.vector
            state = {"n": 0, "off": 0}

            def link(ins):
                ins.then_inc(dch, 1)
                state["n"] += 1
                dve.wait_ge(dch, state["off"] + state["n"])

            def layer_norm(dst, src, count, signal=None):
                for t in range(T):
                    last = v.bn_stats(stats[:, t, :], src[:, t, :])
                link(last)
                v.tensor_copy(junk[:, 0:1], half[:, 0:1])
                for t in range(T):
                    last = v.bn_aggr(mv[:, t, :], stats[:, t, :])
                link(last)
                v.tensor_scalar(rstd[:], mv[:, :, 1], EPS, None, ALU.add).then_inc(s["var"], 1)
                dve.wait_ge(s["rstd"], count)
                for t in range(T):
                    last = v.tensor_scalar(dst[:, t, :], src[:, t, :], mv[:, t, 0:1], rstd[:, t:t + 1], ALU.subtract, ALU.mult)
                return last

            dve.wait_ge(s["const"], n_const)
            v.tensor_scalar(ucat[:, R:2 * R], ucat[:, R:2 * R], alpha[:], None, ALU.mult)
            v.scalar_tensor_tensor(ucat[:, 2 * R:2 * R + 1], bias_t[:], alpha[:], ucat[:, 2 * R:2 * R + 1], ALU.mult,
                                   ALU.add).then_inc(s["uready"], 1)
            dve.wait_ge(s["weff"], 1)
            v.tensor_copy(wa[:], bank[0][:, 0:3 * R])
            v.tensor_copy(wb[:, 0:2 * R], bank[1][:, 0:2 * R])
            v.tensor_copy(uc[:], bank[2][0:2 * R + 1, 0:D]).then_inc(s["weffc"], 3)

            def q_rest(n):
                for i, (rest, p0, bk) in enumerate(((qrest, qparts[0], bB), (krest, kparts[0], bC))):
                    dve.wait_ge(s["q1"], 2 * n + i + 1)
                    if later(n):
                        dve.wait_ge(s["q3"], 2 * n)
                    v.tensor_tensor(rest, bk[:], p0, ALU.subtract).then_inc(s["r1"], 1)

            def maxima(n, q, k):
                u = q * UNITS + k
                dve.wait_ge(s["sa"], UB * n + u + 1)
                bk = bank[u % 2]
                h = 4 * q + k % 4
                if k < 4:
                    last = v.tensor_reduce(M[:, 3, h:h + 1], bk[:], AX.X, ALU.max)
                elif k < 8:
                    v.tensor_reduce(M[:, 2, h:h + 1], bk[:, 0:3 * P], AX.X, ALU.max)
                    last = v.tensor_reduce(M[:, 0, h:h + 1], bk[:, 3 * P:4 * P], AX.X, ALU.max)
                else:
                    h = 4 * q + 2 * (k - 8)
                    last = v.tensor_reduce(M[:, 1, h:h + 2], bk[:].rearrange("p (h n) -> p h n", h=2), AX.X, ALU.max)
                last.then_inc(s["mx"], 2)

            def negate_maxima(n, hf):
                m = M[:, :, hf * HH:(hf + 1) * HH]
                nm = NM[hf]
                dve.wait_ge(s["mx"], 2 * UB * n + UB * (hf + 1))
                link(v.tensor_scalar(nm[:, :, 0, :], m, -1.0, None, ALU.mult))
                link(v.scalar_tensor_tensor(mrest[:], m, -1.0, nm[:, :, 0, :], ALU.mult, ALU.subtract))
                link(v.tensor_copy(nm[:, :, 1, :], mrest[:]))
                v.tensor_tensor(nm[:, :, 2, :], mrest[:], nm[:, :, 1, :], ALU.subtract).then_inc(s["nm"], 1)

            def normalize(n, q, bk):
                dve.wait_ge(s["ntr"], QUADS * n + q + 1)
                o = bk[:].rearrange("p (t h c) -> p t h c", t=T, h=4)
                dq = expdb[:, 4 * q:4 * q + 4].rearrange("p (o h) -> p o h", o=1).to_broadcast([P, T, 4])
                link(v.tensor_tensor(den[:], o[:, :, :, HD], dq, ALU.add))
                link(v.reciprocal(den[:], den[:]))
                v.tensor_tensor(att[:, :, q * 32:(q + 1) * 32].rearrange("p t (h d) -> p t h d", h=4), o[:, :, :, 0:HD],
                                den[:].rearrange("p t (h o) -> p t h o", o=1).to_broadcast([P, T, 4, HD]), ALU.mult)\
                 .then_inc(s["nrm"], 1)

            def attention_norm(n, buf):
                dve.wait_ge(s["wo"], n + 1)
                dve.wait_ge(s["xres"], n + 1)
                link(v.tensor_tensor(res[:], bA[:].rearrange("p (t d) -> p t d", t=T), xres[:], ALU.add))
                if not isinstance(n, int) or n >= 2:
                    dve.wait_ge(scat[buf], 16 * T * (n - buf))
                    dve.wait_ge(x1save[buf], 8 * (n - buf))
                layer_norm(Xb[buf], res, n + 1).then_inc(s["x1"], 1)

            def choose(n, buf):
                dve.wait_ge(s["lg"], n + 1)
                link(v.tensor_copy(logit[:], bB[:, 0:T * E].rearrange("p (t e) -> p t e", t=T)))
                v.tensor_copy(junk[:, 0:1], half[:, 0:1])
                for t in range(T):
                    last = v.max(top[:, t, :], logit[:, t, :])
                link(last)
                v.tensor_tensor(gate[:, :, 0], top[:, :, 1], top[:, :, 0], ALU.subtract).then_inc(s["gd"], 1)
                for t in range(T):
                    last = v.max_index(topi[:, t, :], top[:, t, :], logit[:, t, :])
                link(last)
                link(v.tensor_copy(topf[:], topi[:]))
                io = iota8[:].rearrange("p (o e) -> p o e", o=1).to_broadcast([P, T, E])
                for i in range(2):
                    last = v.tensor_tensor(oh[:, i], io, topf[:, :, i:i + 1].to_broadcast([P, T, E]), ALU.is_equal)
                link(last)
                v.tensor_tensor(ohb[:], oh[:, 0], oh[:, 1], ALU.add).then_inc(s["ohr"], 1)
                dve.wait_ge(s["ge"], n + 1)
                link(v.tensor_scalar(gate[:, :, 0], gate[:, :, 1], 1.0, None, ALU.add))
                link(v.reciprocal(gate[:, :, 0], gate[:, :, 0]))
                link(v.tensor_tensor(gate[:, :, 1], gate[:, :, 1], gate[:, :, 0], ALU.mult))
                link(v.tensor_copy(GATE[:, bass.ds(n * T, T), :], gate[:]))

            def positions(n, buf):
                dve.wait_ge(s["rk"], n + 1)
                link(v.tensor_copy(tpre[:, 0, :], run[:]))
                for t in range(T):
                    link(v.tensor_tensor(tpre[:, t + 1, :], tpre[:, t, :], bA[:, (T + t) * E:(T + t + 1) * E], ALU.add))
                link(v.tensor_copy(run[:], tpre[:, T, :]))
                link(v.tensor_tensor(posf[:], bA[:, 0:T * E].rearrange("p (t e) -> p t e", t=T), tpre[:, 0:T, :], ALU.add))
                link(v.tensor_tensor(posf[:], posf[:], ebase[:].rearrange("p (o e) -> p o e", o=1).to_broadcast([P, T, E]), ALU.add))
                for i in range(2):
                    last = v.tensor_tensor(oh[:, i], oh[:, i], posf[:], ALU.mult)
                link(last)
                link(v.tensor_reduce(pos2[:], oh[:], AX.X, ALU.add))
                link(v.tensor_copy(POS[:, bass.ds(n * T, T), :], pos2[:].rearrange("p i t -> p t i")))
                v.tensor_copy(posb[buf][:], pos2[:].rearrange("p i t -> p t i")).then_inc(s["posr"], 1)

            dve.wait_ge(s["init"], 5)
            dve.wait_ge(s["init_act"], 1)
            q_rest(0)
            q_rest(1)
            for q in range(QUADS):
                for k in range(UNITS):
                    maxima(0, q, k)
                if q % 2:
                    negate_maxima(0, q // 2)

            def step(b, buf, prev=True, nxt=True):
                o = 1 - buf
                for q in range(QUADS):
                    for k in range(UNITS):
                        if nxt:
                            maxima(b + 1, q, k)
                        if q == 0 and k == 9 and prev:
                            normalize(b - 1, 3, bA)
                        if q == 1 and k == 3 and nxt:
                            q_rest(b + 2)
                        if k == 9 and q >= 1:
                            normalize(b, q - 1, bC)
                        if q == 2 and k == 1 and prev:
                            attention_norm(b - 1, o)
                        if q == 3 and k == 5 and prev:
                            choose(b - 1, o)
                    if nxt and q % 2:
                        negate_maxima(b + 1, q // 2)
                if prev:
                    positions(b - 1, o)

            PER = [0]

            def counted(b, buf, **k):
                state["n"] = 0
                step(b, buf, **k)
                return state["n"]

            base_links = state["n"]
            n_first = counted_offset = 0
            step(0, 0, prev=False)
            first = state["n"]
            LPS = 37
            with dve.Fori(0, 3) as i:
                state["off"], state["n"] = first + 2 * LPS * i, 0
                step(2 * i + 1, 1)
                assert state["n"] == LPS, state["n"]
                step(2 * i + 2, 0)
            state["off"], state["n"] = first + 6 * LPS, 0
            step(7, 1, nxt=False)
            normalize(7, 3, bA)
            attention_norm(7, 1)
            choose(7, 1)
            positions(7, 1)

            v.tensor_copy(junk[:, 2:3], half[:, 0:1]).then_inc(s["stageB"], 1)
            link(v.tensor_scalar(cntf, run[:], float(P - 1), None, ALU.add))
            link(v.tensor_copy(cnti, cntf))
            link(v.tensor_scalar(cnti, cnti, 7, None, ALU.logical_shift_right))
            link(v.tensor_copy(ntile, cnti))
            link(v.memset(tend, 1.0))
            link(v.tensor_tensor_scan(tend, tend, ntile, 0.0, ALU.mult, ALU.add))
            jb = jrow[:, 0, :].rearrange("p (j o) -> p j o", o=1).to_broadcast([P, TILES, E])
            link(v.tensor_tensor(tge, jb, tend.rearrange("p (o e) -> p o e", o=1).to_broadcast([P, TILES, E]), ALU.is_ge))
            link(v.tensor_tensor(tnt, tge, ntile.rearrange("p (o e) -> p o e", o=1).to_broadcast([P, TILES, E]), ALU.mult))
            link(v.tensor_reduce(tej, tge, AX.X, ALU.add))
            link(v.tensor_reduce(tst, tnt, AX.X, ALU.add))
            link(v.tensor_scalar(tused, tej, float(E) - 0.5, None, ALU.is_lt))
            link(v.scalar_tensor_tensor(trow, tst, -float(P), jrow[:, 1, :], ALU.mult, ALU.add))
            link(v.scalar_tensor_tensor(trow, tej, float(STRIDE), trow, ALU.mult, ALU.add))
            link(v.tensor_tensor(trow, trow, tused, ALU.mult))
            link(v.tensor_copy(tableb[:, 0, :], trow))
            link(v.tensor_tensor(tej, tej, tused, ALU.mult))
            link(v.tensor_copy(tableb[:, 1, :], tej))
            link(v.tensor_tensor(cntf, run[:], pad_row[:], ALU.add))
            v.tensor_copy(padi, cntf).then_inc(s["table"], 1)

            link(v.tensor_scalar(ystep[:], ntile, float(P), float(-STRIDE), ALU.mult, ALU.add))
            link(v.tensor_copy(ypos[:], POS[:]))
            for e in range(E - 1):
                link(v.tensor_scalar(yadd[:], POS[:], float((e + 1) * STRIDE), ystep[:, e:e + 1], ALU.is_ge, ALU.mult))
                link(v.tensor_tensor(ypos[:], ypos[:], yadd[:], ALU.add))
            dve.wait_ge(s["wload"], 64)
            dve.wait_ge(s["table"], 1)

            def expert_of(j):
                return dve.value_load(tableb[0:1, 1, bass.ds(j, 1)], min_val=0, max_val=E - 1)

            def weights(j, buf, first=False):
                if not first:
                    dve.wait_ge(s["h"], j - 1)
                v.tensor_copy(W1C[buf], w1[:, bass.ds(expert_of(j), 1), :].rearrange("p o f -> p (o f)")).then_inc(s["w1c"], 1)

            def bias_down(j, buf, first=False):
                dve.wait_ge(s["y"], j + 1)
                if not first:
                    dve.wait_ge(ystore[buf], 8 * (j - buf))
                v.tensor_tensor(YS[buf], bank[2 + buf][:, 0:D], b2a[:, bass.ds(expert_of(j), 1), :].rearrange("p o f -> p (o f)"),
                                ALU.add).then_inc(s["ys"], 1)

            weights(0, 0, True)
            weights(1, 1, True)
            weights(2, 0)
            weights(3, 1)
            bias_down(0, 0, True)
            bias_down(1, 1, True)
            with dve.Fori(0, TILES // 2 - 2) as i:
                weights(2 * i + 4, 0)
                bias_down(2 * i + 2, 0)
                weights(2 * i + 5, 1)
                bias_down(2 * i + 3, 1)
            bias_down(TILES - 2, 0)
            bias_down(TILES - 1, 1)

            def send_positions(b, buf):
                v.tensor_copy(posb[buf][:], ypos[:, bass.ds(b * T, T), :]).then_inc(s["gpos"], 1)

            def mixer(b, buf):
                dve.wait_ge(gath[buf], 16 * T * (b - buf) + 32 * T)
                link(v.tensor_copy(GB[:], GATE[:, bass.ds(b * T, T), :]))
                dve.wait_ge(x1load[buf], 8 * (b - buf) + 16)
                for i in range(2):
                    for t in range(T):
                        last = v.scalar_tensor_tensor(res[:, t, :], Y[buf][i][:, t, :], GB[:, t, i:i + 1],
                                                      (Xb[buf][:], res[:])[i][:, t, :], ALU.mult, ALU.add)
                    link(last)
                if not isinstance(b, int) or b < B - 2:
                    send_positions(b + 2, buf)
                layer_norm(X2, res, 8 + 3 * b + 1).then_inc(s["mixed"], 1)
                dve.wait_ge(s["ab"], b + 1)
                link(v.tensor_tensor_scan(SC[0:3 * R, :], onesf[0:3 * R, :], bank[1][0:3 * R, :], 0.0, ALU.mult, ALU.add))
                link(v.tensor_tensor(SCN[0:3 * R, :], SC[0:3 * R, :], inv_count[0:3 * R, :], ALU.mult))
                v.tensor_tensor(G[0:R, :], bank[0][0:R, :], SCN[0:R, :], ALU.mult)
                link(v.tensor_tensor(TZ[R:2 * R, :], bank[0][2 * R:3 * R, :], SCN[2 * R:3 * R, :], ALU.mult))
                v.tensor_tensor(G[R:2 * R, :], TZ[R:2 * R, :], SCN[R:2 * R, :], ALU.mult).then_inc(s["g"], 1)
                dve.wait_ge(s["yl"], b + 1)
                link(v.tensor_tensor(res[:], bank[2][:].rearrange("p (t d) -> p t d", t=T), X2, ALU.add))
                link(layer_norm(N3b, res, 8 + 3 * b + 2))
                link(v.tensor_copy(X3[:, bass.ds(b * T, T), :], N3b))
                link(layer_norm(res, N3b, 8 + 3 * b + 3))
                link(v.tensor_tensor(res[:], res[:], lng[:].rearrange("p (o d) -> p o d", o=1).to_broadcast([P, T, D]), ALU.mult))
                v.tensor_tensor(N3b, res[:], lnb[:].rearrange("p (o d) -> p o d", o=1).to_broadcast([P, T, D]), ALU.add).then_inc(s["n3"], 1)
                dve.wait_ge(s["n3"], b + 1)
                link(v.tensor_copy(N3[:, bass.ds(b * T, T), :], N3b))
                dve.wait_ge(s["sc"], b + 1)
                v.tensor_copy(score[:, bass.ds(b * T, T), :], bank[3][:, 0:T * E].rearrange("p (t e) -> p t e", t=T)).then_inc(s["scc"], 1)

            dve.wait_ge(s["cleared"], 1)
            send_positions(0, 0)
            send_positions(1, 1)
            LPM = 18
            off0 = state["off"] + state["n"]
            with dve.Fori(0, 3) as i:
                state["off"], state["n"] = off0 + 2 * LPM * i, 0
                mixer(2 * i, 0)
                assert state["n"] == LPM, state["n"]
                mixer(2 * i + 1, 1)
            state["off"], state["n"] = off0 + 6 * LPM, 0
            mixer(6, 0)
            mixer(7, 1)

            dve.wait_ge(s["scc"], B)
            link(v.tensor_copy(kwork.bitcast(f32), score.rearrange("p t e -> p e t")))
            link(v.tensor_scalar(kwork2, kwork, 31, None, ALU.arith_shift_right))
            link(v.tensor_scalar(kwork2, kwork2, -2147483648, None, ALU.bitwise_or))
            link(v.tensor_tensor(kwork, kwork, kwork2, ALU.bitwise_xor))
            link(v.tensor_scalar(kwork2, kwork, 10, None, ALU.logical_shift_right))
            link(v.tensor_copy(keyhi, kwork2))
            link(v.tensor_scalar(kwork2, kwork, 1023, 12, ALU.bitwise_and, ALU.logical_shift_left))
            link(v.tensor_copy(keylo, kwork2))
            link(v.tensor_tensor(keylo, keylo, tie[:].rearrange("p (o t) -> p o t", o=1).to_broadcast([P, E, NT]), ALU.add))
            v.memset(cnt, 0.0)
            link(v.memset(free, 1.0))
            rounds = [0]

            def total(ins):
                ins.then_inc(s["asn"], 1)
                rounds[0] += 1
                dve.wait_ge(s["tot"], rounds[0])

            def search(keys, want, col):
                link(v.memset(base[:, col:col + 1], 0.0))
                for d in range(len(DIGITS)):
                    ways = 15 if DIGITS[d] > 0 else 3
                    k3 = keys.rearrange("p (o t) -> p o t", o=1).to_broadcast([P, ways, NT])
                    st = kstep[:, d, 0:ways].rearrange("p (w o) -> p w o", o=1).to_broadcast([P, ways, NT])
                    link(v.scalar_tensor_tensor(cmp[:, 0:ways, :], k3, base[:, col:col + 1], st, ALU.subtract, ALU.is_ge))
                    with nc.allow_low_precision(reason="counts up to 32 are exact"):
                        ins = v.tensor_reduce(cnt[:, 0:ways], cmp[:, 0:ways, :], AX.X, ALU.add)
                    total(ins)
                    link(v.tensor_scalar(junk[:, 0:ways], bank[0][:, 0:ways], want, None, ALU.is_ge, ALU.add, accum_out=nsel))
                    link(v.scalar_tensor_tensor(base[:, col:col + 1], nsel, float(2 ** DIGITS[d]), base[:, col:col + 1], ALU.mult, ALU.add))

            for e in range(E - 1):
                link(v.scalar_tensor_tensor(hi, keyhi[:, e, :], 1.0, free, ALU.add, ALU.mult))
                link(v.tensor_scalar(hi, hi, 1.0, None, ALU.subtract))
                search(hi, float(CAP), 0)
                link(v.tensor_scalar(sel, hi, base[:, 0:1], None, ALU.is_gt))
                with nc.allow_low_precision(reason="counts up to 32 are exact"):
                    ins = v.tensor_reduce(cnt[:, 0:1], sel, AX.X, ALU.add)
                total(ins)
                link(v.tensor_scalar(need, bank[0][:, 0:1], -1.0, float(CAP), ALU.mult, ALU.add))
                link(v.tensor_scalar(eq, hi, base[:, 0:1], None, ALU.is_equal))
                link(v.scalar_tensor_tensor(lo2, keylo[:, e, :], 1.0, eq, ALU.add, ALU.mult))
                link(v.tensor_scalar(lo2, lo2, 1.0, None, ALU.subtract))
                search(lo2, need, 1)
                link(v.scalar_tensor_tensor(sel, lo2, base[:, 1:2], sel, ALU.is_ge, ALU.add))
                link(v.tensor_copy(taken[:, :, e], sel))
                link(v.tensor_tensor(free, free, sel, ALU.subtract))
            assert rounds[0] == COUNTS
            link(v.tensor_copy(taken[:, :, E - 1], free))
            v.tensor_copy(takenb, taken).then_inc(s["rk3"], 1)
            dve.wait_ge(s["rk3m"], 1)
            link(v.tensor_copy(rank, bank[1][:, 0:NT * E].rearrange("p (t e) -> p t e", t=NT)))
            link(v.tensor_scalar(hib[:, 0, :], iota8[:], float(CAP), None, ALU.mult))
            for t in range(NT - 1):
                link(v.tensor_tensor(hib[:, t + 1, :], hib[:, t, :], bank[2][:, t * E:(t + 1) * E], ALU.add) if t else
                     v.tensor_tensor(hib[:, 1, :], bank[2][:, 0:E], hib[:, 0, :], ALU.add))
            link(v.tensor_tensor(rank, rank, hib, ALU.add))
            link(v.tensor_tensor(rank, rank, taken, ALU.mult))
            link(v.tensor_reduce(pos3, rank, AX.X, ALU.add))
            v.tensor_copy(pos3i, pos3).then_inc(s["pos3"], 1)

            dve.wait_ge(s["wload"], 16 * 8)
            for e in range(E):
                dve.wait_ge(s["ye"], e + 1)
                if e >= 1:
                    dve.wait_ge(s["yestore"], 16 * e)
                v.tensor_tensor(YE, bank[4][:].rearrange("p (t d) -> p t d", t=T), b2a[:, e:e + 1, :].to_broadcast([P, T, D]), ALU.add)\
                 .then_inc(s["yes"], 1)
            for b in range(B):
                dve.wait_ge(yg[b % 2], 16 * T * (b // 2 + 1))
                if b >= 1:
                    dve.wait_ge(s["fin"], b)
                link(v.scalar_tensor_tensor(res[:], X3[:, b * T:(b + 1) * T, :], 2.0, YG[b % 2], ALU.mult, ALU.add))
                if b >= 1:
                    dve.wait_ge(s["store"], 16 * b)
                layer_norm(X2, res, 32 + b + 1).then_inc(s["fin"], 1)


def kernel(**inputs):
    import numpy as np
    import ml_dtypes
    import concourse.bacc as bacc
    from concourse import mybir as mb
    from concourse.bass_utils import run_bass_kernel_spmd as run

    nc = bacc.Bacc("TRN2", target_bir_lowering=False, num_devices=1)
    a = {k: np.asarray(x) for k, x in inputs.items()}
    p = np.arange(128)
    big = -3.0e38
    bf = ml_dtypes.bfloat16
    stride, tiles = 4096 + 128, 72
    e8, j = np.arange(8), np.arange(tiles)
    f = np.float32
    arr = {
        "identf": np.eye(128, dtype=f), "identb": np.eye(128).astype(bf),
        "mask_a": np.where(p[None, :] > p[:, None], big, 0.0).astype(bf),
        "mask_t": np.where(p[:, None] > p[None, :], big, 0.0).astype(bf),
        "before": (p[:, None] < p[None, :]).astype(bf),
        "inv_count": np.broadcast_to((1.0 / (1.0 + np.arange(512))).astype(f), (96, 512)),
        "iota8": np.broadcast_to(e8.astype(f), (128, 8)), "ebase": np.broadcast_to((e8 * stride).astype(f), (128, 8)),
        "pad_row": (e8[None, :] * stride + p[:, None]).astype(f),
        "kstep": np.broadcast_to(np.array([[float((k + 1) << d) for k in range(15)] for d in (18, 14, 10, 6, 2, 0)], f), (128, 6, 15)),
        "tie": (4095 - (np.arange(32)[None, :] * 128 + p[:, None])).astype(f),
        "jrow": np.broadcast_to(np.stack([j, 128 * j]).astype(f), (128, 2, tiles)),
        "x": a["L0_attn_x"], "xT": a["L0_attn_x"].transpose(0, 2, 1),
        "wq0": a["L0_attn_Wq"].T, "wk0": a["L0_attn_Wk"].T, "wv0": a["L0_attn_Wv"].T, "wo0": a["L0_attn_Wo"].T,
        "bo0": a["L0_attn_bo"], "denom_bias": a["L0_attn_denom_bias"].reshape(16), "wg": a["L0_ffn_Wg"],
        "wq1": a["L1_attn_Wq"], "wk1": a["L1_attn_Wk"], "wo1": a["L1_attn_Wo"].T,
        "V_b": a["L1_attn_V_b"], "V_t": a["L1_attn_V_t"], "W_b": a["L1_attn_W_b"], "W_t": a["L1_attn_W_t"],
        "U_b": a["L1_attn_U_b"], "U_t": a["L1_attn_U_t"], "X_t": a["L1_attn_X_t"],
        "bias_b": a["L1_attn_bias_b"].reshape(128, 1), "bias_t": a["L1_attn_bias_t"].reshape(128, 1),
        "alpha": np.broadcast_to(a["L1_attn_alpha"].reshape(1, 1), (128, 1)),
        "cent": a["L1_ffn_centroids"].T, "lng": a["L1_ffn_ln_g"], "lnb": a["L1_ffn_ln_b"],
        "b1a": a["L0_ffn_b1"].reshape(8, 4, 128).transpose(2, 0, 1), "b1b": a["L1_ffn_b1"].reshape(8, 4, 128).transpose(2, 0, 1),
        "ptile": np.zeros((1,), f),
    }
    del arr["ptile"]
    for tag, w1, w2, b2 in (("a", "L0_ffn_W1", "L0_ffn_W2", "L0_ffn_b2"), ("b", "L1_ffn_w1", "L1_ffn_w2", "L1_ffn_b2")):
        arr["w1" + tag] = a[w1].transpose(1, 0, 2)
        arr["w2" + tag] = a[w2].reshape(8, 4, 128, 128).transpose(2, 0, 1, 3)
        arr["b2" + tag] = a[b2]
    arrays, I = {}, {}
    for n, x in arr.items():
        x = np.ascontiguousarray(x)
        arrays["in_" + n] = x
        I[n] = nc.dram_tensor("in_" + n, x.shape, mb.dt.from_np(x.dtype), kind="ExternalInput").ap()
    out = nc.dram_tensor("out_x", (8, 512, 128), mb.dt.float32, kind="ExternalOutput").ap()
    sequence_stack_kernel(nc, I, out)
    r = run(nc, [arrays], core_ids=[0])
    return r.results[0]["out_x"]
```

```python
import concourse.bass as bass
from concourse import mybir
from contextlib import ExitStack


def sequence_stack_kernel(nc, I, out):
    f32 = mybir.dt.float32
    bf16 = mybir.dt.bfloat16
    i32 = mybir.dt.int32
    u32 = mybir.dt.uint32
    ALU = mybir.AluOpType
    ACT = mybir.ActivationFunctionType
    AX = mybir.AxisListType
    Cp = ACT.Copy

    B, S, D = 8, 512, 128
    P = 128
    T = S // P
    H, HD = 16, 8
    E, F = 8, 512
    FC = F // P
    R = 32
    NT = B * T
    CAP = B * S // E
    PARTS = 3
    MROW = 96
    SCALE = float(HD) ** -0.5
    EPS = 1e-5
    QUADS = H // 4
    UNITS = 10
    UB = QUADS * UNITS
    Q_PART = [0, 0, 1, 1, 0, 2]
    K_PART = [0, 1, 0, 1, 2, 0]
    HH = H // 2
    MCOLS = P // HH
    STRIDE = B * S + P
    TILES = 2 * B * S // P + E
    WAYS = 16
    DIGITS = [20, 16, 12, 8, 4, 0]
    ROUNDS = 2 * len(DIGITS) - 1

    ctx = ExitStack()
    with ctx:
        def sb(name, shape, dt=f32):
            return ctx.enter_context(nc.sbuf_tensor(name, shape, dt))

        def sem(name):
            return ctx.enter_context(nc.semaphore("s_" + name))

        def later(b):
            return not (isinstance(b, int) and b == 0)

        def spread_count(n, buf):
            return 12 * 16 // 2 * (n - buf) + 12 * 16

        identf = sb("identf", [P, P])
        identb = sb("identb", [P, P], bf16)
        mask_a = sb("mask_a", [P, P], bf16)
        before = sb("before", [P, P], bf16)
        onesb = sb("onesb", [P, P], bf16)
        iota8 = sb("iota8", [P, E])
        ebase = sb("ebase", [P, E])
        kstep = sb("kstep", [P, 2, len(DIGITS)])
        kdelta = sb("kdelta", [P, len(DIGITS)])
        way = sb("way", [P, WAYS], bf16)
        lane = sb("lane", [P, 1])
        jrow = sb("jrow", [P, 2, TILES])
        half = sb("half", [P, T])
        wq0 = sb("wq0", [P, D])
        wk0 = sb("wk0", [P, D])
        wv0 = sb("wv0", [P, D])
        wo0 = sb("wo0", [P, D])
        bo0 = sb("bo0", [P, D])
        expdb = sb("expdb", [P, H])
        wg = sb("wg", [P, E])
        wq1 = sb("wq1", [P, D])
        wk1 = sb("wk1", [P, D])
        wo1 = sb("wo1", [P, D])
        vcat = sb("vcat", [P, 3 * R])
        wcat = sb("wcat", [P, 2 * R])
        ucat = sb("ucat", [P, 2 * R + 1])
        bias_t = sb("bias_t", [P, 1])
        alpha = sb("alpha", [P, 1])
        wa = sb("wa", [P, 3 * R])
        wb = sb("wb", [P, 3 * R])
        uc = sb("uc", [2 * R + 1, D])
        cent = sb("cent", [P, E])
        lng = sb("lng", [P, D])
        lnb = sb("lnb", [P, D])
        w1 = sb("w1", [P, E, F + FC + D])
        w2 = sb("w2", [P, E, FC, D])
        POS = sb("POS", [P, NT, 2])
        GATE = sb("GATE", [P, NT, 2])
        res = sb("res", [P, T, D])
        stats = sb("stats", [P, T, 6])
        mv = sb("mv", [P, T, 2])
        rstd = sb("rstd", [P, T])
        junk = sb("junk", [P, 16])
        pool_junk = sb("pool_junk", [P, 16])
        Xb = [sb(f"Xb{i}", [P, T, D]) for i in range(2)]
        posb = [sb(f"posb{i}", [P, T, 2], i32) for i in range(2)]
        run = sb("run", [P, E])
        zeros = sb("zeros", [P, D])

        arena = sb("arena", [P, 30350])
        place = [0]

        def at(n, shape, dt=f32):
            size = 1
            for x in shape:
                size *= x
            words = size * (2 if dt == bf16 else 4) // 4
            a = arena[:, place[0]:place[0] + words]
            place[0] += words
            assert place[0] <= 30350, (n, place[0])
            if dt != f32:
                a = a.bitcast(dt)
            names = " ".join("abcd"[:len(shape)])
            if len(shape) == 1:
                return a
            return a.rearrange(f"p ({names}) -> p {names}", **{"abcd"[i]: shape[i] for i in range(len(shape))})

        QP = [at("QP", [H, S], bf16) for i in range(2)]
        KP = [at("KP", [H, S], bf16) for i in range(2)]
        PR = at("PR", [2, UNITS, S])
        xT = [at("xT", [S]) for i in range(2)]
        qparts = [at("q", [S], bf16) for i in range(PARTS)]
        kparts = [at("k", [S], bf16) for i in range(PARTS)]
        qrest = at("qrest", [S])
        krest = at("krest", [S])
        NM = [sb(f"NM{i}", [P, T, MCOLS, HH], bf16) for i in range(2)]
        NMT = [sb(f"NMT{i}", [PARTS * HH, S], bf16) for i in range(2)]
        mrest = sb("mrest", [P, T, HH])
        M = sb("M", [P, T, H])
        Vaug = [sb(f"Vaug{i}", [P, T, H, 32]) for i in range(2)]
        OT = [sb(f"OT{i}", [P, S]) for i in range(2)]
        den = sb("den", [P, T, 4])
        att = sb("att", [P, T, D])
        attT = sb("attT", [P, S])
        xres = sb("xres", [P, T, D])
        X1T = sb("X1T", [P, S])
        logit = sb("logit", [P, T, E])
        top = sb("top", [P, T, 8])
        topi = sb("topi", [P, T, 8], u32)
        topf = sb("topf", [P, T, 8])
        gate = sb("gate", [P, T, 2])
        oh = sb("oh", [P, 2, T, E])
        ohb = sb("ohb", [P, T, E], bf16)
        tpre = sb("tpre", [P, E, T + 1])
        fresh = sb("fresh", [P, E, T + 1])
        posf = sb("posf", [P, T, E])
        pos2 = sb("pos2", [P, 2, T])
        place[0] = 0
        XS = [at("XS", [D]) for i in range(2)]
        XST = [at("XST", [P]) for i in range(2)]
        own = [at("own", [F + FC + D]) for i in range(4)]
        HT = [at("HT", [F]) for i in range(2)]
        YS = [at("YS", [D]) for i in range(2)]
        cntf = at("cntf", [E])
        cnti = at("cnti", [E], i32)
        ntile = at("ntile", [E])
        tend = at("tend", [E])
        tge = at("tge", [TILES, E])
        tnt = at("tnt", [TILES, E])
        tej = at("tej", [TILES])
        tst = at("tst", [TILES])
        tused = at("tused", [TILES])
        trow = at("trow", [TILES])
        tableb = at("table", [2, TILES], i32)
        padi = at("padi", [E], i32)
        ypos = sb("ypos", [P, NT, 2])
        yadd = sb("yadd", [P, NT, 2])
        ystep = sb("ystep", [P, E])
        place[0] = max(place[0], 4650)
        y_at = place[0]
        Y = [[at("Y", [T, D]) for j in range(2)] for i in range(2)]
        resc = [at("resc", [T, D]) for i in range(2)]
        SC, SCN, TZ, G, X2T, N3T, score = ([at(n, [S]) for i in range(2)] for n in ("SC", "SCN", "TZ", "G", "X2T", "N3T", "score"))
        X2 = [at("X2", [T, D]) for i in range(2)]
        XN = [at("XN", [T, 2 * D]) for i in range(2)]
        X3b, N3b = [x[:, :, 0:D] for x in XN], [x[:, :, D:2 * D] for x in XN]
        onesf = at("onesf", [S])
        GB = sb("GB", [P, T, 2])
        statsc = [sb(f"statsc{i}", [P, T, 6]) for i in range(2)]
        mvc = [sb(f"mvc{i}", [P, T, 2]) for i in range(2)]
        rstdc = [sb(f"rstdc{i}", [P, T]) for i in range(2)]
        n_c = place[0]
        place[0] = n_c
        pick = at("pick", [E, P])
        tie = at("tie", [S])
        restart = at("restart", [E, NT])
        inv_count = at("inv_count", [S])
        iota = at("iota", [P])
        tile = at("tile", [NT, NT])
        in_row = at("in_row", [NT, P], bf16)
        in_tile = at("in_tile", [NT, 2, NT], bf16)
        place[0] = y_at
        kraw = at("kraw", [S], i32)
        ksign = at("ksign", [S], i32)
        keyhi = at("keyhi", [S])
        keylo = at("keylo", [S])
        free = at("free", [S])
        turned = at("turned", [S])
        scratch = at("scratch", [S], bf16)
        ahead = at("ahead", [1])
        thr = at("thr", [1])
        acc = at("acc", [2], bf16)
        nsel = at("nsel", [1])
        th = at("th", [2])
        need = at("need", [1])
        above = at("above", [1])
        reached = at("reached", [WAYS])
        below = at("below", [WAYS])
        expert3 = at("expert3", [NT])
        takenb = at("takenb", [NT, E], bf16)
        carry = at("carry", [E, NT])
        rank = at("rank", [E, NT])
        pos3 = at("pos3", [NT])
        pos3i = at("pos3i", [NT], i32)
        placei = at("placei", [2, NT], i32)
        place_row = at("place_row", [NT])
        place_tile = at("place_tile", [NT])
        tokens_hl = at("tokens_hl", [2, NT])
        tokens = at("tokens", [NT])
        tokensi = at("tokensi", [NT], i32)
        hi = at("hi", [S])
        lo = at("lo", [S])
        kept = at("kept", [S])
        kepthi = at("kepthi", [S])
        assert place[0] <= y_at + 7000
        place[0] = 0
        XR = [at("XR", [T, 2 * D]) for i in range(4)]
        XET = at("XET", [S])
        assert place[0] <= 4650
        place[0] = y_at + 7000
        HE = at("HE", [FC, S])
        OE = [at("OE", [T, D]) for i in range(2)]

        bank = [ctx.enter_context(nc.psum_tensor(f"bank{i}", [P, S], f32)) for i in range(8)]
        bA, bB, bC = bank[5], bank[6], bank[7]

        q_dram = nc.dram_tensor("q_dram", (PARTS, P, S), bf16, kind="Internal").ap()
        k_dram = nc.dram_tensor("k_dram", (PARTS, P, S), bf16, kind="Internal").ap()
        m_dram = nc.dram_tensor("m_dram", (2, PARTS * HH, S), bf16, kind="Internal").ap()
        x1_dram = nc.dram_tensor("x1_dram", (B, P, T, D), f32, kind="Internal").ap()
        xs_dram = nc.dram_tensor("xs_dram", (E * STRIDE, D), f32, kind="Internal").ap()
        ys_dram = nc.dram_tensor("ys_dram", (TILES * P, D), f32, kind="Internal").ap()
        sc_dram = nc.dram_tensor("sc_dram", (B, E, S), f32, kind="Internal").ap()
        xn_dram = nc.dram_tensor("xn_dram", (B * S, 2 * D), f32, kind="Internal").ap()

        first_loaded = sem("first_loaded")
        const_loaded = sem("const_loaded")
        rows_cleared = sem("rows_cleared")
        ones_set = sem("ones_set")
        small_cleared = sem("small_cleared")
        expdb_ready = sem("expdb_ready")
        ucat_ready = sem("ucat_ready")
        mixer_products = sem("mixer_products")
        mixer_weights = sem("mixer_weights")
        xT_loaded = sem("xT_loaded")
        qk_projected = sem("qk_projected")
        part1_ready = sem("part1_ready")
        rest_ready = sem("rest_ready")
        part2_ready = sem("part2_ready")
        part3_ready = sem("part3_ready")
        v_projected = sem("v_projected")
        v_ready = sem("v_ready")
        max_scores = sem("max_scores")
        maxima_taken = sem("maxima_taken")
        negmax_parts = sem("negmax_parts")
        negmax_turned = sem("negmax_turned")
        negmax_ready = sem("negmax_ready")
        negmax_stored = sem("negmax_stored")
        exp_scores = sem("exp_scores")
        exps_ready = sem("exps_ready")
        later_dropped = sem("later_dropped")
        sums_ready = sem("sums_ready")
        sums_copied = sem("sums_copied")
        sums_turned = sem("sums_turned")
        quad_normalized = sem("quad_normalized")
        attention_turned = sem("attention_turned")
        attention_copied = sem("attention_copied")
        attention_out = sem("attention_out")
        tokens_loaded = sem("tokens_loaded")
        residual_ready = sem("residual_ready")
        var_ready = sem("var_ready")
        rstd_ready = sem("rstd_ready")
        x1_ready = sem("x1_ready")
        x1_turned = sem("x1_turned")
        x1_turned_copied = sem("x1_turned_copied")
        logits_ready = sem("logits_ready")
        logit_gap = sem("logit_gap")
        gap_exp = sem("gap_exp")
        choices_ready = sem("choices_ready")
        ranks_counted = sem("ranks_counted")
        slots_ready = sem("slots_ready")
        table_ready = sem("table_ready")
        pads_stored = sem("pads_stored")
        attention_done = sem("attention_done")
        experts_loaded = sem("experts_loaded")
        slots_turned = sem("slots_turned")
        slots_copied = sem("slots_copied")
        own_ready = sem("own_ready")
        hidden_ready = sem("hidden_ready")
        gelu_ready = sem("gelu_ready")
        tile_out = sem("tile_out")
        tile_out_ready = sem("tile_out_ready")
        mixer_cleared = sem("mixer_cleared")
        late_consts = sem("late_consts")
        rows_wanted = sem("rows_wanted")
        x2_ready = sem("x2_ready")
        x2_turned = sem("x2_turned")
        x2_copied = sem("x2_copied")
        mixer_inputs = sem("mixer_inputs")
        mixer_gated = sem("mixer_gated")
        mixer_out = sem("mixer_out")
        x3_ready = sem("x3_ready")
        row_choices_ready = sem("row_choices_ready")
        tokens_found = sem("tokens_found")
        n3_normed = sem("n3_normed")
        n3_scaled = sem("n3_scaled")
        n3_ready = sem("n3_ready")
        n3_turned = sem("n3_turned")
        n3_copied = sem("n3_copied")
        scores_ready = sem("scores_ready")
        scores_copied = sem("scores_copied")
        scores_loaded = sem("scores_loaded")
        keys_ready = sem("keys_ready")
        keys_spread = sem("keys_spread")
        hi_read = sem("hi_read")
        lo_read = sem("lo_read")
        counts_ready = sem("counts_ready")
        totals_ready = sem("totals_ready")
        experts_found = sem("experts_found")
        experts_turned = sem("experts_turned")
        assigned_ready = sem("assigned_ready")
        assigned_counted = sem("assigned_counted")
        places_ready = sem("places_ready")
        rows_turned = sem("rows_turned")
        rows_copied = sem("rows_copied")
        expert_hidden = sem("expert_hidden")
        expert_gelu = sem("expert_gelu")
        expert_out = sem("expert_out")
        expert_out_read = sem("expert_out_read")
        rows_done = sem("rows_done")
        parts_spread = [[sem(f"parts_spread{hf}_{buf}") for buf in range(2)] for hf in range(2)]
        negmax_spread = [sem(f"negmax_spread{hf}") for hf in range(2)]
        parts_stored = [sem(f"parts_stored{i}") for i in range(PARTS)]
        rows_scattered = [sem(f"rows_scattered{buf}") for buf in range(2)]
        x1_saved = [sem(f"x1_saved{buf}") for buf in range(2)]
        x1_loaded = [sem(f"x1_loaded{buf}") for buf in range(2)]
        slots_loaded = [sem(f"slots_loaded{buf}") for buf in range(2)]
        slots_stored = [sem(f"slots_stored{buf}") for buf in range(2)]
        rows_gathered = [sem(f"rows_gathered{buf}") for buf in range(2)]
        scores_stored = [sem(f"scores_stored{buf}") for buf in range(2)]
        out_stored = [sem(f"out_stored{buf}") for buf in range(2)]
        rows_stored = [sem(f"rows_stored{buf}") for buf in range(2)]
        expert_rows_loaded = [sem(f"expert_rows_loaded{buf}") for buf in range(4)]
        dve_step = sem("dve_step")

        first_loads = [(wq0, "wq0"), (wk0, "wk0"), (wv0, "wv0"), (identb, "identb"), (mask_a, "mask_a")]
        loads = [(expdb, "denom_bias"), (identf, "identf"), (before, "before"),
                 (iota8, "iota8"), (ebase, "ebase"), (run, "ebase"), (fresh, "fresh"), (kstep, "kstep"), (kdelta, "kdelta"),
                 (way, "way"), (lane, "lane"), (jrow, "jrow"),
                 (wo0, "wo0"), (bo0, "bo0"), (wg, "wg"),
                 (wq1, "wq1"), (wk1, "wk1"), (wo1, "wo1"), (alpha, "alpha"), (cent, "cent"), (lng, "lng"), (lnb, "lnb")]
        small = [(vcat[:, 0:R], "V_b"), (vcat[:, R:2 * R], "V_t"), (vcat[:, 2 * R:3 * R], "V_t"),
                 (wcat[:, 0:R], "W_b"), (wcat[:, R:2 * R], "W_t"), (ucat[:, 0:R], "U_b"), (ucat[:, R:2 * R], "U_t"),
                 (bias_t[:, 0:1], "bias_t"), (wb[:, 2 * R:3 * R], "X_t"), (ucat[:, 2 * R:2 * R + 1], "bias_b")]
        n_first = 16 * len(first_loads)
        n_const = 16 * (len(loads) + len(small))
        ROWS = ("bo0", "denom_bias", "lng", "lnb")

        block = ctx.enter_context(nc.Block())

        def load_experts(eng, layer):
            eng.dma_start(w1[:, :, 0:F], I["w1" + layer]).then_inc(experts_loaded, 16)
            eng.dma_start(w1[:, :, F:F + FC], I["b1" + layer]).then_inc(experts_loaded, 16)
            eng.dma_start(w1[:, :, F + FC:F + FC + D], I["b2" + layer].partition_broadcast(P)).then_inc(experts_loaded, 16)
            eng.dma_start(w2[:], I["w2" + layer]).then_inc(experts_loaded, 16)

        @block.sync
        def _(sp):
            def load_xT(b, buf):
                sp.dma_start(xT[buf], I["xT"][b, :, :]).then_inc(xT_loaded, 16)

            load_xT(0, 0)
            for t, n in first_loads:
                sp.dma_start(t[:], I[n]).then_inc(first_loaded, 16)
            sp.wait_ge(xT_loaded, 16)
            load_xT(1, 1)

            def load_constants():
                for t, n in loads:
                    sp.dma_start(t[:], I[n].partition_broadcast(P) if n in ROWS else I[n]).then_inc(const_loaded, 16)
                for dst, n in small:
                    sp.dma_start(dst, I[n]).then_inc(const_loaded, 16)

            def spill_parts(n):
                for part in range(PARTS):
                    sp.wait_ge((part1_ready, part2_ready, part3_ready)[part], 2 * n + 2)
                    sp.dma_start(q_dram[part], qparts[part]).then_inc(parts_stored[part], 16)
                    sp.dma_start(k_dram[part], kparts[part]).then_inc(parts_stored[part], 16)

            def spread(n, hf, buf):
                for part in range(PARTS):
                    if hf == 0:
                        sp.wait_ge(parts_stored[part], 32 * n + 32)
                    for dst, src, order in ((QP[buf], q_dram, Q_PART), (KP[buf], k_dram, K_PART)):
                        for g in range(6):
                            if order[g] == part:
                                sp.dma_start(dst[g * HD:(g + 1) * HD, hf * HH:(hf + 1) * HH, :],
                                             src[part].rearrange("(f h d) n -> f d h n", f=2, d=HD)[hf]).then_inc(parts_spread[hf][buf], 16)

            def max_rows(n, hf, buf):
                sp.wait_ge(negmax_ready, 2 * n + hf + 1)
                sp.dma_start(m_dram[hf], NMT[hf][:]).then_inc(negmax_stored, 16)
                sp.wait_ge(negmax_stored, 32 * n + 16 * hf + 16)
                sp.dma_start(QP[buf][MROW:MROW + PARTS, hf * HH:(hf + 1) * HH, :],
                             m_dram[hf].rearrange("(q h) n -> q h n", q=PARTS)).then_inc(negmax_spread[hf], 16)

            def spill_wait_reads(n, buf):
                for hf in range(2):
                    sp.wait_ge(parts_spread[hf][buf], spread_count(n, buf))

            sp.wait_ge(rows_cleared, 1)
            sp.wait_ge(ones_set, 1)
            spill_parts(0)
            spread(0, 0, 0)
            spread(0, 1, 0)
            load_constants()
            spill_wait_reads(0, 0)
            spill_parts(1)
            sp.wait_ge(rows_cleared, 2)
            sp.wait_ge(ones_set, 3)
            spread(1, 0, 1)
            spread(1, 1, 1)
            max_rows(0, 0, 0)

            def step(b, buf, prev=True, nxt=True):
                if nxt:
                    sp.wait_ge(v_projected, b + 1)
                    load_xT((b + 2) % B, buf)
                max_rows(b, 1, buf)
                if nxt:
                    spill_wait_reads(b + 1, 1 - buf)
                    spill_parts(b + 2)
                    sp.wait_ge(exp_scores, UB * b + UB // 2)
                    spread(b + 2, 0, buf)
                    max_rows(b + 1, 0, 1 - buf)
                    sp.wait_ge(exp_scores, UB * b + UB)
                    spread(b + 2, 1, buf)

            def load_tokens(n):
                sp.dma_start(xres[:], I["x"][n, :, :].rearrange("(t p) d -> p t d", p=P)).then_inc(tokens_loaded, 16)

            def save_x1(n, buf):
                sp.wait_ge(x1_ready, n + 1)
                load_tokens(n + 1)
                sp.dma_start(x1_dram[n, :, :, :], Xb[buf][:]).then_inc(x1_saved[buf], 16)

            load_tokens(0)
            step(0, 0, prev=False)
            with sp.Fori(0, 3) as i:
                step(2 * i + 1, 1)
                save_x1(2 * i, 0)
                step(2 * i + 2, 0)
                save_x1(2 * i + 1, 1)
            step(7, 1, nxt=False)
            save_x1(6, 0)
            spill_wait_reads(B, 0)
            sp.wait_ge(x1_ready, B)
            sp.dma_start(x1_dram[7, :, :, :], Xb[1][:]).then_inc(x1_saved[1], 16)

            sp.wait_ge(attention_done, 1)
            for dst, n in ((inv_count[0:3 * R], "inv_count"), (pick[0:B * E], "pick"), (tie[0:B * E], "tie"), (restart, "restart"), (iota, "iota"), (tile, "tile")):
                sp.dma_start(dst, I[n]).then_inc(late_consts, 16)
            sp.wait_ge(table_ready, 1)
            sp.wait_ge(small_cleared, 1)
            for e in range(E):
                row = sp.value_load(padi[0:1, e:e + 1], min_val=0, max_val=E * STRIDE - P)
                sp.dma_start(xs_dram[bass.ds(row, P), :], zeros[:]).then_inc(pads_stored, 16)
            for buf in range(2):
                sp.wait_ge(rows_scattered[buf], 16 * NT)
            sp.wait_ge(pads_stored, 16 * E)

            def load_slots(j, buf, first=False):
                if not first:
                    sp.wait_ge(slots_turned, j - 1)
                row = sp.value_load(tableb[0:1, 0, bass.ds(j, 1)], min_val=0, max_val=E * STRIDE - P)
                sp.dma_start(XS[buf], xs_dram[bass.ds(row, P), :]).then_inc(slots_loaded[buf], 16)

            def store_slots(j, buf):
                sp.wait_ge(tile_out_ready, j + 1)
                sp.dma_start(ys_dram[bass.ds(j * P, P), :], YS[buf]).then_inc(slots_stored[buf], 16)

            load_slots(0, 0, True)
            load_slots(1, 1, True)
            load_slots(2, 0)
            load_slots(3, 1)
            load_slots(4, 0)
            load_slots(5, 1)
            store_slots(0, 0)
            with sp.Fori(0, TILES // 2 - 3) as i:
                load_slots(2 * i + 6, 0)
                store_slots(2 * i + 1, 1)
                load_slots(2 * i + 7, 1)
                store_slots(2 * i + 2, 0)
            for j in range(TILES - 5, TILES):
                store_slots(j, j % 2)
            for buf in range(2):
                sp.wait_ge(slots_stored[buf], 8 * TILES)
            def load_x1(b, buf):
                if not isinstance(b, int) or b >= 2:
                    sp.wait_ge(x2_ready, b - 1)
                sp.dma_start(Xb[buf][:], x1_dram[b, :, :, :]).then_inc(x1_loaded[buf], 16)

            def store_scores(b, buf):
                sp.wait_ge(n3_ready, b + 1)
                sp.dma_start(xn_dram[bass.ds(b * S, S), :].rearrange("(t p) d -> p t d", p=P), XN[buf]).then_inc(rows_stored[buf], 16)
                sp.wait_ge(scores_copied, b + 1)
                sp.dma_start(sc_dram[b, :, :], score[buf][0:E, :]).then_inc(scores_stored[buf], 16)

            load_x1(0, 0)
            load_x1(1, 1)
            with sp.Fori(0, 3) as i:
                load_x1(2 * i + 2, 0)
                store_scores(2 * i, 0)
                load_x1(2 * i + 3, 1)
                store_scores(2 * i + 1, 1)
            store_scores(6, 0)
            store_scores(7, 1)
            for buf in range(2):
                sp.wait_ge(scores_stored[buf], 8 * B)
            sp.dma_start(kraw[0:B * E].bitcast(f32), sc_dram.rearrange("b e n -> (b e) n")).then_inc(scores_loaded, 16)
            load_experts(sp, "b")

            for buf in range(2):
                sp.wait_ge(out_stored[buf], 16 * T * E // 2)

        @block.tensor
        def _(pe):
            mm, tr = nc.tensor.matmul, nc.tensor.transpose
            def project_qk(n, buf):
                mm(bB[:], wq0[:], xT[buf], start=True, stop=True).then_inc(qk_projected, 1)
                mm(bC[:], wk0[:], xT[buf], start=True, stop=True).then_inc(qk_projected, 1)

            def project_v(n, buf, bk):
                for t in range(T):
                    last = mm(bk[:, t * P:(t + 1) * P], xT[buf][:, t * P:(t + 1) * P], wv0[:], start=True, stop=True)
                last.then_inc(v_projected, 1)

            def sa_unit(n, buf, q, k):
                u = q * UNITS + k
                if not (isinstance(n, int) and n == 0 and u < 2):
                    pe.wait_ge(maxima_taken, 2 * UB * n + 2 * (u - 1))
                bk = bank[u % 2]

                def qk(cols, h, t):
                    w = (t + 1) * P
                    mm(bk[:, cols:cols + w], QP[buf][0:MROW, h, t * P:(t + 1) * P], KP[buf][0:MROW, h, 0:w], start=True, stop=False)
                    return mm(bk[:, cols + w - P:cols + w], identb[:], mask_a[:], start=False, stop=True)

                h = 4 * q + k % 4
                if k < 4:
                    last = qk(0, h, 3)
                elif k < 8:
                    qk(0, h, 2)
                    last = qk(3 * P, h, 0)
                else:
                    h = 4 * q + 2 * (k - 8)
                    qk(0, h, 1)
                    last = qk(2 * P, h + 1, 1)
                last.then_inc(max_scores, 1)

            def st_unit(n, buf, q, k):
                u = q * UNITS + k
                if not (isinstance(n, int) and n == 0 and u < 2):
                    pe.wait_ge(exps_ready, UB * n + u - 1)
                bk = bank[2 + u % 2]

                def kq(cols, h, t):
                    w = S - t * P
                    return mm(bk[:, cols:cols + w], KP[buf][:, h, t * P:(t + 1) * P], QP[buf][:, h, t * P:S], start=True, stop=True)

                h = 4 * q + k % 4
                if k < 4:
                    last = kq(0, h, 0)
                elif k < 8:
                    kq(0, h, 1)
                    last = kq(3 * P, h, 3)
                else:
                    h = 4 * q + 2 * (k - 8)
                    kq(0, h, 2)
                    last = kq(2 * P, h + 1, 2)
                last.then_inc(exp_scores, 1)

            def pv(n, buf, q, part):
                if part != 2:
                    pe.wait_ge(exps_ready, UB * n + UNITS * q + (4, 8, 8, UNITS)[part])
                    pe.wait_ge(later_dropped, 3 * (QUADS * n + q) + (1, 2, 2, 3)[part])
                if part == 0 and not (isinstance(n, int) and n == 0 and q == 0):
                    pe.wait_ge(sums_copied, QUADS * n + q)
                pr = PR[:, q % 2]
                u = (0, 1, 3, 2)[part]
                w = S - u * P
                for j in range(4):
                    src = {0: pr[:, j, 0:w], 1: pr[:, 4 + j, 0:w], 3: pr[:, 4 + j, 3 * P:4 * P],
                           2: pr[:, 8 + j // 2, (j % 2) * 2 * P:(j % 2 + 1) * 2 * P]}[u]
                    last = mm(bank[4][32 * j:32 * j + 32, u * P:S], Vaug[buf][:, u, 4 * q + j, :], src,
                              start=(u == 0), stop=(u == 2))
                if part == 3:
                    last.then_inc(sums_ready, 1)

            def tokens_first(n, q, bk):
                pe.wait_ge(sums_copied, QUADS * n + q + 1)
                for t in range(T):
                    last = tr(bk[:, t * P:(t + 1) * P], OT[q % 2][:, t * P:(t + 1) * P], identf[:])
                last.then_inc(sums_turned, 1)

            def max_transpose(n, hf, bk):
                pe.wait_ge(negmax_parts, 2 * n + hf + 1)
                for t in range(T):
                    last = tr(bk[:].bitcast(bf16)[:, t * P:(t + 1) * P], NM[hf][:, t, :, :], identb[:])
                last.then_inc(negmax_turned, 1)

            def att_transpose(n):
                pe.wait_ge(quad_normalized, QUADS * (n + 1))
                for t in range(T):
                    last = tr(bA[:, t * P:(t + 1) * P], att[:, t, :], identf[:])
                last.then_inc(attention_turned, 1)

            def out_project(n):
                pe.wait_ge(attention_copied, n + 1)
                for t in range(T):
                    last = mm(bA[:, t * P:(t + 1) * P], attT[:, t * P:(t + 1) * P], wo0[:], start=True, stop=True)
                last.then_inc(attention_out, 1)

            def x1_transpose(n, buf):
                pe.wait_ge(x1_ready, n + 1)
                for t in range(T):
                    last = tr(bA[:, t * P:(t + 1) * P], Xb[buf][:, t, :], identf[:])
                last.then_inc(x1_turned, 1)

            def gate_logits(n):
                pe.wait_ge(x1_turned_copied, n + 1)
                for t in range(T):
                    last = mm(bB[:, t * E:(t + 1) * E], X1T[:, t * P:(t + 1) * P], wg[:], start=True, stop=True)
                last.then_inc(logits_ready, 1)

            def ranks(n):
                pe.wait_ge(choices_ready, n + 1)
                mm(bA[:, 0:T * E], before[:], ohb[:], start=True, stop=True)
                mm(bA[:, T * E:2 * T * E], onesb[:], ohb[:], start=True, stop=True).then_inc(ranks_counted, 1)

            pe.wait_ge(first_loaded, n_first)
            pe.wait_ge(xT_loaded, 16)
            project_qk(0, 0)
            project_v(0, 0, bA)
            pe.wait_ge(rest_ready, 2)
            pe.wait_ge(xT_loaded, 32)
            project_qk(1, 1)
            pe.wait_ge(small_cleared, 1)
            pe.wait_ge(rows_cleared, 3)
            for q in range(QUADS):
                if q % 2 == 0:
                    pe.wait_ge(parts_spread[q // 2][0], spread_count(0, 0))
                for k in range(UNITS):
                    sa_unit(0, 0, q, k)
                if q == 2:
                    pe.wait_ge(rest_ready, 4)
                    max_transpose(0, 0, bC)
            pe.wait_ge(const_loaded, n_const)
            pe.wait_ge(ucat_ready, 1)
            mm(bank[2][:, 0:3 * R], wq1[:], vcat[:], start=True, stop=True)
            mm(bank[3][:, 0:2 * R], wk1[:], wcat[:], start=True, stop=True)
            mm(bank[4][0:2 * R + 1, 0:D], ucat[:], wo1[:], start=True, stop=True).then_inc(mixer_products, 1)
            pe.wait_ge(mixer_weights, 1)

            def step(b, buf, prev=True, nxt=True, before=True):
                o = 1 - buf
                for q in range(QUADS):
                    if nxt and q % 2 == 0:
                        pe.wait_ge(parts_spread[q // 2][o], spread_count(b + 1, o))
                    if q % 2 == 0:
                        pe.wait_ge(negmax_spread[q // 2], 16 * (b + 1))
                    for k in range(UNITS):
                        if nxt:
                            sa_unit(b + 1, o, q, k)
                        st_unit(b, buf, q, k)
                        if q == 0 and k < 4 and prev:
                            pv(b - 1, o, 3, k)
                        if q >= 1 and k < 4:
                            pv(b, buf, q - 1, k)
                        if q == 0 and k == 1 and before:
                            ranks(b - 2)
                        if q == 0 and k == 5:
                            if prev:
                                pe.wait_ge(quad_normalized, QUADS * b - 1)
                            pe.wait_ge(negmax_ready, 2 * b + 1)
                            max_transpose(b, 1, bC)
                        if q == 1 and k == 0 and prev:
                            if before:
                                pe.wait_ge(slots_ready, b - 1)
                            tokens_first(b - 1, 3, bA)
                        if q == 1 and k == 1 and nxt:
                            if before:
                                pe.wait_ge(logit_gap, b - 1)
                            pe.wait_ge(negmax_ready, 2 * b + 2)
                            pe.wait_ge(xT_loaded, 16 * (b + 3))
                            project_qk(b + 2, buf)
                        if q == 1 and k == 5 and prev:
                            att_transpose(b - 1)
                        if q == 1 and k == 8 and nxt:
                            pe.wait_ge(rest_ready, 2 * b + 6)
                            pe.wait_ge(sums_ready, QUADS * b) if later(b) else None
                            project_v(b + 1, o, bB)
                        if q == 1 and k == 7:
                            if nxt:
                                pe.wait_ge(rest_ready, 2 * b + 6)
                            tokens_first(b, 0, bC)
                        if q == 1 and k == 9 and prev:
                            out_project(b - 1)
                        if q == 2 and k == 8 and nxt:
                            pe.wait_ge(v_ready, b + 2)
                            max_transpose(b + 1, 0, bB)
                        if q == 2 and k == 6:
                            pe.wait_ge(quad_normalized, QUADS * b + 1)
                            tokens_first(b, 1, bC)
                        if q == 3 and k == 0 and prev:
                            x1_transpose(b - 1, o)
                        if q == 3 and k == 3 and prev:
                            if nxt:
                                pe.wait_ge(negmax_ready, 2 * b + 3)
                            gate_logits(b - 1)
                        if q == 3 and k == 6:
                            pe.wait_ge(quad_normalized, QUADS * b + 2)
                            tokens_first(b, 2, bC)

            step(0, 0, prev=False, before=False)
            step(1, 1, before=False)
            with pe.Fori(1, 3) as i:
                step(2 * i, 0)
                step(2 * i + 1, 1)
            step(6, 0)
            step(7, 1, nxt=False)
            ranks(6)
            for part in range(4):
                pv(7, 1, 3, part)
            pe.wait_ge(slots_ready, 7)
            tokens_first(7, 3, bA)
            att_transpose(7)
            out_project(7)
            x1_transpose(7, 1)
            gate_logits(7)
            ranks(7)

            pe.wait_ge(table_ready, 1)
            pe.wait_ge(slots_ready, B)

            def slot_transpose(j, buf, first=False):
                pe.wait_ge(slots_loaded[buf], 8 * (j - buf) + 16)
                if not first:
                    pe.wait_ge(slots_copied, j - 1)
                tr(bank[6 + buf][:, 0:P], XS[buf], identf[:]).then_inc(slots_turned, 1)

            def up(j, buf, ring, first=False):
                pe.wait_ge(slots_copied, j + 1)
                pe.wait_ge(own_ready, j + 1)
                if not first:
                    pe.wait_ge(gelu_ready, j - 1)
                for f in range(FC):
                    last = mm(bank[buf][:, f * P:(f + 1) * P], own[ring][:, f * P:(f + 1) * P], XST[buf], start=True, stop=True)
                last.then_inc(hidden_ready, 1)

            def down(j, buf, first=False):
                e = pe.value_load(tableb[0:1, 1, bass.ds(j, 1)], min_val=0, max_val=E - 1)
                pe.wait_ge(gelu_ready, j + 1)
                if not first:
                    pe.wait_ge(tile_out_ready, j - 1)
                for f in range(FC):
                    last = mm(bank[2 + buf][:, 0:D], HT[buf][:, f * P:(f + 1) * P], w2[:, bass.ds(e, 1), f, :].rearrange("p o d -> p (o d)"),
                              start=(f == 0), stop=(f == FC - 1))
                last.then_inc(tile_out, 1)

            pe.wait_ge(experts_loaded, 64)
            slot_transpose(0, 0, True)
            slot_transpose(1, 1, True)
            up(0, 0, 0, True)
            slot_transpose(2, 0)
            up(1, 1, 1, True)
            down(0, 0, True)
            slot_transpose(3, 1)
            up(2, 0, 2)
            down(1, 1, True)
            with pe.Fori(0, TILES // 4 - 1) as i:
                for c in range(2, 6):
                    slot_transpose(4 * i + c + 2, c % 2)
                    up(4 * i + c + 1, (c + 1) % 2, (c + 1) % 4)
                    down(4 * i + c, c % 2)
            up(TILES - 1, 1, 3)
            down(TILES - 2, 0)
            down(TILES - 1, 1)

            def x2_products(b, buf):
                pe.wait_ge(x2_ready, b + 1)
                for t in range(T):
                    last = tr(bank[6 + buf][:, t * P:(t + 1) * P], X2[buf][:, t, :], identf[:])
                last.then_inc(x2_turned, 1)
                pe.wait_ge(x2_copied, b + 1)
                mm(bank[2 * buf][0:3 * R, :], wa[:], X2T[buf], start=True, stop=True)
                mm(bank[2 * buf + 1][0:3 * R, :], wb[:], X2T[buf], start=True, stop=True).then_inc(mixer_inputs, 1)

            def low_rank_out(b, buf):
                pe.wait_ge(mixer_gated, b + 1)
                if not isinstance(b, int) or b >= 2:
                    pe.wait_ge(scores_copied, b - 1)
                for t in range(T):
                    last = mm(bank[4 + buf][:, t * P:(t + 1) * P], G[buf][0:2 * R + 1, t * P:(t + 1) * P], uc[:], start=True, stop=True)
                last.then_inc(mixer_out, 1)

            def router_scores(b, buf):
                pe.wait_ge(n3_ready, b + 1)
                for t in range(T):
                    last = tr(bank[6 + buf][:, t * P:(t + 1) * P], N3b[buf][:, t, :], identf[:])
                last.then_inc(n3_turned, 1)
                pe.wait_ge(n3_copied, b + 1)
                mm(bank[4 + buf][0:E, :], cent[:], N3T[buf], start=True, stop=True).then_inc(scores_ready, 1)

            def mixer(b, buf, nxt=True):
                if nxt:
                    x2_products(b + 1, 1 - buf)
                    low_rank_out(b + 1, 1 - buf)
                router_scores(b, buf)

            pe.wait_ge(tile_out_ready, TILES)
            x2_products(0, 0)
            low_rank_out(0, 0)
            mixer(0, 0)
            with pe.Fori(0, 3) as i:
                mixer(2 * i + 1, 1)
                mixer(2 * i + 2, 0)
            mixer(7, 1, nxt=False)

            def to_ways(bk, keys, e):
                mm(bk[:], pick[0:B * E, e, :], keys[0:B * E], start=True, stop=True).then_inc(keys_spread, 1)

            pe.wait_ge(keys_ready, 1)
            pe.wait_ge(late_consts, 96)
            to_ways(bank[2], keyhi, 0)
            for e in range(E - 1):
                for n in range(ROUNDS):
                    pe.wait_ge(counts_ready, ROUNDS * e + n + 1)
                    mm(bank[(ROUNDS * e + n) % 2][:, 0:WAYS], acc[:, 0:1].to_broadcast([P, P]), way[:], start=True, stop=True).then_inc(totals_ready, 1)
                    if n == 0:
                        if e >= 1:
                            pe.wait_ge(lo_read, e)
                        to_ways(bank[4], keylo, e)
                    if n == 1 and e < E - 2:
                        pe.wait_ge(hi_read, e + 1)
                        to_ways(bank[2], keyhi, e + 1)
            pe.wait_ge(experts_found, 1)
            for t in range(T):
                last = mm(bank[6][:, t * B:(t + 1) * B], turned[:, t * P:(t + 1) * P], identf[:, 0:B], start=True, stop=True)
            last.then_inc(experts_turned, 1)
            pe.wait_ge(assigned_ready, 1)
            mm(bank[1][:, 0:NT * E], before[:], takenb, start=True, stop=True)
            mm(bank[2][:, 0:NT * E], onesb[:], takenb, start=True, stop=True).then_inc(assigned_counted, 1)

            for q in range(4):
                pe.wait_ge(row_choices_ready, q + 1)
                for t in range(8 * q, 8 * q + 8):
                    last = mm(bank[3][:, 0:2 * NT], in_row[:, t, :], in_tile[:, t].rearrange("p i c -> p (i c)"), start=(t == 0), stop=(t == NT - 1))
            last.then_inc(tokens_found, 1)

            def rows_transpose(e):
                pe.wait_ge(expert_rows_loaded[e % 4], 16 * T * (e // 4 + 1))
                for t in range(T):
                    last = tr(bank[6][:, t * P:(t + 1) * P], XR[e % 4][:, t, D:2 * D], identf[:])
                last.then_inc(rows_turned, 1)

            pe.wait_ge(places_ready, 1)
            pe.wait_ge(experts_loaded, 16 * 8)
            rows_transpose(0)
            for e in range(E):
                pe.wait_ge(rows_copied, e + 1)
                for f in range(FC):
                    n = e * FC + f
                    if n >= 4:
                        pe.wait_ge(expert_gelu, n - 3)
                    mm(bank[n % 4][:], w1[:, e, f * P:(f + 1) * P], XET, start=True, stop=True).then_inc(expert_hidden, 1)
                if e + 1 < E:
                    rows_transpose(e + 1)
                pe.wait_ge(expert_gelu, FC * (e + 1))
                if e >= 2:
                    pe.wait_ge(expert_out_read, e - 1)
                for t in range(T):
                    for f in range(FC):
                        last = mm(bank[4 + e % 2][:, t * P:(t + 1) * P], HE[:, f, t * P:(t + 1) * P], w2[:, e, f, :],
                                  start=(f == 0), stop=(f == FC - 1))
                last.then_inc(expert_out, 1)

        @block.scalar
        def _(act):
            A = nc.scalar.activation

            def q_first(n):
                for i, (dst, bk) in enumerate(((qparts[0], bB), (kparts[0], bC))):
                    act.wait_ge(qk_projected, 2 * n + i + 1)
                    if later(n):
                        act.wait_ge(parts_stored[0], 32 * n)
                    A(dst, bk[:], Cp).then_inc(part1_ready, 1)

            def q_second(n):
                for i, (dst, rest) in enumerate(((qparts[1], qrest), (kparts[1], krest))):
                    act.wait_ge(rest_ready, 2 * n + i + 1)
                    if later(n):
                        act.wait_ge(parts_stored[1], 32 * n)
                    A(dst, rest, Cp).then_inc(part2_ready, 1)

            def v_copy(n, buf, bk):
                act.wait_ge(v_projected, n + 1)
                A(Vaug[buf][:, :, :, 0:HD], bk[:].rearrange("p (t h d) -> p t h d", t=T, h=H), Cp).then_inc(v_ready, 1)

            def nmt_copy(n, hf, bk):
                act.wait_ge(negmax_turned, 2 * n + hf + 1)
                if later(n):
                    act.wait_ge(negmax_stored, 32 * n - 16 + 16 * hf)
                A(NMT[hf][:], bk[:].bitcast(bf16)[0:PARTS * HH, 0:S], Cp).then_inc(negmax_ready, 1)

            def o_copy(n, q):
                act.wait_ge(sums_ready, QUADS * n + q + 1)
                if not (isinstance(n, int) and n == 0 and q < 2):
                    act.wait_ge(sums_turned, QUADS * n + q - 1)
                A(OT[q % 2][:], bank[4][:], Cp).then_inc(sums_copied, 1)

            q_first(0)
            v_copy(0, 0, bA)
            q_second(0)
            q_first(1)
            load_experts(act, "a")
            q_second(1)
            nmt_copy(0, 0, bC)
            act.wait_ge(const_loaded, n_const)
            A(expdb[:], expdb[:], ACT.Exp).then_inc(expdb_ready, 1)

            def step(b, buf, prev=True, nxt=True):
                o = 1 - buf
                for q in range(QUADS):
                    for k in range(UNITS):
                        u = q * UNITS + k
                        act.wait_ge(exp_scores, UB * b + u + 1)
                        if k == 0 and not (isinstance(b, int) and b == 0 and q < 2):
                            act.wait_ge(sums_ready, QUADS * b + q - 1)
                        A(PR[:, q % 2, k, :], bank[2 + u % 2][:], ACT.Exp, scale=SCALE).then_inc(exps_ready, 1)
                        if q == 0 and k == 5 and prev:
                            o_copy(b - 1, 3)
                        if q == 0 and k == 7:
                            nmt_copy(b, 1, bC)
                        if q == 1 and k == 2 and nxt:
                            q_first(b + 2)
                        if k == 4 and q >= 1:
                            o_copy(b, q - 1)
                        if q == 1 and k == 6 and nxt:
                            q_second(b + 2)
                        if q == 1 and k == 7 and prev:
                            act.wait_ge(attention_turned, b)
                            A(attT[:], bA[:], Cp).then_inc(attention_copied, 1)
                        if q == 1 and k == 9 and nxt:
                            v_copy(b + 1, o, bB)
                        if q == 2 and k == 9 and nxt:
                            nmt_copy(b + 1, 0, bB)
                        if q == 3 and k == 1 and prev:
                            x1t_copy(b - 1)
                        if q == 3 and k == 7 and prev:
                            gate_exp(b - 1)

            def x1t_copy(n):
                act.wait_ge(x1_turned, n + 1)
                A(X1T[:], bA[:], Cp).then_inc(x1_turned_copied, 1)

            def gate_exp(n):
                act.wait_ge(logit_gap, n + 1)
                A(gate[:, :, 1], gate[:, :, 0], ACT.Exp).then_inc(gap_exp, 1)

            step(0, 0, prev=False)
            with act.Fori(0, 3) as i:
                step(2 * i + 1, 1)
                step(2 * i + 2, 0)
            step(7, 1, nxt=False)
            o_copy(7, 3)
            act.wait_ge(attention_turned, 8)
            A(attT[:], bA[:], Cp).then_inc(attention_copied, 1)
            x1t_copy(7)
            gate_exp(7)

            act.wait_ge(table_ready, 1)

            def slots(j, buf, first=False):
                act.wait_ge(slots_turned, j + 1)
                if not first:
                    act.wait_ge(hidden_ready, j - 1)
                A(XST[buf], bank[6 + buf][:, 0:P], Cp).then_inc(slots_copied, 1)

            def hidden(j, buf, ring, first=False):
                act.wait_ge(hidden_ready, j + 1)
                if not first:
                    act.wait_ge(tile_out, j - 1)
                for f in range(FC):
                    last = A(HT[buf][:, f * P:(f + 1) * P], bank[buf][:, f * P:(f + 1) * P], ACT.Gelu_apprx_tanh,
                             bias=own[ring][:, F + f:F + f + 1])
                last.then_inc(gelu_ready, 1)

            act.wait_ge(experts_loaded, 64)
            slots(0, 0, True)
            slots(1, 1, True)
            hidden(0, 0, 0, True)
            slots(2, 0)
            hidden(1, 1, 1, True)
            slots(3, 1)
            with act.Fori(0, TILES // 4 - 1) as i:
                for c in range(2, 6):
                    hidden(4 * i + c, c % 2, c % 4)
                    slots(4 * i + c + 2, c % 2)
            hidden(TILES - 2, 0, 2)
            hidden(TILES - 1, 1, 3)

            def x2_copy(b, buf):
                act.wait_ge(x2_turned, b + 1)
                A(X2T[buf], bank[6 + buf][:], Cp).then_inc(x2_copied, 1)

            def mixer(b, buf, nxt=True):
                if nxt:
                    x2_copy(b + 1, 1 - buf)
                act.wait_ge(n3_turned, b + 1)
                A(N3T[buf], bank[6 + buf][:], Cp).then_inc(n3_copied, 1)
                act.wait_ge(scores_ready, b + 1)
                if not isinstance(b, int) or b >= 2:
                    act.wait_ge(scores_stored[buf], 8 * (b - buf))
                A(score[buf][0:E, :], bank[4 + buf][0:E, :], Cp).then_inc(scores_copied, 1)

            x2_copy(0, 0)
            mixer(0, 0)
            mixer(1, 1)
            with act.Fori(0, B // 2 - 2) as i:
                mixer(2 * i + 2, 0)
                mixer(2 * i + 3, 1)
            mixer(6, 0)
            mixer(7, 1, nxt=False)

            for e in range(E):
                act.wait_ge(rows_turned, e + 1)
                if e >= 1:
                    act.wait_ge(expert_hidden, e * FC)
                A(XET, bank[6][:], Cp).then_inc(rows_copied, 1)
                if e >= 1:
                    act.wait_ge(expert_out, e)
                for f in range(FC):
                    act.wait_ge(expert_hidden, e * FC + f + 1)
                    A(HE[:, f, :], bank[(e * FC + f) % 4][:], ACT.Gelu_apprx_tanh, bias=w1[:, e, F + f:F + f + 1]).then_inc(expert_gelu, 1)

        @block.gpsimd
        def _(pool):
            g = nc.gpsimd
            two_ones = 1.0 + 0x3F80 / 2.0 ** 23
            g.memset(KP[0][MROW:P].bitcast(f32), two_ones).then_inc(ones_set, 1)
            pool.wait_ge(ones_set, 1)
            g.memset(half[:], -0.5)
            for i in range(2):
                g.memset(NM[i][:], 0.0)
            g.memset(onesb[:], 1.0)
            g.memset(zeros[:], 0.0).then_inc(small_cleared, 1)

            def after_wait(k):
                g.tensor_tensor(pool_junk[:, k:k + 1], half[:, 0:1], half[:, 0:1], ALU.add)

            def parts(n):
                for i, (dst, src, sub) in enumerate(((qparts[2], qrest, qparts[1]), (kparts[2], krest, kparts[1]))):
                    pool.wait_ge(part2_ready, 2 * n + i + 1)
                    if later(n):
                        pool.wait_ge(parts_stored[2], 32 * n)
                    g.tensor_tensor(dst, src, sub, ALU.subtract).then_inc(part3_ready, 1)

            def rsqrt(n, x=rstd):
                pool.wait_ge(var_ready, n)
                g.tensor_tensor(x[:], x[:], half[:], ALU.pow).then_inc(rstd_ready, 1)

            def residual(n):
                pool.wait_ge(tokens_loaded, 16 * n + 16)
                g.tensor_tensor(xres[:], xres[:], bo0[:].rearrange("p (o d) -> p o d", o=1).to_broadcast([P, T, D]), ALU.add)\
                 .then_inc(residual_ready, 1)

            def scatter(n, buf, tiles=range(T)):
                if 0 in tiles:
                    pool.wait_ge(slots_ready, n + 1)
                    if not isinstance(n, int):
                        after_wait(2)
                for t in tiles:
                    for i in range(2):
                        g.indirect_dma_start(xs_dram, bass.IndirectOffsetOnAxis(ap=posb[buf][:, t, i:i + 1], axis=0),
                                             Xb[buf][:, t, :], None).then_inc(rows_scattered[buf], 16)

            def drop_later(n, q, which=(0, 1, 2)):
                pr = PR[:, q % 2]
                for part, (units, blocks) in enumerate(((4, (pr[:, 0:4, 0:P],)), (8, (pr[:, 4:8, 0:P], pr[:, 4:8, 3 * P:S])),
                                                        (UNITS, (pr[:, 8:10, 0:P], pr[:, 8:10, 2 * P:3 * P])))):
                    if part not in which:
                        continue
                    pool.wait_ge(exps_ready, UB * n + UNITS * q + units)
                    if not isinstance(n, int):
                        after_wait(4 + 3 * q + part)
                    for x in blocks:
                        last = g.affine_select(out=x, in_=x, compare_op=ALU.is_ge, fill=0.0, base=0,
                                               pattern=[[0, int(x.shape[1])], [1, P]], channel_multiplier=-1)
                    last.then_inc(later_dropped, 1)

            parts(0)
            g.memset(KP[1][0:MROW].bitcast(f32), 0.0).then_inc(ones_set, 1)
            pool.wait_ge(ones_set, 2)
            g.memset(KP[1][MROW:P].bitcast(f32), two_ones).then_inc(ones_set, 1)
            pool.wait_ge(ones_set, 3)
            parts(1)

            def step(b, buf, prev=True, nxt=True, before=True):
                drop_later(b, 0)
                if prev:
                    residual(b - 1)
                if before:
                    scatter(b - 2, buf, (0, 1))
                drop_later(b, 1, (0, 1))
                if nxt:
                    parts(b + 2)
                drop_later(b, 1, (2,))
                if before:
                    scatter(b - 2, buf, (2,))
                if prev:
                    rsqrt(b)
                drop_later(b, 2)
                if before:
                    scatter(b - 2, buf, (3,))
                drop_later(b, 3)

            step(0, 0, prev=False, before=False)
            step(1, 1, before=False)
            with pool.Fori(1, 3) as i:
                step(2 * i, 0)
                step(2 * i + 1, 1)
            step(6, 0)
            step(7, 1, nxt=False)
            residual(7)
            scatter(6, 0)
            rsqrt(8)
            scatter(7, 1)
            for buf in range(2):
                g.memset(G[buf], 1.0)
            g.memset(onesf, 1.0).then_inc(mixer_cleared, 1)
            pool.wait_ge(tile_out_ready, TILES)
            for buf in range(2):
                pool.wait_ge(slots_stored[buf], 8 * TILES)

            def gather(b, pieces):
                if 0 in pieces:
                    pool.wait_ge(rows_wanted, b + 1)
                for t, i in ((k // 2, k % 2) for k in pieces):
                    g.indirect_dma_start(Y[b % 2][i][:, t, :], None, ys_dram,
                                         bass.IndirectOffsetOnAxis(ap=posb[b % 2][:, t, i:i + 1], axis=0)).then_inc(rows_gathered[b % 2], 16)

            def scale_shift(b, buf):
                pool.wait_ge(n3_normed, b + 1)
                g.tensor_tensor(N3b[buf], N3b[buf], lng[:].rearrange("p (o d) -> p o d", o=1).to_broadcast([P, T, D]), ALU.mult)\
                 .then_inc(n3_scaled, 1)
                pool.wait_ge(n3_scaled, b + 1)
                g.tensor_tensor(N3b[buf], N3b[buf], lnb[:].rearrange("p (o d) -> p o d", o=1).to_broadcast([P, T, D]), ALU.add)\
                 .then_inc(n3_ready, 1)

            gather(0, range(8))
            gather(1, range(4))
            rsqrt(9, rstdc[0])
            gather(1, range(4, 8))
            gather(2, range(8))
            gather(3, range(3))
            for b in range(B):
                if b + 1 < B:
                    rsqrt(8 + 3 * b + 2, rstdc[(b + 1) % 2])
                k = 8 + 3 * b + (3 if b + 1 < B else 2)
                rsqrt(k, rstdc[b % 2])
                if b + 3 < B:
                    gather(b + 3, (3, 4))
                rsqrt(k + 1, rstdc[b % 2])
                if b + 3 < B:
                    gather(b + 3, (5, 6, 7))
                scale_shift(b, b % 2)
                if b + 4 < B:
                    gather(b + 4, range(3))

            pool.wait_ge(places_ready, 1)
            for buf in range(2):
                pool.wait_ge(rows_stored[buf], 8 * B)

            def fetch(e):
                if e >= 4:
                    pool.wait_ge(rows_done, e - 3)
                for t in range(T):
                    g.indirect_dma_start(XR[e % 4][:, t, :], None, xn_dram,
                                         bass.IndirectOffsetOnAxis(ap=tokensi[:, e * T + t:e * T + t + 1], axis=0)).then_inc(expert_rows_loaded[e % 4], 16)

            fetch(0)
            fetch(1)
            fetch(2)
            fetch(3)
            out_rows = out.rearrange("b n d -> (b n) d")
            for e in range(E):
                rsqrt(8 + 24 + e + 1)
                if e >= 1 and e + 3 < E:
                    fetch(e + 3)
                pool.wait_ge(rows_done, e + 1)
                for t in range(T):
                    g.indirect_dma_start(out_rows, bass.IndirectOffsetOnAxis(ap=tokensi[:, e * T + t:e * T + t + 1], axis=0),
                                         OE[e % 2][:, t, :], None).then_inc(out_stored[e % 2], 16)

        @block.vector
        def _(dve):
            v = nc.vector
            state = {"n": 0, "off": 0}

            def mark(ins):
                ins.then_inc(dve_step, 1)
                state["n"] += 1

            def settle():
                dve.wait_ge(dve_step, state["off"] + state["n"])

            def link(ins):
                ins.then_inc(dve_step, 1)
                state["n"] += 1
                dve.wait_ge(dve_step, state["off"] + state["n"])

            def layer_norm(dst, src, count):
                for t in range(T):
                    last = v.bn_stats(stats[:, t, :], src[:, t, :])
                link(last)
                v.tensor_copy(junk[:, 0:1], half[:, 0:1])
                for t in range(T):
                    last = v.bn_aggr(mv[:, t, :], stats[:, t, :])
                link(last)
                v.tensor_scalar(rstd[:], mv[:, :, 1], EPS, None, ALU.add).then_inc(var_ready, 1)
                dve.wait_ge(rstd_ready, count)
                for t in range(T):
                    last = v.tensor_scalar(dst[:, t, :], src[:, t, :], mv[:, t, 0:1], rstd[:, t:t + 1], ALU.subtract, ALU.mult)
                return last

            v.memset(QP[0].bitcast(f32), 0.0)
            v.memset(KP[0][0:MROW].bitcast(f32), 0.0).then_inc(rows_cleared, 1)

            def q_rest(n, which=(0, 1)):
                for i in which:
                    rest, p0, bk = ((qrest, qparts[0], bB), (krest, kparts[0], bC))[i]
                    dve.wait_ge(part1_ready, 2 * n + i + 1)
                    if later(n):
                        dve.wait_ge(part3_ready, 2 * n)
                    v.tensor_tensor(rest, bk[:], p0, ALU.subtract).then_inc(rest_ready, 1)

            def maxima(n, q, k):
                u = q * UNITS + k
                dve.wait_ge(max_scores, UB * n + u + 1)
                bk = bank[u % 2]
                h = 4 * q + k % 4
                if k < 4:
                    last = v.tensor_reduce(M[:, 3, h:h + 1], bk[:], AX.X, ALU.max)
                elif k < 8:
                    v.tensor_reduce(M[:, 2, h:h + 1], bk[:, 0:3 * P], AX.X, ALU.max)
                    last = v.tensor_reduce(M[:, 0, h:h + 1], bk[:, 3 * P:4 * P], AX.X, ALU.max)
                else:
                    h = 4 * q + 2 * (k - 8)
                    last = v.tensor_reduce(M[:, 1, h:h + 2], bk[:].rearrange("p (h n) -> p h n", h=2), AX.X, ALU.max)
                last.then_inc(maxima_taken, 2)

            def negate_maxima(n, hf, part):
                m = M[:, :, hf * HH:(hf + 1) * HH]
                nm = NM[hf]
                if part == 0:
                    dve.wait_ge(maxima_taken, 2 * UB * n + UB * (hf + 1))
                    mark(v.tensor_scalar(nm[:, :, 0, :], m, -1.0, None, ALU.mult))
                elif part == 1:
                    settle()
                    mark(v.scalar_tensor_tensor(mrest[:], m, -1.0, nm[:, :, 0, :], ALU.mult, ALU.subtract))
                elif part == 2:
                    settle()
                    mark(v.tensor_copy(nm[:, :, 1, :], mrest[:]))
                else:
                    settle()
                    v.tensor_tensor(nm[:, :, 2, :], mrest[:], nm[:, :, 1, :], ALU.subtract).then_inc(negmax_parts, 1)

            def normalize(n, q, bk, part):
                o = bk[:].rearrange("p (t h c) -> p t h c", t=T, h=4)
                if part == 0:
                    dve.wait_ge(sums_turned, QUADS * n + q + 1)
                    dq = expdb[:, 4 * q:4 * q + 4].rearrange("p (o h) -> p o h", o=1).to_broadcast([P, T, 4])
                    mark(v.tensor_tensor(den[:], o[:, :, :, HD], dq, ALU.add))
                elif part == 1:
                    settle()
                    mark(v.reciprocal(den[:], den[:]))
                else:
                    settle()
                    v.tensor_tensor(att[:, :, q * 32:(q + 1) * 32].rearrange("p t (h d) -> p t h d", h=4), o[:, :, :, 0:HD],
                                    den[:].rearrange("p t (h o) -> p t h o", o=1).to_broadcast([P, T, 4, HD]), ALU.mult)\
                     .then_inc(quad_normalized, 1)

            def attention_norm(n, buf, part):
                if part == 0:
                    dve.wait_ge(attention_out, n + 1)
                    dve.wait_ge(residual_ready, n + 1)
                    mark(v.tensor_tensor(res[:], bA[:].rearrange("p (t d) -> p t d", t=T), xres[:], ALU.add))
                elif part in (1, 2):
                    settle()
                    for t in (2 * part - 2, 2 * part - 1):
                        last = v.bn_stats(stats[:, t, :], res[:, t, :])
                    mark(last)
                elif part == 3:
                    settle()
                    v.tensor_copy(junk[:, 0:1], half[:, 0:1])
                    for t in range(T):
                        last = v.bn_aggr(mv[:, t, :], stats[:, t, :])
                    mark(last)
                elif part == 4:
                    settle()
                    v.tensor_scalar(rstd[:], mv[:, :, 1], EPS, None, ALU.add).then_inc(var_ready, 1)
                else:
                    if part == 5:
                        dve.wait_ge(rstd_ready, n + 1)
                        if not isinstance(n, int) or n >= 2:
                            dve.wait_ge(rows_scattered[buf], 16 * T * (n - buf))
                            dve.wait_ge(x1_saved[buf], 8 * (n - buf))
                    for t in (2 * part - 10, 2 * part - 9):
                        last = v.tensor_scalar(Xb[buf][:, t, :], res[:, t, :], mv[:, t, 0:1], rstd[:, t:t + 1], ALU.subtract, ALU.mult)
                    if part == 6:
                        last.then_inc(x1_ready, 1)

            def choose(n, part):
                if part == 0:
                    dve.wait_ge(logits_ready, n + 1)
                    mark(v.tensor_copy(logit[:], bB[:, 0:T * E].rearrange("p (t e) -> p t e", t=T)))
                elif part == 1:
                    settle()
                    v.tensor_copy(junk[:, 0:1], half[:, 0:1])
                    for t in range(T):
                        last = v.max(top[:, t, :], logit[:, t, :])
                    mark(last)
                elif part == 2:
                    settle()
                    v.tensor_tensor(gate[:, :, 0], top[:, :, 1], top[:, :, 0], ALU.subtract).then_inc(logit_gap, 1)
                    for t in range(T):
                        last = v.max_index(topi[:, t, :], top[:, t, :], logit[:, t, :])
                    mark(last)
                elif part == 3:
                    settle()
                    mark(v.tensor_copy(topf[:], topi[:]))
                elif part == 4:
                    settle()
                    io = iota8[:].rearrange("p (o e) -> p o e", o=1).to_broadcast([P, T, E])
                    for i in range(2):
                        last = v.tensor_tensor(oh[:, i], io, topf[:, :, i:i + 1].to_broadcast([P, T, E]), ALU.is_equal)
                    mark(last)
                else:
                    settle()
                    v.tensor_tensor(ohb[:], oh[:, 0], oh[:, 1], ALU.add).then_inc(choices_ready, 1)

            def gates(n, part):
                if part == 0:
                    dve.wait_ge(gap_exp, n + 1)
                    mark(v.tensor_scalar(gate[:, :, 0], gate[:, :, 1], 1.0, None, ALU.add))
                elif part == 1:
                    settle()
                    mark(v.reciprocal(gate[:, :, 0], gate[:, :, 0]))
                elif part == 2:
                    settle()
                    mark(v.tensor_tensor(gate[:, :, 1], gate[:, :, 1], gate[:, :, 0], ALU.mult))
                else:
                    settle()
                    mark(v.tensor_copy(GATE[:, bass.ds(n * T, T), :], gate[:]))

            def positions(n, buf, part):
                if part == 0:
                    dve.wait_ge(ranks_counted, n + 1)
                    v.tensor_copy(tpre[:, :, 0], run[:])
                    mark(v.tensor_copy(tpre[:, :, 1:T + 1], bA[:, T * E:2 * T * E].rearrange("p (t e) -> p e t", t=T)))
                elif part == 1:
                    settle()
                    flat = tpre[:].rearrange("p e t -> p (e t)")
                    mark(v.tensor_tensor_scan(flat, fresh[:].rearrange("p e t -> p (e t)"), flat, 0.0, ALU.mult, ALU.add))
                elif part == 2:
                    settle()
                    v.tensor_copy(run[:], tpre[:, :, T])
                    mark(v.tensor_tensor(posf[:], bA[:, 0:T * E].rearrange("p (t e) -> p t e", t=T),
                                         tpre[:, :, 0:T].rearrange("p e t -> p t e"), ALU.add))
                elif part == 3:
                    settle()
                    for i in range(2):
                        last = v.tensor_tensor(oh[:, i], oh[:, i], posf[:], ALU.mult)
                    mark(last)
                elif part == 4:
                    settle()
                    mark(v.tensor_reduce(pos2[:], oh[:], AX.X, ALU.add))
                else:
                    settle()
                    mark(v.tensor_copy(POS[:, bass.ds(n * T, T), :], pos2[:].rearrange("p i t -> p t i")))
                    v.tensor_copy(posb[buf][:], pos2[:].rearrange("p i t -> p t i")).then_inc(slots_ready, 1)

            q_rest(0)
            v.memset(QP[1].bitcast(f32), 0.0).then_inc(rows_cleared, 1)
            q_rest(1)
            for i in range(2):
                v.memset(Vaug[i][:, :, :, HD + 1:32], 0.0)
                last = v.memset(Vaug[i][:, :, :, HD:HD + 1], 1.0)
            last.then_inc(rows_cleared, 1)
            dve.wait_ge(small_cleared, 1)
            for q in range(QUADS):
                for k in range(UNITS):
                    maxima(0, q, k)
                if q % 2:
                    for part in range(4):
                        negate_maxima(0, q // 2, part)
            dve.wait_ge(const_loaded, n_const)
            dve.wait_ge(expdb_ready, 1)
            v.tensor_scalar(ucat[:, R:2 * R], ucat[:, R:2 * R], alpha[:], None, ALU.mult)
            v.scalar_tensor_tensor(ucat[:, 2 * R:2 * R + 1], bias_t[:], alpha[:], ucat[:, 2 * R:2 * R + 1], ALU.mult,
                                   ALU.add).then_inc(ucat_ready, 1)
            dve.wait_ge(mixer_products, 1)
            v.tensor_copy(wa[:], bank[2][:, 0:3 * R])
            v.tensor_copy(wb[:, 0:2 * R], bank[3][:, 0:2 * R])
            v.tensor_copy(uc[:], bank[4][0:2 * R + 1, 0:D]).then_inc(mixer_weights, 1)

            def step(b, buf, prev=True, nxt=True, before=True):
                o = 1 - buf
                for q in range(QUADS):
                    for k in range(UNITS):
                        if nxt:
                            maxima(b + 1, q, k)
                        if q == 0:
                            if prev and k < 4:
                                negate_maxima(b, 1, k)
                            if before and k < 4:
                                gates(b - 2, k)
                            if before and 3 <= k < 9:
                                positions(b - 2, buf, k - 3)
                        if q == 1:
                            if prev and 1 <= k < 4:
                                normalize(b - 1, 3, bA, k - 1)
                            if k in (4, 5) and nxt:
                                q_rest(b + 2, (k - 4,))
                        if q >= 1 and k >= 7:
                            normalize(b, q - 1, bC, k - 7)
                        if q == 2:
                            if nxt and k < 4:
                                negate_maxima(b + 1, 0, k)
                            if prev and 1 <= k < 6:
                                attention_norm(b - 1, o, k - 1)
                            if prev and k >= 8:
                                attention_norm(b - 1, o, k - 3)
                        if q == 3 and prev and k >= 4:
                            choose(b - 1, k - 4)

            step(0, 0, prev=False, before=False)
            step(1, 1, before=False)
            step(2, 0)
            first = state["n"]
            LPS = 33
            with dve.Fori(0, 2) as i:
                state["off"], state["n"] = first + 2 * LPS * i, 0
                step(2 * i + 3, 1)
                assert state["n"] == LPS, state["n"]
                step(2 * i + 4, 0)
            state["off"], state["n"] = first + 4 * LPS, 0
            step(7, 1, nxt=False)
            for part in range(4):
                gates(6, part)
            for part in range(6):
                positions(6, 0, part)
            for part in range(3):
                normalize(7, 3, bA, part)
            for part in range(7):
                attention_norm(7, 1, part)
            for part in range(6):
                choose(7, part)
            for part in range(4):
                gates(7, part)
            for part in range(6):
                positions(7, 1, part)

            v.tensor_copy(junk[:, 2:3], half[:, 0:1]).then_inc(attention_done, 1)
            settle()
            link(v.tensor_tensor(cntf, run[:], ebase[:], ALU.subtract))
            link(v.tensor_scalar(cntf, cntf, float(P - 1), None, ALU.add))
            link(v.tensor_copy(cnti, cntf))
            link(v.tensor_scalar(cnti, cnti, 7, None, ALU.logical_shift_right))
            link(v.tensor_copy(ntile, cnti))
            link(v.memset(tend, 1.0))
            link(v.tensor_tensor_scan(tend, tend, ntile, 0.0, ALU.mult, ALU.add))
            jb = jrow[:, 0, :].rearrange("p (j o) -> p j o", o=1).to_broadcast([P, TILES, E])
            link(v.tensor_tensor(tge, jb, tend.rearrange("p (o e) -> p o e", o=1).to_broadcast([P, TILES, E]), ALU.is_ge))
            link(v.tensor_tensor(tnt, tge, ntile.rearrange("p (o e) -> p o e", o=1).to_broadcast([P, TILES, E]), ALU.mult))
            link(v.tensor_reduce(tej, tge, AX.X, ALU.add))
            link(v.tensor_reduce(tst, tnt, AX.X, ALU.add))
            link(v.tensor_scalar(tused, tej, float(E) - 0.5, None, ALU.is_lt))
            link(v.scalar_tensor_tensor(trow, tst, -float(P), jrow[:, 1, :], ALU.mult, ALU.add))
            link(v.scalar_tensor_tensor(trow, tej, float(STRIDE), trow, ALU.mult, ALU.add))
            link(v.tensor_tensor(trow, trow, tused, ALU.mult))
            link(v.tensor_copy(tableb[:, 0, :], trow))
            link(v.tensor_tensor(tej, tej, tused, ALU.mult))
            link(v.tensor_copy(tableb[:, 1, :], tej))
            v.tensor_copy(padi, run[:]).then_inc(table_ready, 1)

            link(v.tensor_scalar(ystep[:], ntile, float(P), float(-STRIDE), ALU.mult, ALU.add))
            link(v.tensor_copy(ypos[:], POS[:]))
            for e in range(E - 1):
                link(v.tensor_scalar(yadd[:], POS[:], float((e + 1) * STRIDE), ystep[:, e:e + 1], ALU.is_ge, ALU.mult))
                link(v.tensor_tensor(ypos[:], ypos[:], yadd[:], ALU.add))
            dve.wait_ge(experts_loaded, 64)
            dve.wait_ge(table_ready, 1)

            def expert_of(j):
                return dve.value_load(tableb[0:1, 1, bass.ds(j, 1)], min_val=0, max_val=E - 1)

            def weights(j, ring, first=False):
                if not first:
                    dve.wait_ge(gelu_ready, j - 3)
                    dve.wait_ge(tile_out_ready, j - 3)
                v.tensor_copy(own[ring], w1[:, bass.ds(expert_of(j), 1), :].rearrange("p o f -> p (o f)")).then_inc(own_ready, 1)

            def bias_down(j, buf, ring, first=False):
                dve.wait_ge(tile_out, j + 1)
                if not first:
                    dve.wait_ge(slots_stored[buf], 8 * (j - buf))
                v.tensor_tensor(YS[buf], bank[2 + buf][:, 0:D], own[ring][:, F + FC:F + FC + D], ALU.add).then_inc(tile_out_ready, 1)

            for j in range(4):
                weights(j, j, True)
            dve.wait_ge(own_ready, 4)
            bias_down(0, 0, 0, True)
            bias_down(1, 1, 1, True)
            with dve.Fori(0, TILES // 4 - 1) as i:
                for c in range(2, 6):
                    weights(4 * i + c + 2, c % 4 ^ 2)
                    bias_down(4 * i + c, c % 2, c % 4)
            bias_down(TILES - 2, 0, 2)
            bias_down(TILES - 1, 1, 3)

            def send_positions(b, buf):
                v.tensor_copy(posb[buf][:], ypos[:, b * T:(b + 1) * T, :]).then_inc(rows_wanted, 1)

            def norm_stats(src, buf):
                for t in range(T):
                    last = v.bn_stats(statsc[buf][:, t, :], src[:, t, :])
                link(last)
                v.tensor_copy(junk[:, 0:1], half[:, 0:1])
                for t in range(T):
                    last = v.bn_aggr(mvc[buf][:, t, :], statsc[buf][:, t, :])
                link(last)
                v.tensor_scalar(rstdc[buf][:], mvc[buf][:, :, 1], EPS, None, ALU.add).then_inc(var_ready, 1)

            def norm_apply(dst, src, buf, count):
                dve.wait_ge(rstd_ready, count)
                for t in range(T):
                    last = v.tensor_scalar(dst[:, t, :], src[:, t, :], mvc[buf][:, t, 0:1], rstdc[buf][:, t:t + 1], ALU.subtract, ALU.mult)
                return last

            def combine(b, buf):
                dve.wait_ge(rows_gathered[buf], 16 * T * (b - buf) + 32 * T)
                link(v.tensor_copy(GB[:], GATE[:, b * T:(b + 1) * T, :]))
                dve.wait_ge(x1_loaded[buf], 8 * (b - buf) + 16)
                for i in range(2):
                    for t in range(T):
                        last = v.scalar_tensor_tensor(resc[buf][:, t, :], Y[buf][i][:, t, :], GB[:, t, i:i + 1],
                                                      (Xb[buf][:], resc[buf])[i][:, t, :], ALU.mult, ALU.add)
                    link(last)
                if b + 2 < B:
                    send_positions(b + 2, buf)

            def x2_norm(b, buf, count):
                norm_apply(X2[buf], resc[buf], buf, count).then_inc(x2_ready, 1)

            def low_rank(b, buf):
                dve.wait_ge(mixer_inputs, b + 1)
                pa, pb = bank[2 * buf], bank[2 * buf + 1]
                link(v.tensor_tensor_scan(SC[buf][0:3 * R, :], onesf[0:3 * R, :], pb[0:3 * R, :], 0.0, ALU.mult, ALU.add))
                link(v.tensor_tensor(SCN[buf][0:3 * R, :], SC[buf][0:3 * R, :], inv_count[0:3 * R], ALU.mult))
                v.tensor_tensor(G[buf][0:R, :], pa[0:R, :], SCN[buf][0:R, :], ALU.mult)
                link(v.tensor_tensor(TZ[buf][R:2 * R, :], pa[2 * R:3 * R, :], SCN[buf][2 * R:3 * R, :], ALU.mult))
                v.tensor_tensor(G[buf][R:2 * R, :], TZ[buf][R:2 * R, :], SCN[buf][R:2 * R, :], ALU.mult).then_inc(mixer_gated, 1)

            def add_low_rank(b, buf):
                dve.wait_ge(mixer_out, b + 1)
                dve.wait_ge(x2_ready, b + 1)
                link(v.tensor_tensor(resc[buf], bank[4 + buf][:].rearrange("p (t d) -> p t d", t=T), X2[buf], ALU.add))
                norm_stats(resc[buf], buf)

            def x3_norm(b, buf, count):
                if not isinstance(b, int) or b >= 2:
                    dve.wait_ge(rows_stored[buf], 8 * (b - buf))
                norm_apply(X3b[buf], resc[buf], buf, count).then_inc(x3_ready, 1)
                dve.wait_ge(x3_ready, b + 1)
                norm_stats(X3b[buf], buf)

            def n3_norm(b, buf, count):
                if b >= 2:
                    dve.wait_ge(n3_copied, b - 1)
                norm_apply(N3b[buf], X3b[buf], buf, count).then_inc(n3_normed, 1)

            dve.wait_ge(mixer_cleared, 1)
            dve.wait_ge(late_consts, 96)
            send_positions(0, 0)
            send_positions(1, 1)
            combine(0, 0)
            norm_stats(resc[0], 0)
            x2_norm(0, 0, 9)
            combine(1, 1)
            low_rank(0, 0)
            for b in range(B):
                buf, o = b % 2, 1 - b % 2
                k = 8 + 3 * b + (3 if b + 1 < B else 2)
                if b + 1 < B:
                    norm_stats(resc[o], o)
                add_low_rank(b, buf)
                if b + 1 < B:
                    x2_norm(b + 1, o, k - 1)
                x3_norm(b, buf, k)
                n3_norm(b, buf, k + 1)
                if b + 2 < B:
                    combine(b + 2, buf)
                if b + 1 < B:
                    low_rank(b + 1, o)

            dve.wait_ge(scores_loaded, 16)
            dve.wait_ge(late_consts, 96)
            K = slice(0, B * E)
            link(v.tensor_scalar(ksign[K], kraw[K], 31, None, ALU.arith_shift_right))
            link(v.tensor_scalar(ksign[K], ksign[K], -2147483648, None, ALU.bitwise_or))
            link(v.tensor_tensor(kraw[K], kraw[K], ksign[K], ALU.bitwise_xor))
            link(v.tensor_scalar(ksign[K], kraw[K], 8, None, ALU.logical_shift_right))
            link(v.tensor_copy(keyhi[K], ksign[K]))
            link(v.tensor_scalar(keyhi[K], keyhi[K], 1.0, None, ALU.add))
            link(v.tensor_scalar(ksign[K], kraw[K], 255, 12, ALU.bitwise_and, ALU.logical_shift_left))
            link(v.tensor_copy(keylo[K], ksign[K]))
            v.tensor_tensor(keylo[K], keylo[K], tie[K], ALU.add).then_inc(keys_ready, 1)

            rounds = [0]
            def search(keys, want, digits, result, meanwhile, last_round=None):
                for n, d in enumerate(digits):
                    size = float(2 ** DIGITS[d])
                    first = kstep[:, 1, d:d + 1]
                    with nc.allow_low_precision(reason="counts from -256 to 256 are exact"):
                        v.tensor_scalar(scratch, keys, thr if n else first, -256.0, ALU.is_ge, ALU.add, accum_out=acc[:, 0:1])\
                         .then_inc(counts_ready, 1)
                    rounds[0] += 1
                    if n:
                        mark(v.tensor_tensor(ahead, thr, kdelta[:, d:d + 1], ALU.add))
                    meanwhile(n)
                    dve.wait_ge(totals_ready, rounds[0])
                    link(v.tensor_scalar(reached, bank[(rounds[0] - 1) % 2][:, 0:WAYS], want, 0.0, ALU.is_ge, ALU.add, accum_out=nsel))
                    link(v.scalar_tensor_tensor(thr if n + 1 < len(digits) else result, nsel, size,
                                                ahead if n else kstep[:, 1, d + 1:d + 2], ALU.mult, ALU.add))

            all_digits = list(range(len(DIGITS)))
            OFFSET = float(B * S // 2)
            for e in range(E - 1):
                if e == 0:
                    dve.wait_ge(keys_spread, 1)
                    v.tensor_copy(hi, bank[2][:]).then_inc(hi_read, 1)
                    dve.wait_ge(hi_read, 1)

                def settle_last(n):
                    c = slice(n % 2 * S // 2, (n % 2 + 1) * S // 2)
                    if e and n < 2:
                        mark(v.scalar_tensor_tensor(free[:, c], lo[:, c], th[:, 1:2], kept[:, c], ALU.is_lt, ALU.mult))
                    if e and 2 <= n < 4:
                        mark(v.tensor_copy(turned[:, c], free[:, c]) if e == 1 else
                             v.tensor_tensor(turned[:, c], turned[:, c], free[:, c], ALU.add))

                search(hi, CAP - OFFSET, all_digits, th[:, 0:1], settle_last)
                last_counts = bank[(rounds[0] - 1) % 2][:, 0:WAYS]
                dve.wait_ge(keys_spread, 2 + 2 * e)
                v.scalar_tensor_tensor(lo, hi, th[:, 0:1], bank[4][:], ALU.is_equal, ALU.mult).then_inc(lo_read, 1)
                dve.wait_ge(lo_read, e + 1)

                def keep(n):
                    if n == 0:
                        link(v.scalar_tensor_tensor(below, reached, -2 * OFFSET, last_counts, ALU.mult, ALU.add))
                        link(v.tensor_reduce(above, below, AX.X, ALU.max))
                        link(v.tensor_scalar(need, above, -1.0, CAP - 2 * OFFSET, ALU.mult, ALU.add))
                    c = slice((n + 1) % 2 * S // 2, ((n + 1) % 2 + 1) * S // 2)
                    if n in (1, 2):
                        if e == 0:
                            mark(v.tensor_scalar(kept[:, c], hi[:, c], th[:, 0:1], None, ALU.is_le))
                        else:
                            mark(v.scalar_tensor_tensor(kept[:, c], hi[:, c], th[:, 0:1], free[:, c], ALU.is_le, ALU.mult))
                    if n in (3, 4) and e < E - 2:
                        dve.wait_ge(keys_spread, 3 + 2 * e)
                        ins = v.tensor_tensor(kepthi[:, c], kept[:, c], bank[2][:, c], ALU.mult)
                        if n == 3:
                            mark(ins)
                        else:
                            ins.then_inc(hi_read, 1)

                search(lo, need, all_digits[1:], th[:, 1:2], keep)
                if e < E - 2:
                    dve.wait_ge(hi_read, e + 2)
                    link(v.scalar_tensor_tensor(hi, lo, th[:, 1:2], kepthi, ALU.is_lt, ALU.mult))
            link(v.scalar_tensor_tensor(free, lo, th[:, 1:2], kept, ALU.is_lt, ALU.mult))
            v.tensor_tensor(turned, turned, free, ALU.add).then_inc(experts_found, 1)
            dve.wait_ge(experts_turned, 1)
            link(v.tensor_copy(expert3, bank[6][:, 0:NT].rearrange("p (t b) -> p b t", t=T)))
            v.tensor_tensor(takenb, iota8[:].rearrange("p (o e) -> p o e", o=1).to_broadcast([P, NT, E]),
                            expert3.rearrange("p (t o) -> p t o", o=1).to_broadcast([P, NT, E]), ALU.is_equal).then_inc(assigned_ready, 1)
            dve.wait_ge(assigned_counted, 1)
            link(v.tensor_scalar(carry[:, :, 0], iota8[:], float(CAP), None, ALU.mult))
            link(v.tensor_copy(carry[:, :, 1:NT], bank[2][:, 0:(NT - 1) * E].rearrange("p (t e) -> p e t", e=E)))
            flat = carry.rearrange("p e t -> p (e t)")
            link(v.tensor_tensor_scan(flat, restart.rearrange("p e t -> p (e t)"), flat, 0.0, ALU.mult, ALU.add))
            link(v.tensor_tensor(rank, bank[1][:, 0:NT * E].rearrange("p (t e) -> p e t", e=E), carry, ALU.add))
            link(v.tensor_tensor(rank, rank, takenb.rearrange("p t e -> p e t"), ALU.mult))
            link(v.tensor_reduce(pos3, rank.rearrange("p e t -> p t e"), AX.X, ALU.add))
            link(v.tensor_copy(pos3i, pos3))
            v.tensor_scalar(placei[:, 0, :], pos3i, P - 1, None, ALU.bitwise_and)
            link(v.tensor_scalar(placei[:, 1, :], pos3i, 7, None, ALU.logical_shift_right))
            v.tensor_copy(place_row, placei[:, 0, :])
            link(v.tensor_copy(place_tile, placei[:, 1, :]))
            mark(v.tensor_tensor(in_tile[:, :, 1, :], iota[:, 0:NT].rearrange("p (o c) -> p o c", o=1).to_broadcast([P, NT, NT]),
                                 place_tile.rearrange("p (t o) -> p t o", o=1).to_broadcast([P, NT, NT]), ALU.is_equal))
            settle()
            v.tensor_tensor(in_tile[:, :, 0, :], in_tile[:, :, 1, :], tile, ALU.mult)
            mark(v.tensor_scalar(in_tile[:, :, 1, :], in_tile[:, :, 1, :], lane[:], None, ALU.mult))
            for q in range(4):
                ts = slice(8 * q, 8 * q + 8)
                v.tensor_tensor(in_row[:, ts, :], iota.rearrange("p (o r) -> p o r", o=1).to_broadcast([P, 8, P]),
                                place_row[:, ts].rearrange("p (t o) -> p t o", o=1).to_broadcast([P, 8, P]), ALU.is_equal)\
                 .then_inc(row_choices_ready, 1)
            dve.wait_ge(tokens_found, 1)
            link(v.tensor_copy(tokens_hl.rearrange("p i c -> p (i c)"), bank[3][:, 0:2 * NT]))
            link(v.scalar_tensor_tensor(tokens, tokens_hl[:, 0, :], float(P), tokens_hl[:, 1, :], ALU.mult, ALU.add))
            v.tensor_copy(tokensi, tokens).then_inc(places_ready, 1)

            dve.wait_ge(experts_loaded, 16 * 8)
            for e in range(E):
                dve.wait_ge(expert_out, e + 1)
                dve.wait_ge(expert_rows_loaded[e % 4], 16 * T * (e // 4 + 1))
                if e >= 1:
                    dve.wait_ge(rows_done, e)
                v.tensor_tensor(res[:], bank[4 + e % 2][:].rearrange("p (t d) -> p t d", t=T), w1[:, e:e + 1, F + FC:F + FC + D].to_broadcast([P, T, D]),
                                ALU.add).then_inc(expert_out_read, 1)
                dve.wait_ge(expert_out_read, e + 1)
                link(v.scalar_tensor_tensor(res[:], XR[e % 4][:, :, 0:D], 2.0, res[:], ALU.mult, ALU.add))
                if e >= 2:
                    dve.wait_ge(out_stored[e % 2], 16 * T * (e // 2))
                layer_norm(OE[e % 2], res, 32 + e + 1).then_inc(rows_done, 1)


def kernel(**inputs):
    import numpy as np
    import ml_dtypes
    import concourse.bacc as bacc
    from concourse import mybir as mb
    from concourse.bass_utils import run_bass_kernel_spmd as run

    nc = bacc.Bacc("TRN2", target_bir_lowering=False, num_devices=1)
    a = {k: np.asarray(x) for k, x in inputs.items()}
    p = np.arange(128)
    big = -3.0e38
    bf = ml_dtypes.bfloat16
    stride, tiles = 4096 + 128, 72
    e8, j = np.arange(8), np.arange(tiles)
    f = np.float32
    arr = {
        "identf": np.eye(128, dtype=f), "identb": np.eye(128).astype(bf),
        "mask_a": np.where(p[None, :] > p[:, None], big, 0.0).astype(bf),
        "before": (p[:, None] < p[None, :]).astype(bf),
        "inv_count": np.broadcast_to((1.0 / (1.0 + np.arange(512))).astype(f), (96, 512)),
        "iota8": np.broadcast_to(e8.astype(f), (128, 8)), "ebase": np.broadcast_to((e8 * stride).astype(f), (128, 8)),
        "kstep": ((p // 8 + 1)[:, None, None] * 2.0 ** np.array([20, 16, 12, 8, 4, 0])
                  + np.array([0.0, 1.0])[None, :, None]).astype(f),
        "kdelta": ((p // 8 + 1)[:, None] * np.append(np.diff(2.0 ** np.array([20, 16, 12, 8, 4, 0])), -1.0)).astype(f),
        "fresh": np.broadcast_to((np.arange(5) > 0).astype(f), (128, 8, 5)),
        "way": (p[:, None] // 8 == np.arange(16)).astype(bf),
        "pick": (np.arange(64)[:, None, None] == (p % 8)[None, None, :] * 8 + e8[None, :, None]).astype(f),
        "tie": np.broadcast_to((4096 - np.arange(4096)).reshape(8, 1, 512).astype(f), (8, 8, 512)).reshape(64, 512),
        "restart": np.broadcast_to((np.arange(32) > 0).astype(f), (128, 8, 32)),
        "lane": p[:, None].astype(f), "iota": np.broadcast_to(p.astype(f), (128, 128)),
        "tile": np.broadcast_to(np.arange(32).astype(f)[None, :, None], (128, 32, 32)),
        "jrow": np.broadcast_to(np.stack([j, 128 * j]).astype(f), (128, 2, tiles)),
        "x": a["L0_attn_x"], "xT": a["L0_attn_x"].transpose(0, 2, 1),
        "wq0": a["L0_attn_Wq"].T, "wk0": a["L0_attn_Wk"].T, "wv0": a["L0_attn_Wv"].T, "wo0": a["L0_attn_Wo"].T,
        "bo0": a["L0_attn_bo"], "denom_bias": a["L0_attn_denom_bias"].reshape(16), "wg": a["L0_ffn_Wg"],
        "wq1": a["L1_attn_Wq"], "wk1": a["L1_attn_Wk"], "wo1": a["L1_attn_Wo"].T,
        "V_b": a["L1_attn_V_b"], "V_t": a["L1_attn_V_t"], "W_b": a["L1_attn_W_b"], "W_t": a["L1_attn_W_t"],
        "U_b": a["L1_attn_U_b"], "U_t": a["L1_attn_U_t"], "X_t": a["L1_attn_X_t"],
        "bias_b": a["L1_attn_bias_b"].reshape(128, 1), "bias_t": a["L1_attn_bias_t"].reshape(128, 1),
        "alpha": np.broadcast_to(a["L1_attn_alpha"].reshape(1, 1), (128, 1)),
        "cent": a["L1_ffn_centroids"].T, "lng": a["L1_ffn_ln_g"], "lnb": a["L1_ffn_ln_b"],
        "b1a": a["L0_ffn_b1"].reshape(8, 4, 128).transpose(2, 0, 1), "b1b": a["L1_ffn_b1"].reshape(8, 4, 128).transpose(2, 0, 1),
    }
    for tag, w1, w2, b2 in (("a", "L0_ffn_W1", "L0_ffn_W2", "L0_ffn_b2"), ("b", "L1_ffn_w1", "L1_ffn_w2", "L1_ffn_b2")):
        arr["w1" + tag] = a[w1].transpose(1, 0, 2)
        arr["w2" + tag] = a[w2].reshape(8, 4, 128, 128).transpose(2, 0, 1, 3)
        arr["b2" + tag] = a[b2]
    arrays, I = {}, {}
    for n, x in arr.items():
        x = np.ascontiguousarray(x)
        arrays["in_" + n] = x
        I[n] = nc.dram_tensor("in_" + n, x.shape, mb.dt.from_np(x.dtype), kind="ExternalInput").ap()
    out = nc.dram_tensor("out_x", (8, 512, 128), mb.dt.float32, kind="ExternalOutput").ap()
    sequence_stack_kernel(nc, I, out)
    r = run(nc, [arrays], core_ids=[0])
    return r.results[0]["out_x"]
```
